# Optimizing a Trainium2 kernel written in Bass

```python
import numpy as np
import jax
import jax.numpy as jnp

def _softmax(x, axis=-1):
    return jax.nn.softmax(x, axis=axis)

def _gelu(x):
    return jax.nn.gelu(x, approximate=True)

def _silu(x):
    return jax.nn.silu(x)

def _sigmoid(x):
    return jax.nn.sigmoid(x)

def _layernorm(x, axis=-1, eps=1e-05):
    m = jnp.mean(x, axis=axis, keepdims=True)
    v = jnp.var(x, axis=axis, keepdims=True)
    return (x - m) / jnp.sqrt(v + eps)

def _scatter_add(tgt, idx, src, axis=0):
    return tgt.at[idx].add(src)

def _segment_sum(src, seg, n):
    return jax.ops.segment_sum(src, seg, n)
kernel_name = 'mk_gnn_ffn_d1_gnn_r32_d356f4'

def setup_inputs(seed: int=0):
    np.random.seed(seed)
    _w = jnp.asarray

    def _rec_inputs():
        import jax
        import jax.numpy as jnp
        _gk = jax.random.key(seed)
        x = -0.0002117 + 1 * jax.random.normal(jax.random.fold_in(_gk, 1), (10000, 512), jnp.float32)
        src = jax.random.randint(jax.random.fold_in(_gk, 2), (10000,), 0, 10000, jnp.int32)
        dst = jnp.minimum((10000 * jax.random.uniform(jax.random.fold_in(_gk, 3), (10000,)) ** 2.0).astype(jnp.int32), 9999)
        _o = jnp.argsort(dst, stable=True)
        src = src[_o]
        dst = dst[_o]
        return (x, src, dst)
    x, src, dst = _rec_inputs()

    def _L0_gnn_setup():
        import jax, jax.numpy as jnp
        import numpy as np
        N_NODES = 50000
        N_EDGES = 25000
        D = 512
        N_LAYERS = 3
        EPS = 1e-12
        key = jax.random.key(seed)
        ks = jax.random.split(key, 6)
        x = jax.random.normal(ks[0], (N_NODES, D), dtype=jnp.float32)
        src = jax.random.randint(ks[1], (N_EDGES,), 0, N_NODES, dtype=jnp.int64)
        dst = jax.random.randint(ks[2], (N_EDGES,), 0, N_NODES, dtype=jnp.int64)
        scale = 1.0 / np.sqrt(D)
        W_self = jax.random.normal(ks[3], (N_LAYERS, D, D), dtype=jnp.float32) * scale
        W_neigh = jax.random.normal(ks[4], (N_LAYERS, D, D), dtype=jnp.float32) * scale
        b = jax.random.normal(ks[5], (N_LAYERS, D), dtype=jnp.float32) * 0.01
        return {'x': x, 'src': src, 'dst': dst, 'W_self': W_self, 'W_neigh': W_neigh, 'b': b}
    _L0_gnn_all = _L0_gnn_setup()
    _L0_gnn_in = {k: v for k, v in _L0_gnn_all.items() if k in ('W_self', 'W_neigh', 'b')}
    del _L0_gnn_all

    def _L0_ffn_setup():
        import jax, jax.numpy as jnp
        import numpy as np
        EPS = 1e-05
        TOP_K = 2

        def layer_norm(x, g, b):
            m = x.mean(-1, keepdims=True)
            v = ((x - m) ** 2).mean(-1, keepdims=True)
            return (x - m) / jnp.sqrt(v + EPS) * g + b
        key = jax.random.key(seed)
        ks = jax.random.split(key, 8)
        B, S, D, E, H = (8, 512, 512, 8, 64)
        x = jax.random.normal(ks[0], (B, S, D), dtype=jnp.float32)
        Wg = jax.random.normal(ks[1], (D, E), dtype=jnp.float32) * 0.02
        W1 = jax.random.normal(ks[2], (E, D, H), dtype=jnp.float32) * 0.02
        b1 = jnp.zeros((E, H), dtype=jnp.float32)
        W2 = jax.random.normal(ks[3], (E, H, D), dtype=jnp.float32) * 0.02
        b2 = jnp.zeros((E, D), dtype=jnp.float32)
        ln_g = jnp.ones((D,), dtype=jnp.float32)
        ln_b = jnp.zeros((D,), dtype=jnp.float32)
        out_g = jnp.ones((D,), dtype=jnp.float32)
        out_b = jnp.zeros((D,), dtype=jnp.float32)
        return {'x': x, 'Wg': Wg, 'W1': W1, 'b1': b1, 'W2': W2, 'b2': b2, 'ln_g': ln_g, 'ln_b': ln_b, 'out_g': out_g, 'out_b': out_b}
    _L0_ffn_all = _L0_ffn_setup()
    _L0_ffn_in = {k: v for k, v in _L0_ffn_all.items() if k in ('Wg', 'W1', 'b1', 'W2', 'b2', 'ln_g', 'ln_b', 'out_g', 'out_b')}
    del _L0_ffn_all
    return {'x': x, 'src': src, 'dst': dst, 'L0_gnn_W_self': _L0_gnn_in['W_self'], 'L0_gnn_W_neigh': _L0_gnn_in['W_neigh'], 'L0_gnn_b': _L0_gnn_in['b'], 'L0_ffn_Wg': _L0_ffn_in['Wg'], 'L0_ffn_W1': _L0_ffn_in['W1'], 'L0_ffn_b1': _L0_ffn_in['b1'], 'L0_ffn_W2': _L0_ffn_in['W2'], 'L0_ffn_b2': _L0_ffn_in['b2'], 'L0_ffn_ln_g': _L0_ffn_in['ln_g'], 'L0_ffn_ln_b': _L0_ffn_in['ln_b'], 'L0_ffn_out_g': _L0_ffn_in['out_g'], 'L0_ffn_out_b': _L0_ffn_in['out_b']}

def reference(x, src, dst, L0_gnn_W_self, L0_gnn_W_neigh, L0_gnn_b, L0_ffn_Wg, L0_ffn_W1, L0_ffn_b1, L0_ffn_W2, L0_ffn_b2, L0_ffn_ln_g, L0_ffn_ln_b, L0_ffn_out_g, L0_ffn_out_b):
    import jax
    import jax.numpy as jnp

    def _L0_gnn_ref(x, src, dst, W_self, W_neigh, b):
        import jax, jax.numpy as jnp
        import numpy as np
        N_NODES = 50000
        N_EDGES = 25000
        D = 512
        N_LAYERS = 3
        EPS = 1e-12
        n = x.shape[0]
        deg = jax.ops.segment_sum(jnp.ones_like(dst, dtype=x.dtype), dst, num_segments=n)
        deg = jnp.maximum(deg, 1.0)[:, None]
        h = x
        for l in range(N_LAYERS):
            h_neigh = jax.ops.segment_sum(h[src], dst, num_segments=n) / deg
            rst = h @ W_self[l] + h_neigh @ W_neigh[l] + b[l]
            rst = jax.nn.relu(rst)
            nrm = jnp.sqrt(jnp.sum(rst * rst, axis=-1, keepdims=True))
            h = rst / jnp.maximum(nrm, EPS)
        return h

    def _L0_ffn_ref(x, Wg, W1, b1, W2, b2, ln_g, ln_b, out_g, out_b):
        import jax, jax.numpy as jnp
        import numpy as np
        EPS = 1e-05
        TOP_K = 2

        def layer_norm(x, g, b):
            m = x.mean(-1, keepdims=True)
            v = ((x - m) ** 2).mean(-1, keepdims=True)
            return (x - m) / jnp.sqrt(v + EPS) * g + b
        xn = layer_norm(x, ln_g, ln_b)
        logits = jnp.einsum('bsd,de->bse', xn, Wg)
        probs = jax.nn.softmax(logits, axis=-1)
        top_p, top_i = jax.lax.top_k(probs, TOP_K)
        conf = top_p / top_p.sum(-1, keepdims=True)
        h = jax.nn.gelu(jnp.einsum('bsd,edh->bseh', xn, W1) + b1)
        o = jnp.einsum('bseh,ehd->bsed', h, W2) + b2
        sel = jnp.take_along_axis(o, top_i[..., None], axis=2)
        combined = jnp.einsum('bskd,bsk->bsd', sel, conf)
        return layer_norm(x + combined, out_g, out_b)
    x = x + _L0_gnn_ref(_layernorm(x, axis=-1), src, dst, L0_gnn_W_self, L0_gnn_W_neigh, L0_gnn_b)
    x = x + _L0_ffn_ref(_layernorm(x, axis=-1)[None], L0_ffn_Wg, L0_ffn_W1, L0_ffn_b1, L0_ffn_W2, L0_ffn_b2, L0_ffn_ln_g, L0_ffn_ln_b, L0_ffn_out_g, L0_ffn_out_b)[0]
    return x

_drawn_inputs = setup_inputs


def setup_inputs(seed=0):
    import zlib

    import numpy as np

    out = dict(_drawn_inputs(seed))
    spreads = {'L0_ffn_b1': (0.0, 0.8),
     'L0_ffn_b2': (0.0, 0.1),
     'L0_ffn_ln_g': (1.0, 0.6),
     'L0_ffn_ln_b': (0.0, 0.607),
     'L0_ffn_out_g': (1.0, 0.2),
     'L0_ffn_out_b': (0.0, 0.1)}
    factors = {'L0_gnn_b': 4.567, 'L0_ffn_W1': 3.699, 'L0_ffn_W2': 3.44}
    for name, (base, spread) in spreads.items():
        noise = np.random.default_rng([zlib.crc32(name.encode()), seed]).standard_normal(out[name].shape)
        drawn = base * np.exp(spread * noise) if base else spread * noise
        out[name] = jnp.asarray(drawn.astype(out[name].dtype))
    for name, factor in factors.items():
        out[name] = (out[name] * factor).astype(out[name].dtype)
    return out
```

```python
from contextlib import ExitStack

import concourse.bass as bass
from concourse import mybir

ALU = mybir.AluOpType
ACT = mybir.ActivationFunctionType
AX = mybir.AxisListType
F32 = mybir.dt.float32
F16 = mybir.dt.float16
I32 = mybir.dt.int32
U32 = mybir.dt.uint32

P = 128
N = 10000
E = 10000
D = 512
KC = D // P
LAYERS = 3
EXPERTS = 8
HIDDEN = 64
EPT = P - 1
T = -(-E // EPT)
TN = -(-N // P)
NLAST = N - (TN - 1) * P
NP_, NF = 80, N // 80
SLOTS = T * P
BIG = float(1 << 20)
LN_EPS = 1e-5
CARRY = 2.0 ** 14

WUP = 2.0 ** 12
LN_UP = 2.0 ** 10
H_UP = 2.0 ** 14
FF_UP = 2.0 ** 13
Y_LN, Y_H = 2.0 ** 8, 2.0 ** 13
ROOT_D = 22.63


class Tile:

    def __init__(self, U, j, k, run=0):
        self.U, self.j, self.k, self.run = U, j, k, run

    def __add__(self, n):
        return Tile(self.U, self.j, self.k + n, self.run)

    @property
    def t(self):
        return self.j * self.U + self.k

    @property
    def n(self):
        return self.t + self.run * T

    def slot(self, ring):
        return self.k % ring

    def landed(self, ring):
        before = self.run * ((T + ring - 1 - self.k % ring) // ring)
        return 16 * (self.j * (self.U // ring) + self.k // ring + 1 + before)


def run_tiles(eng, U, tiles, stages, run=0):
    offs = [o for o, _ in stages]
    lo = U if min(offs) >= 0 else U * (-(-(2 - min(offs)) // U))
    trips = (tiles - 1 - max(max(offs), 0) - lo) // U

    def step(j, k, first, last):
        for off, f in stages:
            if first is None or 0 <= first + off < tiles:
                f(Tile(U, j, k + off, run))

    for t in range(-max(max(offs), 0), lo):
        step(0, t, t, None)
    with eng.Fori(lo // U, lo // U + trips) as j:
        for k in range(U):
            step(j, k, None, None)
    for t in range(lo + U * trips, tiles - min(min(offs), 0)):
        step(0, t, t, None)


def after(eng, sem, n):
    if not (isinstance(n, int) and n <= 0):
        eng.wait_ge(sem, n)


def hold(eng, done, *waits):
    for _, n in waits:
        if not isinstance(n, int):
            eng.lower_val(n)
    eng.wait_ge(done, 1)
    for sem, n in waits:
        if not (isinstance(n, int) and n <= 0):
            eng.wait_ge(sem, n)


class NaturalSems:

    def __init__(self, sem):
        self.x = [sem(f"p0_x{i}") for i in range(2)]
        self.ys = [sem(f"p0_ys{i}") for i in range(2)]
        self.s2 = [sem(f"p0_s2{i}") for i in range(2)]
        self.r = sem("p0_stats")
        self.dv = sem("p0_mean_var")
        self.ss = sem("p0_var_eps")
        self.sc = sem("p0_rstd")
        self.rr = sem("p0_rows")
        self.hhi = sem("p0_hhi")
        self.hlo = sem("p0_hlo")
        self.tr = sem("p0_turned")
        self.ht = sem("p0_ht")
        self.y = sem("p0_y")
        self.yhi = sem("p0_yhi")
        self.ylo = sem("p0_ylo")
        self.sp = sem("p0_own")
        self.sev = sem("p0_self")


class SlotSems:

    def __init__(self, sem, l):
        self.x = [sem(f"p{l}_x{i}") for i in range(2)]
        self.g = [sem(f"p{l}_g{i}") for i in range(2)]
        self.col = sem(f"p{l}_col")
        self.idx = sem(f"p{l}_idx")
        self.dv = sem(f"p{l}_idx_node")
        self.tr2 = sem(f"p{l}_idx_out")
        self.smat = sem(f"p{l}_smat")
        self.c0 = sem(f"p{l}_c0")
        self.chi = sem(f"p{l}_chi")
        self.clo = sem(f"p{l}_clo")
        self.agg = sem(f"p{l}_agg")
        self.r = sem(f"p{l}_r")
        self.rr = sem(f"p{l}_relu")
        self.dv2 = sem(f"p{l}_sumsq")
        self.ss = sem(f"p{l}_sumsq_max")
        self.sc = sem(f"p{l}_rnorm")
        if l < 3:
            self.ys = [sem(f"p{l}_ys{i}") for i in range(2)]
            self.s2 = [sem(f"p{l}_s2{i}") for i in range(2)]
            self.hhi = sem(f"p{l}_hhi")
            self.hlo = sem(f"p{l}_hlo")
            self.tr = sem(f"p{l}_turned")
            self.ht = sem(f"p{l}_ht")
            self.y = sem(f"p{l}_y")
            self.yhi = sem(f"p{l}_yhi")
            self.ylo = sem(f"p{l}_ylo")
            self.sp = sem(f"p{l}_own")
            self.sev = sem(f"p{l}_self")
        else:
            self.xg = [sem(f"p{l}_xg{i}") for i in range(2)]


class FfnSems:

    def __init__(self, sem):
        self.out = [sem(f"f3_out{i}") for i in range(2)]
        self.x2 = sem("f3_x2")
        self.tiny = sem("f3_tiny")
        self.v2 = sem("f3_v2")
        self.rs = sem("f3_rs")
        self.r2s = sem("f3_r2s")
        self.y = sem("f3_y")
        self.xhi = sem("f3_xhi")
        self.xlo = sem("f3_xlo")
        self.tx = sem("f3_tx")
        self.txc = sem("f3_txc")
        self.pre = sem("f3_pre")
        self.u = sem("f3_u")
        self.gel = sem("f3_gel")
        self.tiny2 = sem("f3_tiny2")
        self.lg = sem("f3_lg")
        self.th = sem("f3_th")
        self.w = sem("f3_w")
        self.wsp = sem("f3_wsp")
        self.z24 = sem("f3_z24")
        self.w24 = sem("f3_w24")
        self.hs = sem("f3_hs")
        self.hhi = sem("f3_hhi")
        self.hlo = sem("f3_hlo")
        self.th2 = sem("f3_th2")
        self.wtt = sem("f3_wtt")
        self.thc = sem("f3_thc")
        self.cmb = sem("f3_cmb")
        self.z = sem("f3_z")
        self.tiny3 = sem("f3_tiny3")
        self.zv = sem("f3_zv")
        self.zr = sem("f3_zr")
        self.o1 = sem("f3_o1")
        self.xob = sem("f3_xob")
        self.o = sem("f3_o")


def build(nc, x, src, dst, W_self, W_neigh, b, Wg, W1, b1, W2, b2, ln_g, ln_b, out_g, out_b, out):
    with ExitStack() as ctx:
        def sb(name, shape, dt=F32):
            return ctx.enter_context(nc.sbuf_tensor(name, shape, dt))

        def ps(name, shape, dt=F32):
            return ctx.enter_context(nc.psum_tensor(name, shape, dt))

        def sem(name):
            return ctx.enter_context(nc.semaphore(name))

        def dram(name, shape, dt):
            return nc.dram_tensor(name, shape, dt)

        Yd = [dram(f"y_rows{l}", [N, 2 * D], F16) for l in range(LAYERS)]
        Sd0 = dram("self_rows0", [N, D], F32)
        Sd = [None] + [dram(f"self_rows{l}", [SLOTS, D], F32) for l in (1, 2)]
        info = dram("node_info", [N, 2], F32)
        table = dram("slot_table", [SLOTS, 2], F32)

        NAMES = ["n0", "s0", "n1", "s1", "n2", "s2", "w1", "w2"]
        WT = {n: sb(f"w_{n}", [P, 2, KC, D], F16) for n in NAMES}
        wg16 = sb("wg16", [P, KC, 2 * EXPERTS], F16)
        b2s = sb("b2s", [3 * EXPERTS, D], F16)
        raw = sb("raw", [P, 2, KC, D])
        sq = sb("sq", [P, KC, D])
        ups = sb("ups", [P, 16])
        downs = sb("downs", [P, 16])
        nrm = sb("nrm", [P, 16])
        cmax = sb("cmax", [P, 16])
        bias = sb("bias", [P, LAYERS, D])
        b1b = sb("b1b", [P, D])
        ogb = sb("ogb", [P, D])
        obb = sb("obb", [P, D])
        wgr = sb("wgr", [P, KC, EXPERTS])
        wgs = sb("wgs", [P, KC, EXPERTS])
        bgb = sb("bgb", [P, EXPERTS])
        b2r = sb("b2r", [3 * EXPERTS, D])
        b2h = sb("b2h", [3 * EXPERTS, D], F16)
        sqb2 = sb("sqb2", [EXPERTS, D])
        rowmask = sb("rowmask", [3 * EXPERTS, 1])
        gcol = sb("gcol", [P, KC])
        bcol = sb("bcol", [P, KC])
        bmat = sb("bmat", [P, KC, P])
        small = sb("small", [P, 16])

        ones = sb("ones", [P, P])
        iden = sb("iden", [P, P])
        iden16 = sb("iden16", [P, P], F16)
        upper = sb("upper", [P, P])
        iota_i = sb("iota_i", [P, 3 * P], I32)
        iota_row = sb("iota_row", [P, P])
        iota127 = sb("iota127", [P, P])
        edge_no = sb("edge_no", [P, EPT])
        node_no_i = sb("node_no_i", [NP_, NF], I32)
        node_no = sb("node_no", [NP_, NF])
        tile128 = sb("tile128", [P, 1])
        rowval = sb("rowval", [P, 1])
        halfpow = sb("halfpow", [P, 2])
        mhalf2 = sb("mhalf2", [P, 2])
        expo = sb("expo", [P, 1], U32)

        colT = sb("colT", [P, T])
        srcT = sb("srcT", [P, T], U32)
        pinT = sb("pinT", [P, T], U32)
        poutT = sb("poutT", [P, T], U32)
        invdeg = sb("invdeg", [P, T])
        invs = sb("invs", [P, LAYERS, T])

        area = sb("area", [P, 12288])

        G = [sb(f"G{i}", [P, 2 * D], F16) for i in range(2)]
        Sm = [sb(f"Sm{i}", [P, P], F16) for i in range(2)]
        Sl = [sb(f"Sl{i}", [P, D]) for i in range(2)]
        X = [sb(f"X{i}", [P, D]) for i in range(2)]
        R = [sb(f"R{i}", [P, D]) for i in range(2)]
        RR = [sb(f"RR{i}", [P, D]) for i in range(2)]
        junk = sb("junk", [P, D])
        HH = [sb(f"HH{i}", [P, 2, D], F16) for i in range(2)]
        HT = [sb(f"HT{i}", [P, 2, KC, P], F16) for i in range(2)]
        YB = [sb(f"YB{i}", [P, 2 * D], F16) for i in range(2)]
        SB = [sb(f"SB{i}", [P, D]) for i in range(2)]
        idx = [[sb(f"idx{a}{i}", [P, 1], U32) for i in range(2)] for a in range(3)]
        colr = [sb(f"colr{i}", [P, 1]) for i in range(2)]
        ss = sb("ss", [P, 2])
        ssm = sb("ssm", [P, 2])
        scl = sb("scl", [P, 2])
        st6 = sb("st6", [P, 6])
        mv = sb("mv", [P, 2, 2])
        gi = sb("gi", [P, 2, 8], U32)
        gv = sb("gv", [P, 2, 16])

        psA = [ps(f"psA{i}", [P, D]) for i in range(2)]
        psT = [ps(f"psT{i}", [P, 2, KC, P], F16) for i in range(2)]
        psY = [ps(f"psY{i}", [P, D]) for i in range(2)]
        psS = [ps(f"psS{i}", [P, D]) for i in range(2)]

        s_const = sem("s_const")
        s_constv = sem("s_constv")
        s_wload = [sem(f"s_wload{i}") for i in range(2)]
        s_sq = sem("s_sq")
        s_sqb = sem("s_sqb")
        s_b1done = sem("s_b1done")
        s_cn = sem("s_cn")
        s_cmax = sem("s_cmax")
        s_nrm = sem("s_nrm")
        s_scale = sem("s_scale")
        s_whi = sem("s_whi")
        s_wlo = sem("s_wlo")
        s_bload = sem("s_bload")
        s_dv = sem("s_dv")
        s_pl = sem("s_pl")
        s_bm = sem("s_bm")
        s_ffb = sem("s_ffb")
        s_wgain = sem("s_wgain")
        s_epad = sem("s_epad")
        s_eload = sem("s_eload")
        s_tab = sem("s_tab")
        s_tabp = sem("s_tabp")
        s_infoz = sem("s_infoz")
        s_self2 = [sem(f"s_self2_{i}") for i in range(2)]
        s_sc = [sem(f"s_scat{i}") for i in range(2)]
        s_nload = sem("s_nload")
        s_tload = sem("s_tload")
        s_tinit = sem("s_tinit")
        s_scat_in = sem("s_scat_in")
        s_scat_cp = sem("s_scat_cp")
        s_tables = sem("s_tables")

        def view(at, parts, n, dt=F32):
            v = area[0:parts, at:at + n]
            return v if dt is F32 else v.bitcast(dt)

        eDi, eNi, eSi = (view(P * i, T, EPT, I32) for i in range(3))
        eD, eN, eL, eCS, eEX, eM, eT1 = (view(P * (3 + i), T, P) for i in range(7))
        eCOL, eSLOT, eDEG, eDST, eSRC, eSC = (view(P * (10 + i), T, P) for i in range(6))
        pm_row = view(P * 16, 1, P)
        pm_col = view(P * 17, T, 2)
        dstT = view(P * 18, P, 80, U32)
        infoT = view(P * 19, P, 160).rearrange("p (t two) -> p t two", two=2)
        cpI = [view(P * (21 + i), P, 8, U32) for i in range(2)]
        cpV = [view(P * (21 + i) + 16, P, 16).rearrange("p (t two) -> p t two", two=2) for i in range(2)]
        zero = view(P * 23, NP_, 2 * NF)
        tinit = view(P * 25, T, 2 * P).rearrange("p (k two) -> p k two", two=2)
        stot = view(P * 27, T, 1)
        smat = view(P * 28, T, NP_)
        iu = view(P * 29, T, 2 * T)
        NB = 0
        nI = view(NB, NP_, 2 * NF).rearrange("p (k two) -> p k two", two=2)
        nZ, nCZ, nR, nSL, nDG = (view(NB + P * (2 + i), NP_, NF) for i in range(5))
        Fj = view(NB + P * 7, NP_, T)
        S1 = view(NB + P * 8, NP_, T)
        slotT = view(P * 9, P, 80, U32)
        ndT = view(P * 10, P, 160).rearrange("p (t two) -> p t two", two=2)
        tI = view(P * 12, T, 2 * P).rearrange("p (k two) -> p k two", two=2)
        tA = view(P * 14, T, P)
        tB = view(P * 15, T, P)
        permf = view(P * 16, P, T)
        degf = view(P * 17, P, T)
        cube = raw.rearrange("p a c n -> p (a c n)")

        M_OF = {"n0": (W_neigh, 0), "s0": (W_self, 0), "n1": (W_neigh, 1), "s1": (W_self, 1),
                "n2": (W_neigh, 2), "s2": (W_self, 2)}

        C = {n: i for i, n in enumerate(NAMES)}
        CG, CB = 8, 9
        FINAL = 10
        NPREP = 10

        ctx.enter_context(nc.allow_non_contiguous_dma(reason="the layernorm's gain and bias, as columns"))
        block = ctx.enter_context(nc.Block())
        EX_ = EXPERTS

        p0, p1, p3 = NaturalSems(sem), SlotSems(sem, 1), SlotSems(sem, 3)
        ph = [p0, p1, p1, p3]
        f3 = FfnSems(sem)

        def ring(at, n):
            return [area[:, at + D * i:at + D * (i + 1)] for i in range(n)]

        X2 = ring(0, 6)
        YF = ring(6 * D, 6)
        PRE = ring(12 * D, 2)
        GEL = ring(14 * D, 2)
        HS = ring(16 * D, 2)
        Z = ring(18 * D, 2)
        O1 = ring(20 * D, 2)
        XOB = ring(22 * D, 2)
        rawf = raw.rearrange("p a c n -> p (a c n)")
        OUT = [rawf[:, D * i:D * (i + 1)] for i in range(2)]
        FH = [rawf[:, D * (2 + i):D * (3 + i)].bitcast(F16).rearrange("p (a n) -> p a n", a=2) for i in range(2)]
        FT = [rawf[:, D * (4 + i):D * (5 + i)].bitcast(F16).rearrange("p (a c n) -> p a c n", a=2, c=KC)
              for i in range(2)]
        W24 = [sb(f"W24_{i}", [P, 3 * EXPERTS], F16) for i in range(2)]
        WTT = [sb(f"WTT{i}", [3 * EXPERTS, P], F16) for i in range(2)]
        wsc = sb("wsc", [P, 2, 8])
        mv3 = sb("mv3", [P, 2, 2])
        vv = sb("vv", [P, 2, 2])
        rs = sb("rs", [P, 2, 2])
        r2s = sb("r2s", [P, 2])
        zv = sb("zv", [P, 2])
        zr = sb("zr", [P, 2])
        zm = sb("zm", [P, 2, 2])
        st6b = sb("st6b", [P, 6])
        psX = psT[0]
        psH = psT[1]
        psG = psA[1]
        psG16 = psA[1][:, :].bitcast(F16)

        def products(eng, acc, lhs, w, stop=True):
            n = 0
            for c in range(KC):
                for a, bpart in ((0, 0), (0, 1), (1, 0)):
                    mm = eng.matmul(acc, lhs[:, a, c, :], w[:, bpart, c, :], start=(n == 0),
                                    stop=(stop and n == 3 * KC - 1))
                    n += 1
            return mm

        @block.sync
        def _(sp):
            sp.dma_start(bcol[:, :], ln_b.rearrange("(c p) -> p c", p=P)).then_inc(s_bload, 16)
            sp.dma_start(gcol[:, :], ln_g.rearrange("(c p) -> p c", p=P)).then_inc(s_bload, 16)
            for l in range(LAYERS):
                sp.dma_start(bias[:, l, :], b[l, :].partition_broadcast(P)).then_inc(s_bload, 16)
            sp.dma_start(b1b[:, :], b1.rearrange("e h -> (e h)").partition_broadcast(P)).then_inc(s_bload, 16)
            sp.dma_start(ogb[:, :], out_g.partition_broadcast(P)).then_inc(s_bload, 16)
            sp.dma_start(obb[:, :], out_b.partition_broadcast(P)).then_inc(s_bload, 16)
            sp.dma_start(wgr[:, :, :], Wg.rearrange("(c p) e -> p c e", p=P)).then_inc(s_bload, 16)
            for i in range(3):
                sp.dma_start(b2r[EX_ * i:EX_ * (i + 1), :], b2[:, :]).then_inc(s_bload, 16)
            sp.wait_ge(s_epad, 3)
            full = (E // EPT) * EPT
            for to, frm, count in ((eDi, dst, E), (eSi, src, E), (eNi, dst[1:E], E - 1)):
                sp.dma_start(to[0:T - 1, :], frm[0:full].rearrange("(t k) -> t k", k=EPT)).then_inc(s_eload, 16)
                sp.dma_start(to[T - 1:T, 0:count - full], frm[full:count].rearrange("(a k) -> a k", a=1)
                             ).then_inc(s_eload, 16)
            for m, name in enumerate(NAMES):
                if m >= 2:
                    sp.wait_ge(s_wlo, m - 1)
                    sp.wait_ge(s_whi, m - 1)
                to = raw[:, m % 2, :, :]
                if name == "w1":
                    for c in range(KC):
                        sp.dma_start(to[:, c, :].rearrange("p (e h) -> p e h", e=EX_),
                                     W1[:, c * P:(c + 1) * P, :].rearrange("e p h -> p e h")).then_inc(s_wload[m % 2], 16)
                elif name == "w2":
                    w2f = W2.rearrange("e h d -> (e h) d")
                    for c in range(KC):
                        sp.dma_start(to[:, c, :], w2f[c * P:(c + 1) * P, :]).then_inc(s_wload[m % 2], 16)
                else:
                    w, l = M_OF[name]
                    for c in range(KC):
                        sp.dma_start(to[:, c, :], w[l, c * P:(c + 1) * P, :]).then_inc(s_wload[m % 2], 16)
            sp.wait_ge(s_infoz, 2)
            sp.dma_start(info.rearrange("(p k) two -> p (k two)", p=NP_), zero).then_inc(s_tinit, 16)
            sp.dma_start(table.rearrange("(p k) two -> p k two", p=T), tinit).then_inc(s_tinit, 16)

            s = ph[0]

            def load_x(t):
                after(sp, s.rr, (t + -1).n)
                rows = P if not (isinstance(t.t, int) and t.t == TN - 1) else NLAST
                sp.dma_start(X[t.slot(2)][0:rows, :], x[bass.ds(t.t * P, rows), :]).then_inc(s.x[t.slot(2)], 16)

            def store(t):
                rows = P if not (isinstance(t.t, int) and t.t == TN - 1) else NLAST
                sp.wait_ge(s.yhi, (t + 1).n)
                sp.wait_ge(s.ylo, (t + 1).n)
                sp.dma_start(Yd[0][bass.ds(t.t * P, rows), :], YB[t.slot(2)][0:rows, :]).then_inc(s.ys[t.slot(2)], 16)
                sp.wait_ge(s.sev, (t + 1).n)
                sp.dma_start(Sd0[bass.ds(t.t * P, rows), :], SB[t.slot(2)][0:rows, :]).then_inc(s.s2[t.slot(2)], 16)

            run_tiles(sp, 2, TN, [(4, load_x), (0, store)])
            for l in (1, 2):
                s = ph[l]
                q = ph[l - 1]
                if l == 2:
                    for i in range(2):
                        sp.wait_ge(q.s2[i], 16 * ((T + 1 - i) // 2))

                def load_self(t, s=s, l=l):
                    after(sp, s.r, (t + -1).n)
                    sp.dma_start(Sl[t.slot(2)][:, :], Sd[l - 1][bass.ds(t.t * P, P), :]).then_inc(s_self2[t.slot(2)], 16)

                def store_self(t, s=s, l=l):
                    sp.wait_ge(s.sev, (t + 1).n)
                    sp.dma_start(Sd[l][bass.ds(t.t * P, P), :], SB[t.slot(2)][:, :]).then_inc(s.s2[t.slot(2)], 16)

                if l == 1:
                    run_tiles(sp, 2, T, [(0, store_self)])
                else:
                    run_tiles(sp, 2, T, [(0, store_self), (5, load_self)], 1)
            s = ph[3]
            for i in range(2):
                sp.wait_ge(ph[2].s2[i], 2 * 16 * ((T + 1 - i) // 2))

            def load_self3(t):
                after(sp, s.r, (t + -1).n)
                sp.dma_start(Sl[t.slot(2)][:, :], Sd[2][bass.ds(t.t * P, P), :]).then_inc(s.x[t.slot(2)], 16)

            run_tiles(sp, 6, T, [(6, load_self3)])

        @block.gpsimd
        def _(pool):
            node_limit = pool.alloc_register("node_limit")
            slot_limit = pool.alloc_register("slot_limit")
            pool.reg_mov(node_limit, N - 1)
            pool.reg_mov(slot_limit, SLOTS - 1)
            n = [0]

            def link(ins):
                n[0] += 1
                ins.then_inc(s_pl, 1)
                pool.wait_ge(s_pl, n[0])

            pool.memset(ones[:, :], 1.0).then_inc(s_const, 1)
            link(pool.memset(iden[:, :], 0.0))
            link(pool.affine_select(out=iden[:, :], in_=iden[:, :], compare_op=ALU.not_equal, fill=1.0, base=0,
                                    pattern=[[-1, P]], channel_multiplier=1))
            link(pool.memset(upper[:, :], 1.0))
            link(pool.affine_select(out=upper[:, :], in_=upper[:, :], compare_op=ALU.is_gt, fill=0.0, base=0,
                                    pattern=[[1, P]], channel_multiplier=-1))
            link(pool.iota(iota_i[:, 0:P], [[1, P]], base=0, channel_multiplier=0))
            link(pool.iota(iota_i[:, P:2 * P], [[EPT, P]], base=0, channel_multiplier=0))
            link(pool.iota(iota_i[:, 2 * P:2 * P + EPT], [[1, EPT]], base=1, channel_multiplier=EPT))
            link(pool.iota(iota_i[:, 3 * P - 1:3 * P], [[1, 1]], base=0, channel_multiplier=P))
            link(pool.iota(node_no_i[:, :], [[1, NF]], base=0, channel_multiplier=NF))
            link(pool.memset(rowval[:, :], 1.0))
            link(pool.memset(rowval[0:1, :], CARRY))
            link(pool.memset(halfpow[:, 0:1], 0.5))
            link(pool.memset(halfpow[:, 1:2], -0.5))
            link(pool.memset(mhalf2[:, :], -0.5))
            link(pool.memset(rowmask[:, :], 1.0))
            pool.memset(rowmask[0:1, :], 1.0).then_inc(s_const, 1)
            for m in range(NPREP - 1):
                pool.wait_ge(s_cmax, m + 1)
                pool.tensor_tensor(nrm[:, m:m + 1], cmax[:, m:m + 1], halfpow[:, 0:1], ALU.pow).then_inc(s_nrm, 1)

            def scatter_pass(index, value, to, limit, rows, base):
                def one(g, i, landed, copied):
                    if landed is not None:
                        pool.wait_ge(s_sc[i], landed)
                    pool.tensor_copy(cpI[i][0:rows, :], index[0:rows, bass.ds(g * 8, 8)]).then_inc(s_scat_cp, 1)
                    pool.tensor_copy(cpV[i][0:rows, :, :], value[0:rows, bass.ds(g * 8, 8), :]).then_inc(s_scat_cp, 1)
                    hold(pool, s_const, (s_scat_cp, copied))
                    for k in range(8):
                        pool.indirect_dma_start(
                            to[:, :], bass.IndirectOffsetOnAxis(ap=cpI[i][0:rows, k:k + 1], axis=0),
                            cpV[i][0:rows, k, :], None, bounds_check=limit, oob_is_err=False).then_inc(s_sc[i], 16)

                one(0, 0, None if base == 0 else base * 5 * 128, base * 20 + 2)
                one(1, 1, None if base == 0 else base * 5 * 128, base * 20 + 4)
                with pool.Fori(1, 5) as j:
                    one(j * 2, 0, base * 5 * 128 + j * 128, base * 20 + j * 4 + 2)
                    one(j * 2 + 1, 1, base * 5 * 128 + j * 128, base * 20 + j * 4 + 4)

            pool.wait_ge(s_tinit, 32)
            pool.wait_ge(s_scat_in, 1)
            scatter_pass(dstT, infoT, info, node_limit, P, 0)
            for i in range(2):
                pool.wait_ge(s_sc[i], 640)
            pool.dma_start(nI, info.rearrange("(p k) two -> p k two", p=NP_)).then_inc(s_nload, 16)
            pool.wait_ge(s_scat_in, 2)
            scatter_pass(slotT, ndT, table, slot_limit, NF, 1)
            for i in range(2):
                pool.wait_ge(s_sc[i], 1280)
            pool.dma_start(tI, table.rearrange("(p k) two -> p k two", p=T)).then_inc(s_tload, 16)

            s = ph[0]

            def dev0(t):
                pool.wait_ge(s.ss, (t + 1).n)
                after(pool, s.rr, (t + -1).n)
                pool.tensor_tensor(scl[:, t.slot(2):t.slot(2) + 1], ssm[:, t.slot(2):t.slot(2) + 1],
                                   halfpow[:, 1:2], ALU.pow).then_inc(s.sc, 1)

            run_tiles(pool, 2, TN, [(3, dev0)])
            pool.wait_ge(s_tables, 1)

            for l in (1, 2, 3):
                s = ph[l]
                U = 2 if l < 3 else 6
                last = ph[l - 1]
                tiles = TN if l == 1 else T
                for i in range(2):
                    pool.wait_ge(last.ys[i], (2 if l == 3 else 1) * 16 * ((tiles + 1 - i) // 2))
                    if l == 1:
                        pool.wait_ge(last.s2[i], 16 * ((tiles + 1 - i) // 2))

                def gather(t, s=s, l=l):
                    i = t.slot(2)
                    after(pool, s.agg, (t + -1).n)
                    pool.tensor_copy(idx[0][i][:, :], srcT[:, bass.ds(t.t, 1)]).then_inc(s.idx, 1)
                    pool.tensor_copy(colr[i][:, :], colT[:, bass.ds(t.t, 1)]).then_inc(s.col, 1)
                    hold(pool, s_const, (s.col, (t + 1).n))
                    pool.tensor_scalar(Sm[i][:, :], iota_row[:, :], colr[i][:, 0:1], rowval[:, 0:1],
                                       ALU.is_equal, ALU.mult).then_inc(s.smat, 1)
                    hold(pool, s_const, (s.idx, (t + 1).n))
                    pool.indirect_dma_start(G[i][:, :], None, Yd[l - 1][:, :],
                                            bass.IndirectOffsetOnAxis(ap=idx[0][i][:, 0:1], axis=0),
                                            bounds_check=node_limit, oob_is_err=False).then_inc(s.g[i], 16)

                def by_node(t, s=s, l=l):
                    i = t.slot(2)
                    if l == 1:
                        after(pool, s.r, (t + -1).n)
                    else:
                        after(pool, f3.x2, (t + -1).n)
                    pool.tensor_copy(idx[1][i][:, :], pinT[:, bass.ds(t.t, 1)]).then_inc(s.dv, 1)
                    to, frm = (Sl[i], Sd0) if l == 1 else (X[i], x)
                    hold(pool, s_const, (s.dv, (t + 1).n))
                    pool.indirect_dma_start(to[:, :], None, frm[:, :],
                                            bass.IndirectOffsetOnAxis(ap=idx[1][i][:, 0:1], axis=0),
                                            bounds_check=node_limit, oob_is_err=False
                                            ).then_inc((s.x if l == 1 else s.xg)[i], 16)

                def norm(t, s=s, l=l):
                    i = t.slot(2)
                    pool.wait_ge(s.ss, (t + 1).n)
                    if l < 3:
                        after(pool, s.hlo, (t + -1).n)
                    else:
                        after(pool, f3.x2, (t + -1).n)
                    pool.tensor_tensor(scl[:, i:i + 1], ssm[:, i:i + 1], halfpow[:, 1:2], ALU.pow).then_inc(s.sc, 1)

                def put_y(t, s=s, l=l):
                    i = t.slot(2)
                    if not (isinstance(t.t, int) and t.t < 2):
                        pool.wait_ge(s.ys[i], (t + -2).landed(2))
                    pool.tensor_copy(idx[2][i][:, :], poutT[:, bass.ds(t.t, 1)]).then_inc(s.tr2, 1)
                    hold(pool, s_const, (s.tr2, (t + 1).n), (s.yhi, (t + 1).n), (s.ylo, (t + 1).n))
                    pool.indirect_dma_start(Yd[l][:, :], bass.IndirectOffsetOnAxis(ap=idx[2][i][:, 0:1], axis=0),
                                            YB[i][:, :], None, bounds_check=node_limit, oob_is_err=False
                                            ).then_inc(s.ys[i], 16)

                if l < 3:
                    st = [(0, put_y), (3, norm), (5, gather)]
                    if l == 1:
                        st.append((5, by_node))
                    run_tiles(pool, U, T, st, l - 1)
            s = ph[3]

            def rs_of(t):
                i = t.slot(2)
                pool.wait_ge(f3.v2, (t + 1).n)
                after(pool, f3.xlo, (t + -1).n)
                pool.tensor_tensor(rs[:, i, :], vv[:, i, :], mhalf2[:, :], ALU.pow).then_inc(f3.rs, 1)
                hold(pool, s_const, (f3.rs, (t + 1).n))
                pool.tensor_scalar(r2s[:, i:i + 1], rs[:, i, 1:2], LN_UP, 1.0, ALU.mult, ALU.mult).then_inc(f3.r2s, 1)

            def xob(t):
                pool.wait_ge(f3.x2, (t + 1).n)
                after(pool, f3.o, (t + -1).n)
                pool.tensor_tensor(XOB[t.slot(2)], X2[t.slot(6)], obb[:, :], ALU.add).then_inc(f3.xob, 1)

            def hs_of(t):
                pool.wait_ge(f3.gel, (t + 1).n)
                pool.wait_ge(f3.wsp, (t + 1).n)
                after(pool, f3.hlo, (t + -1).n)
                i = t.slot(2)
                pool.tensor_tensor(HS[i].rearrange("p (e h) -> p e h", e=EX_),
                                   GEL[i].rearrange("p (e h) -> p e h", e=EX_),
                                   wsc[:, i, :].unsqueeze(2).to_broadcast([P, EX_, HIDDEN]), ALU.mult
                                   ).then_inc(f3.hs, 1)

            def zr_of(t):
                i = t.slot(2)
                pool.wait_ge(f3.zv, (t + 1).n)
                after(pool, f3.o, (t + -1).n)
                pool.tensor_tensor(zr[:, i:i + 1], zv[:, i:i + 1], halfpow[:, 1:2], ALU.pow).then_inc(f3.zr, 1)

            def put_out(t):
                i = t.slot(2)
                if not (isinstance(t.t, int) and t.t < 2):
                    pool.wait_ge(f3.out[i], (t + -2).landed(2))
                pool.tensor_copy(idx[2][i][:, :], poutT[:, bass.ds(t.t, 1)]).then_inc(ph[3].tr2, 1)
                hold(pool, s_const, (ph[3].tr2, (t + 1).n), (f3.o, (t + 1).n))
                pool.indirect_dma_start(out[:, :], bass.IndirectOffsetOnAxis(ap=idx[2][i][:, 0:1], axis=0),
                                        OUT[i], None, bounds_check=node_limit, oob_is_err=False
                                        ).then_inc(f3.out[i], 16)

            run_tiles(pool, 6, T, [(0, hs_of), (-2, zr_of), (-2, xob), (-2, put_out), (4, norm), (3, rs_of),
                                   (6, gather), (5, by_node)])
            for i in range(2):
                pool.wait_ge(f3.out[i], 16 * ((T + 1 - i) // 2))

        @block.scalar
        def _(act):
            act.wait_ge(s_bload, 0 + 16 * 12)
            for m, name in enumerate(NAMES):
                act.wait_ge(s_wload[m % 2], 64 * (m // 2 + 1))
                if name == "w1":
                    act.wait_ge(s_wgain, 1)
                after(act, s_cn, m)
                act.activation(sq[:, :, :], raw[:, m % 2, :, :], ACT.Square).then_inc(s_sq, 1)
                if name == "w2":
                    act.activation(sqb2[:, :], b2r[0:EX_, :], ACT.Square).then_inc(s_sqb, 1)
                act.wait_ge(s_scale, m + 1)
                act.activation(WT[name][:, 0, :, :], raw[:, m % 2, :, :], ACT.Copy, scale=ups[:, m:m + 1]
                               ).then_inc(s_whi, 1)
            act.wait_ge(s_wgain, 2)
            act.wait_ge(s_cn, 8)
            act.activation(sq[:, 0, 0:KC * EX_].rearrange("p (c e) -> p c e", c=KC), wgs[:, :, :], ACT.Square
                           ).then_inc(s_sq, 1)

            s = ph[0]

            def hi0(t):
                i = t.slot(2)
                act.wait_ge(s.rr, (t + 1).n)
                after(act, s.tr, (t + -1).n)
                act.activation(HH[i][:, 0, :], R[i][:, :], ACT.Copy, scale=LN_UP).then_inc(s.hhi, 1)

            def yhi(t, l):
                i = t.slot(2)
                s = ph[l]
                act.wait_ge(s.y, (t + 1).n)
                if not (isinstance(t.t, int) and t.t < 2):
                    act.wait_ge(s.ys[i], (t + -2).landed(2))
                k = Y_LN / (WUP * LN_UP) if l == 0 else Y_H / (WUP * H_UP)
                act.activation(YB[i][:, 0:D], psY[i][:, :], ACT.Copy, scale=k).then_inc(s.yhi, 1)

            run_tiles(act, 2, TN, [(2, hi0), (0, lambda t: yhi(t, 0))])

            def carry_hi(t, l):
                s = ph[l]
                i, o = t.slot(2), (t + 1).slot(2)
                if isinstance(t.t, int) and t.t == T - 1:
                    return
                act.wait_ge(s.agg, (t + 1).n)
                act.wait_ge(s.g[o], (t + 1).landed(2))
                act.activation(G[o][0:1, 0:D], psA[0 if l == 3 else i][0:1, :], ACT.Copy, scale=1.0 / CARRY
                               ).then_inc(s.chi, 1)

            def relu(t, l):
                s = ph[l]
                i = t.slot(2)
                act.wait_ge(s.r, (t + 1).n)
                if l < 3:
                    after(act, s.hlo, (t + -1).n)
                else:
                    after(act, f3.x2, (t + -1).n)
                act.activation(RR[i][:, :], R[i][:, :], ACT.Relu).then_inc(s.rr, 1)

            def hhi(t, l):
                s = ph[l]
                i = t.slot(2)
                act.wait_ge(s.sc, (t + 1).n)
                act.wait_ge(s.rr, (t + 1).n)
                after(act, s.tr, (t + -1).n)
                act.activation(HH[i][:, 0, :], RR[i][:, :], ACT.Copy, scale=scl[:, i:i + 1]).then_inc(s.hhi, 1)

            def first_carry(l):
                act.wait_ge(ph[l].g[0], Tile(2, 0, 0, 1 if l == 2 else 0).landed(2))
                act.activation(G[0][0:1, :], G[0][0:1, :], ACT.Copy, scale=0.0).then_inc(ph[l].c0, 1)

            for l in (1, 2):
                first_carry(l)
                run_tiles(act, 2, T, [(2, lambda t, l=l: hhi(t, l)), (0, lambda t, l=l: yhi(t, l)),
                                      (3, lambda t, l=l: carry_hi(t, l)), (3, lambda t, l=l: relu(t, l))], l - 1)
            first_carry(3)

            def xhi(t):
                i = t.slot(2)
                act.wait_ge(f3.y, (t + 1).n)
                act.wait_ge(f3.r2s, (t + 1).n)
                after(act, f3.tx, (t + -1).n)
                act.activation(HH[i][:, 0, :], YF[t.slot(6)], ACT.Copy, scale=r2s[:, i:i + 1]).then_inc(f3.xhi, 1)

            def gelu(t):
                i = t.slot(2)
                act.wait_ge(f3.u, (t + 1).n)
                after(act, f3.hs, (t + -1).n)
                act.activation(GEL[i], PRE[i], ACT.Gelu_apprx_tanh).then_inc(f3.gel, 1)

            def gate(t):
                i = t.slot(2)
                act.wait_ge(f3.lg, (t + 1).n)
                after(act, f3.w, (t + -1).n)
                act.activation(gv[:, i, 9:10], gv[:, i, 8:9], ACT.Tanh, scale=0.5).then_inc(f3.th, 1)

            def fhi(t):
                i = t.slot(2)
                act.wait_ge(f3.hs, (t + 1).n)
                after(act, f3.th2, (t + -1).n)
                act.activation(FH[i][:, 0, :], HS[i], ACT.Copy).then_inc(f3.hhi, 1)

            run_tiles(act, 6, T, [(2, xhi), (0, gelu), (0, gate), (0, fhi),
                                  (4, lambda t: carry_hi(t, 3)), (4, lambda t: relu(t, 3))])

        @block.vector
        def _(dve):
            n = [0]

            def link(ins):
                n[0] += 1
                ins.then_inc(s_dv, 1)
                dve.wait_ge(s_dv, n[0])

            dve.memset(eDi, -1).then_inc(s_epad, 1)
            dve.memset(eNi, -1).then_inc(s_epad, 1)
            dve.memset(eSi, 0).then_inc(s_epad, 1)
            dve.memset(zero, 0.0).then_inc(s_infoz, 1)
            link(dve.memset(tinit[:, :, 0:1], BIG))
            dve.memset(tinit[:, :, 1:2], 1.0).then_inc(s_infoz, 1)
            dve.wait_ge(s_const, 2)
            link(dve.tensor_copy(iden16[:, :], iden[:, :]))
            link(dve.tensor_copy(iota_row[:, :], iota_i[:, 0:P]))
            link(dve.tensor_copy(iota127[:, :], iota_i[:, P:2 * P]))
            link(dve.tensor_copy(edge_no[:, :], iota_i[:, 2 * P:2 * P + EPT]))
            link(dve.tensor_copy(tile128[:, :], iota_i[:, 3 * P - 1:3 * P]))
            link(dve.tensor_copy(node_no[:, :], node_no_i[:, :]))
            link(dve.tensor_reduce(small[0:24, 0:1], iden[0:24, 8:16], AX.X, ALU.add))
            dve.tensor_scalar(rowmask[:, :], small[0:24, 0:1], -1.0, 1.0, ALU.mult, ALU.add).then_inc(s_constv, 1)

            def scales(c, k):
                dve.wait_ge(s_nrm, k)
                bits = nrm[:, c:c + 1].bitcast(U32)
                link(dve.tensor_scalar(expo[:, :], bits, 0x7F800000, None, ALU.bitwise_and))
                link(dve.tensor_scalar(downs[:, c:c + 1], expo[:, :].bitcast(F32), 0.5 / WUP, None, ALU.mult))
                link(dve.tensor_scalar(ups[:, c:c + 1].bitcast(U32), expo[:, :], 0x7F800000, None, ALU.bitwise_xor))
                return dve.tensor_scalar(ups[:, c:c + 1], ups[:, c:c + 1], WUP, None, ALU.mult)

            dve.wait_ge(s_bload, 16 * 12)
            for c in range(KC):
                link(dve.tensor_scalar(bmat[:, c, :], ones[:, :], bcol[:, c:c + 1], None, ALU.mult))
            dve.tensor_scalar(small[:, 0:1], ones[:, 0:1], 1.0, None, ALU.mult).then_inc(s_bm, 1)
            for m, name in enumerate(NAMES):
                w = raw[:, m % 2, :, :]
                dve.wait_ge(s_wload[m % 2], 64 * (m // 2 + 1))
                if name == "w1":
                    dve.wait_ge(s_ffb, 1)
                    dve.tensor_tensor(b1b[:, :], psA[1][:, :], b1b[:, :], ALU.add).then_inc(s_b1done, 1)
                    dve.wait_ge(s_b1done, 1)
                    dve.wait_ge(s_ffb, 2)
                    link(dve.tensor_copy(bgb[:, :], psA[1][:, 0:EX_]))
                    for c in range(KC):
                        link(dve.tensor_scalar(w[:, c, :], w[:, c, :], gcol[:, c:c + 1], None, ALU.mult))
                    dve.tensor_scalar(small[:, 0:1], ones[:, 0:1], 1.0, None, ALU.mult).then_inc(s_wgain, 1)
                    for c in range(KC):
                        link(dve.tensor_scalar(wgs[:, c, :], wgr[:, c, :], gcol[:, c:c + 1], None, ALU.mult))
                    dve.tensor_scalar(small[:, 0:1], ones[:, 0:1], 1.0, None, ALU.mult).then_inc(s_wgain, 1)
                dve.wait_ge(s_cn, m + 1)
                link(dve.tensor_reduce(cmax[:, m:m + 1], psA[0][:, :], AX.X, ALU.max))
                dve.tensor_scalar(cmax[:, m:m + 1], cmax[:, m:m + 1], 1e-30, None, ALU.max).then_inc(s_cmax, 1)
                scales(m, m + 1).then_inc(s_scale, 1)
                dve.wait_ge(s_scale, m + 1)
                dve.wait_ge(s_whi, m + 1)
                dve.scalar_tensor_tensor(WT[name][:, 1, :, :].rearrange("p c n -> p (c n)"),
                                         w.rearrange("p c n -> p (c n)"), ups[:, m:m + 1],
                                         WT[name][:, 0, :, :].rearrange("p c n -> p (c n)"),
                                         ALU.mult, ALU.subtract).then_inc(s_wlo, 1)
            dve.wait_ge(s_cn, 9)
            link(dve.tensor_reduce(cmax[:, CG:CG + 1], psA[0][:, 0:EX_], AX.X, ALU.max))
            dve.tensor_scalar(cmax[:, CG:CG + 1], cmax[:, CG:CG + 1], 1e-30, None, ALU.max).then_inc(s_cmax, 1)
            link(scales(CG, 9))
            link(dve.tensor_scalar(wg16[:, :, 0:EX_], wgs[:, :, :], ups[:, CG:CG + 1], None, ALU.mult))
            link(dve.scalar_tensor_tensor(wg16[:, :, EX_:2 * EX_], wgs[:, :, :], ups[:, CG:CG + 1],
                                          wg16[:, :, 0:EX_], ALU.mult, ALU.subtract))
            link(dve.tensor_reduce(small[:, 2:3], b1b[:, :], AX.X, ALU.max, apply_absolute_value=True))
            c1 = C["w1"]
            link(dve.tensor_scalar(small[:, 3:4], nrm[:, c1:c1 + 1], ROOT_D, small[:, 2:3], ALU.mult, ALU.add))
            link(dve.tensor_scalar(small[:, 3:4], small[:, 3:4], 1.0, None, ALU.max))
            link(dve.tensor_scalar(expo[:, :], small[:, 3:4].bitcast(U32), 0x7F800000, None, ALU.bitwise_and))
            link(dve.tensor_scalar(downs[:, CB:CB + 1], expo[:, :].bitcast(F32), 0.5 / FF_UP, None, ALU.mult))
            link(dve.tensor_scalar(ups[:, CB:CB + 1].bitcast(U32), expo[:, :], 0x7F800000, None, ALU.bitwise_xor))
            link(dve.tensor_scalar(ups[:, CB:CB + 1], ups[:, CB:CB + 1], FF_UP, None, ALU.mult))
            c2 = C["w2"]
            link(dve.tensor_scalar(downs[:, FINAL:FINAL + 1], downs[:, CB:CB + 1], downs[:, c2:c2 + 1], None, ALU.mult))
            for c in (CG, c1, C["s0"]):
                link(dve.tensor_scalar(downs[:, c:c + 1], downs[:, c:c + 1], 1.0 / LN_UP, None, ALU.mult))
            for name in ("s1", "s2"):
                c = C[name]
                link(dve.tensor_scalar(downs[:, c:c + 1], downs[:, c:c + 1], 1.0 / H_UP, None, ALU.mult))
            link(dve.tensor_scalar(b2h[:, :], b2r[:, :], ups[0:24, c2:c2 + 1], None, ALU.mult))
            lo24 = sq[0:24, 1, :]
            hi24 = sq[0:24, 2, :]
            link(dve.scalar_tensor_tensor(lo24, b2r[:, :], ups[0:24, c2:c2 + 1], b2h[:, :], ALU.mult, ALU.subtract))
            link(dve.tensor_scalar(hi24, b2h[:, :], rowmask[:, 0:1], None, ALU.mult))
            link(dve.tensor_scalar(small[0:24, 4:5], rowmask[:, 0:1], -1.0, 1.0, ALU.mult, ALU.add))
            link(dve.scalar_tensor_tensor(b2s[:, :], lo24, small[0:24, 4:5], hi24, ALU.mult, ALU.add))

            dve.wait_ge(s_eload, 96)
            r1 = slice(0, EPT)
            link(dve.tensor_copy(eD[:, r1], eDi))
            link(dve.tensor_copy(eN[:, r1], eNi))
            link(dve.tensor_copy(eSRC[:, 1:P], eSi))
            link(dve.memset(eSRC[:, 0:1], 0.0))
            link(dve.tensor_tensor(eL[:, r1], eD[:, r1], eN[:, r1], ALU.not_equal))
            link(dve.tensor_tensor_scan(eCS[:, r1], ones[0:T, r1], eL[:, r1], 0.0, ALU.mult, ALU.add))
            link(dve.tensor_copy(stot, eCS[:, EPT - 1:EPT]))
            link(dve.tensor_tensor(eEX[:, r1], eCS[:, r1], eL[:, r1], ALU.subtract))
            link(dve.tensor_scalar(eT1[:, r1], eEX[:, r1], stot, None, ALU.is_lt))
            link(dve.scalar_tensor_tensor(eCOL[:, 1:P], eEX[:, r1], 1.0, eT1[:, r1], ALU.add, ALU.mult))
            link(dve.tensor_copy(eCOL[:, 0:1], eCOL[:, 1:2]))
            link(dve.tensor_tensor(eM[:, r1], eL[:, r1], edge_no[0:T, :], ALU.mult))
            link(dve.memset(eSC[:, 0:1], 0.0))
            link(dve.tensor_tensor_scan(eSC[:, 1:P], eM[:, r1], eM[:, r1], 0.0, ALU.max, ALU.max))
            dve.tensor_copy(pm_col[:, 0:1], eSC[:, P - 1:P]).then_inc(s_tab, 1)
            dve.wait_ge(s_tabp, 1)
            link(dve.tensor_copy(eT1[0:1, 0:T], psA[1][0:1, 0:T]))
            link(dve.memset(pm_row[0:1, 0:1], 0.0))
            dve.tensor_tensor_scan(pm_row[0:1, 1:T + 1], eT1[0:1, 0:T], eT1[0:1, 0:T], 0.0, ALU.max, ALU.max
                                   ).then_inc(s_tab, 1)
            dve.wait_ge(s_tabp, 2)
            link(dve.tensor_copy(pm_col[:, 1:2], psA[1][0:T, 0:1]))
            link(dve.tensor_scalar(eT1[:, r1], eSC[:, 0:EPT], pm_col[:, 1:2], None, ALU.max))
            link(dve.tensor_tensor(eDEG[:, 1:P], edge_no[0:T, :], eT1[:, r1], ALU.subtract))
            link(dve.memset(eDEG[:, 0:1], 1.0))
            link(dve.tensor_scalar(eSLOT[:, :], eCOL[:, :], tile128[0:T, 0:1], None, ALU.add))
            link(dve.scalar_tensor_tensor(eDST[:, 1:P], eD[:, r1], -BIG, eL[:, r1], ALU.add, ALU.mult))
            link(dve.memset(eDST[:, 0:1], 0.0))
            dve.tensor_scalar(eDST[:, :], eDST[:, :], BIG, None, ALU.add).then_inc(s_tab, 1)
            dve.wait_ge(s_tabp, 3)
            link(dve.memset(dstT[:, 79:80].bitcast(I32), int(BIG)))
            link(dve.memset(infoT[:, 79:80, :], 0.0))
            link(dve.tensor_copy(colT[:, :], psA[1][:, 0:T]))
            link(dve.tensor_copy(infoT[:, 0:T, 0], psA[1][:, T:2 * T]))
            link(dve.tensor_copy(infoT[:, 0:T, 1], psA[1][:, 2 * T:3 * T]))
            link(dve.tensor_copy(dstT[:, 0:T], psA[1][:, 3 * T:4 * T]))
            dve.tensor_copy(srcT[:, :], psA[1][:, 4 * T:5 * T]).then_inc(s_scat_in, 1)

            link(dve.tensor_scalar(smat, ones[0:T, 0:NP_], stot, None, ALU.mult))
            link(dve.tensor_copy(iu[:, 0:T], iden[0:T, 0:T]))
            link(dve.tensor_copy(iu[:, T:2 * T], upper[0:T, 0:T]))
            dve.wait_ge(s_nload, 16)
            link(dve.tensor_scalar(nZ, nI[:, :, 0], 0.0, None, ALU.is_equal))
            link(dve.tensor_tensor_scan(nCZ, ones[0:NP_, 0:NF], nZ, 0.0, ALU.mult, ALU.add))
            dve.tensor_copy(small[0:NP_, 5:6], nCZ[:, NF - 1:NF]).then_inc(s_tab, 1)
            dve.wait_ge(s_tabp, 4)
            link(dve.tensor_copy(small[0:NP_, 6:7], psA[1][0:NP_, 0:1]))
            link(dve.tensor_scalar(S1, psA[1][0:NP_, 1:1 + T], 1.0, None, ALU.add))
            link(dve.tensor_tensor(Fj, iota127[0:NP_, 0:T], psA[1][0:NP_, 1 + T:1 + 2 * T], ALU.subtract))
            link(dve.tensor_tensor(nR, nCZ, nZ, ALU.subtract))
            link(dve.tensor_scalar(nR, nR, small[0:NP_, 6:7], None, ALU.add))
            for q in range(NF // 25):
                cq = cube[0:NP_, 0:25 * T].rearrange("p (k t) -> p k t", t=T)
                rq = nR[:, q * 25:(q + 1) * 25].unsqueeze(2).to_broadcast([NP_, 25, T])
                link(dve.tensor_tensor(cq, rq, Fj.unsqueeze(1).to_broadcast([NP_, 25, T]), ALU.is_ge))
                link(dve.tensor_tensor(cq, cq, S1.unsqueeze(1).to_broadcast([NP_, 25, T]), ALU.mult))
                link(dve.tensor_reduce(nSL[:, q * 25:(q + 1) * 25], cq, AX.X, ALU.add))
            link(dve.tensor_tensor(nSL, nSL, nR, ALU.add))
            link(dve.tensor_tensor(nSL, nSL, nZ, ALU.mult))
            link(dve.tensor_tensor(nSL, nSL, nI[:, :, 0], ALU.add))
            dve.tensor_scalar(nDG, nI[:, :, 1], 1.0, None, ALU.max).then_inc(s_tab, 1)
            dve.wait_ge(s_tabp, 5)
            link(dve.tensor_copy(slotT[0:NF, :], psA[1][0:NF, 0:NP_]))
            link(dve.tensor_copy(ndT[0:NF, :, 0], psA[1][0:NF, NP_:2 * NP_]))
            dve.tensor_copy(ndT[0:NF, :, 1], psA[1][0:NF, 2 * NP_:3 * NP_]).then_inc(s_scat_in, 1)
            dve.wait_ge(s_tload, 16)
            link(dve.tensor_copy(tA, tI[:, :, 0]))
            dve.tensor_copy(tB, tI[:, :, 1]).then_inc(s_tab, 1)
            dve.wait_ge(s_tabp, 6)
            link(dve.tensor_copy(permf, psA[1][:, 0:T]))
            link(dve.tensor_copy(degf, psA[1][:, T:2 * T]))
            link(dve.tensor_copy(poutT[:, :], permf))
            link(dve.scalar_tensor_tensor(pinT[:, :], permf, float(N), permf, ALU.is_lt, ALU.mult))
            link(dve.reciprocal(invdeg[:, :], degf))
            for l in range(LAYERS):
                c = C[f"n{l}"]
                link(dve.tensor_scalar(invs[:, l, :], invdeg[:, :], downs[:, c:c + 1],
                                       WUP / (Y_LN if l == 0 else Y_H), ALU.mult, ALU.mult))
            dve.tensor_scalar(small[:, 0:1], ones[:, 0:1], 1.0, None, ALU.mult).then_inc(s_tables, 1)

            s = ph[0]

            def stats0(t):
                i = t.slot(2)
                dve.wait_ge(s.x[i], t.landed(2))
                after(dve, s.rr, (t + -1).n)
                dve.bn_stats(st6[:, :], X[i][:, :]).then_inc(s.r, 1)
                hold(dve, s_const, (s.r, (t + 1).n))
                dve.bn_aggr(mv[:, i, :], st6[:, :]).then_inc(s.dv, 1)
                dve.wait_ge(s.dv, (t + 1).n)
                after(dve, s.sc, (t + -1).n)
                dve.tensor_scalar(ssm[:, i:i + 1], mv[:, i, 1:2], LN_EPS, None, ALU.add).then_inc(s.ss, 1)

            def norm0(t):
                i = t.slot(2)
                dve.wait_ge(s.sc, (t + 1).n)
                after(dve, s.hhi, (t + -1).n)
                after(dve, s.hlo, (t + -1).n)
                dve.tensor_scalar(R[i][:, :], X[i][:, :], mv[:, i, 0:1], scl[:, i:i + 1], ALU.subtract, ALU.mult
                                  ).then_inc(s.rr, 1)
                dve.wait_ge(s.hhi, (t + 1).n)
                dve.wait_ge(s.rr, (t + 1).n)
                dve.scalar_tensor_tensor(HH[i][:, 1, :], R[i][:, :], LN_UP, HH[i][:, 0, :], ALU.mult, ALU.subtract
                                         ).then_inc(s.hlo, 1)

            def turn(t, l):
                s = ph[l]
                i = t.slot(2)
                dve.wait_ge(s.tr, (t + 1).n)
                after(dve, s.sp, (t + -1).n)
                dve.tensor_copy(HT[i][:, :, :, :], psT[i][:, :, :, :]).then_inc(s.ht, 1)

            def ylo(t, l):
                s = ph[l]
                i = t.slot(2)
                dve.wait_ge(s.yhi, (t + 1).n)
                k = Y_LN / (WUP * LN_UP) if l == 0 else Y_H / (WUP * H_UP)
                dve.scalar_tensor_tensor(YB[i][:, D:2 * D], psY[i][:, :], k, YB[i][:, 0:D], ALU.mult, ALU.subtract
                                         ).then_inc(s.ylo, 1)

            def sev(t, l):
                s = ph[l]
                i = t.slot(2)
                dve.wait_ge(s.sp, (t + 1).n)
                if not (isinstance(t.t, int) and t.t < 2):
                    dve.wait_ge(s.s2[i], (t + -2).landed(2))
                c = C[f"s{l}"]
                dve.scalar_tensor_tensor(SB[i][:, :], psS[i][:, :], downs[:, c:c + 1], bias[:, l, :],
                                         ALU.mult, ALU.add).then_inc(s.sev, 1)

            run_tiles(dve, 2, TN, [(2, norm0), (0, lambda t: ylo(t, 0)), (1, lambda t: turn(t, 0)),
                                   (3, stats0), (0, lambda t: sev(t, 0))])

            def carry_lo(t, l):
                s = ph[l]
                i, o = t.slot(2), (t + 1).slot(2)
                if isinstance(t.t, int) and t.t == T - 1:
                    return
                dve.wait_ge(s.chi, (t + 1).n - t.run)
                dve.scalar_tensor_tensor(G[o][0:1, D:2 * D], psA[0 if l == 3 else i][0:1, :], 1.0 / CARRY,
                                         G[o][0:1, 0:D], ALU.mult, ALU.subtract).then_inc(s.clo, 1)

            def combine(t, l):
                s = ph[l]
                i = t.slot(2)
                if l == 2:
                    dve.wait_ge(s_self2[i], Tile(t.U, t.j, t.k).landed(2))
                else:
                    dve.wait_ge(s.x[i], t.landed(2))
                dve.wait_ge(s.agg, (t + 1).n)
                after(dve, s.rr, (t + -1).n)
                dve.scalar_tensor_tensor(R[i][:, :], psA[0 if l == 3 else i][:, :], invs[:, l - 1, bass.ds(t.t, 1)],
                                         Sl[i][:, :], ALU.mult, ALU.add).then_inc(s.r, 1)
                dve.wait_ge(s.r, (t + 1).n)
                dve.scalar_tensor_tensor(junk[:, :], R[i][:, :], 0.0, R[i][:, :], ALU.max, ALU.mult,
                                         accum_out=ss[:, i:i + 1]).then_inc(s.dv2, 1)
                dve.wait_ge(s.dv2, (t + 1).n)
                after(dve, s.sc, (t + -1).n)
                up = 1.0 if l == 3 else H_UP ** -2
                dve.tensor_scalar(ssm[:, i:i + 1], ss[:, i:i + 1], 1e-24, up, ALU.max, ALU.mult).then_inc(s.ss, 1)

            def hlo(t, l):
                s = ph[l]
                i = t.slot(2)
                dve.wait_ge(s.hhi, (t + 1).n)
                dve.scalar_tensor_tensor(HH[i][:, 1, :], RR[i][:, :], scl[:, i:i + 1], HH[i][:, 0, :],
                                         ALU.mult, ALU.subtract).then_inc(s.hlo, 1)

            for l in (1, 2):
                run_tiles(dve, 2, T, [(2, lambda t, l=l: hlo(t, l)), (0, lambda t, l=l: ylo(t, l)),
                                      (1, lambda t, l=l: turn(t, l)), (3, lambda t, l=l: carry_lo(t, l)),
                                      (3, lambda t, l=l: combine(t, l)), (0, lambda t, l=l: sev(t, l))], l - 1)

            s = ph[3]

            def x2(t):
                i, q = t.slot(2), t.slot(6)
                dve.wait_ge(s.sc, (t + 1).n)
                dve.wait_ge(s.rr, (t + 1).n)
                dve.wait_ge(s.xg[i], t.landed(2))
                after(dve, f3.xob, (t + -5).n)
                dve.scalar_tensor_tensor(X2[q], RR[i][:, :], scl[:, i:i + 1], X[i][:, :], ALU.mult, ALU.add
                                         ).then_inc(f3.x2, 1)
                dve.wait_ge(f3.x2, (t + 1).n)
                dve.bn_stats(st6[:, :], X2[q]).then_inc(f3.tiny, 1)
                hold(dve, s_const, (f3.tiny, (t.t) * 4 + 1), (f3.y, (t + -1).n))
                dve.bn_aggr(mv3[:, i, :], st6[:, :]).then_inc(f3.tiny, 1)
                dve.wait_ge(f3.tiny, (t.t) * 4 + 2)
                after(dve, f3.rs, (t + -1).n)
                dve.tensor_scalar(vv[:, i, 0:1], mv3[:, i, 1:2], LN_EPS, None, ALU.add).then_inc(f3.tiny, 1)
                dve.wait_ge(f3.tiny, (t.t) * 4 + 3)
                dve.reciprocal(vv[:, i, 1:2], vv[:, i, 0:1]).then_inc(f3.tiny, 1)
                dve.wait_ge(f3.tiny, (t.t) * 4 + 4)
                dve.tensor_scalar(vv[:, i, 1:2], vv[:, i, 1:2], mv3[:, i, 1:2], LN_EPS, ALU.mult, ALU.add
                                  ).then_inc(f3.v2, 1)

            def yf(t):
                i, q = t.slot(2), t.slot(6)
                dve.wait_ge(f3.rs, (t + 1).n)
                after(dve, f3.z, (t + -5).n)
                dve.tensor_scalar(YF[q], X2[q], mv3[:, i, 0:1], rs[:, i, 0:1], ALU.subtract, ALU.mult
                                  ).then_inc(f3.y, 1)

            def xlo(t):
                i, q = t.slot(2), t.slot(6)
                dve.wait_ge(f3.y, (t + 1).n)
                dve.wait_ge(f3.xhi, (t + 1).n)
                dve.scalar_tensor_tensor(HH[i][:, 1, :], YF[q], r2s[:, i:i + 1], HH[i][:, 0, :],
                                         ALU.mult, ALU.subtract).then_inc(f3.xlo, 1)

            def txc(t):
                i = t.slot(2)
                dve.wait_ge(f3.tx, (t + 1).n)
                after(dve, f3.pre, (t + -1).n)
                dve.tensor_copy(HT[i][:, :, :, :], psX[:, :, :, :]).then_inc(f3.txc, 1)

            def pre(t):
                i = t.slot(2)
                dve.wait_ge(f3.pre, (t + 1).n)
                after(dve, f3.gel, (t + -1).n)
                c = C["w1"]
                dve.scalar_tensor_tensor(PRE[i], psY[i][:, :], downs[:, c:c + 1], b1b[:, :], ALU.mult, ALU.add
                                         ).then_inc(f3.u, 1)

            def gates(t):
                i = t.slot(2)
                base = t.t * 8

                def nxt(ins, k):
                    ins.then_inc(f3.tiny2, 1)
                    hold(dve, s_const, (f3.tiny2, base + k))

                dve.wait_ge(f3.pre, (t + 1).n)
                lg = gv[:, i, 0:8]
                g = wsc[:, i, :]
                after(dve, f3.hs, (t + -1).n)
                nxt(dve.scalar_tensor_tensor(g, psG[:, 0:8], downs[:, CG:CG + 1], bgb[:, :], ALU.mult, ALU.add), 1)
                nxt(dve.scalar_tensor_tensor(g, psG[:, 8:16], downs[:, CG:CG + 1], g, ALU.mult, ALU.add), 2)
                nxt(dve.max(lg, g), 3)
                nxt(dve.max_index(gi[:, i, :], lg, g), 4)
                dve.tensor_scalar(gv[:, i, 8:9], lg[:, 0:1], lg[:, 1:2], None, ALU.subtract).then_inc(f3.lg, 1)
                nxt(dve.tensor_copy(gv[:, i, 10:12], gi[:, i, 0:2]), 5)
                dve.wait_ge(f3.th, (t + 1).n)
                nxt(dve.tensor_scalar(gv[:, i, 12:13], gv[:, i, 9:10], 0.5, 0.5, ALU.mult, ALU.add), 6)
                nxt(dve.tensor_scalar(gv[:, i, 13:14], gv[:, i, 9:10], -0.5, 0.5, ALU.mult, ALU.add), 7)
                nxt(dve.tensor_scalar(lg, iota_row[:, 0:8], gv[:, i, 10:11], gv[:, i, 12:13], ALU.is_equal, ALU.mult), 8)
                dve.tensor_scalar(g, iota_row[:, 0:8], gv[:, i, 11:12], gv[:, i, 13:14], ALU.is_equal, ALU.mult
                                  ).then_inc(f3.w, 1)
                dve.wait_ge(f3.w, (t + 1).n)
                dve.tensor_tensor(g, g, lg, ALU.add).then_inc(f3.z24, 1)
                dve.wait_ge(f3.z24, t.t * 3 + 1)
                dve.tensor_scalar(g, g, ups[:, CB:CB + 1], None, ALU.mult).then_inc(f3.wsp, 1)
                dve.wait_ge(f3.wsp, (t + 1).n)
                after(dve, f3.th2, (t + -1).n)
                dve.tensor_copy(W24[i][:, 0:8], g).then_inc(f3.z24, 1)
                dve.wait_ge(f3.z24, t.t * 3 + 2)
                dve.tensor_copy(W24[i][:, 8:16], W24[i][:, 0:8]).then_inc(f3.z24, 1)
                dve.tensor_tensor(W24[i][:, 16:24], g, W24[i][:, 0:8], ALU.subtract).then_inc(f3.w24, 1)

            def flo(t):
                i = t.slot(2)
                dve.wait_ge(f3.hhi, (t + 1).n)
                dve.tensor_tensor(FH[i][:, 1, :], HS[i], FH[i][:, 0, :], ALU.subtract).then_inc(f3.hlo, 1)

            def thc(t):
                i = t.slot(2)
                dve.wait_ge(f3.th2, (t + 1).n)
                after(dve, f3.cmb, (t + -1).n)
                dve.tensor_copy(WTT[i][:, :], psG16[0:24, 512:640]).then_inc(f3.wtt, 1)
                dve.tensor_copy(FT[i], psH[:, :, :, :]).then_inc(f3.thc, 1)

            def zf(t):
                i, q = t.slot(2), t.slot(6)
                dve.wait_ge(f3.cmb, (t + 1).n)
                after(dve, f3.o1, (t + -1).n)
                dve.scalar_tensor_tensor(Z[i], psS[i][:, :], downs[:, FINAL:FINAL + 1], YF[q], ALU.mult, ALU.add
                                         ).then_inc(f3.z, 1)
                dve.wait_ge(f3.z, (t + 1).n)
                dve.bn_stats(st6b[:, :], Z[i]).then_inc(f3.tiny3, 1)
                hold(dve, s_const, (f3.tiny3, t.t * 2 + 1))
                dve.bn_aggr(zm[:, i, :], st6b[:, :]).then_inc(f3.tiny3, 1)
                dve.wait_ge(f3.tiny3, t.t * 2 + 2)
                after(dve, f3.zr, (t + -1).n)
                dve.tensor_scalar(zv[:, i:i + 1], zm[:, i, 1:2], LN_EPS, None, ALU.add).then_inc(f3.zv, 1)
                after(dve, f3.o, (t + -1).n)
                dve.scalar_tensor_tensor(O1[i], Z[i], zm[:, i, 0:1], ogb[:, :], ALU.subtract, ALU.mult
                                         ).then_inc(f3.o1, 1)
                dve.wait_ge(f3.o1, (t + 1).n)
                dve.wait_ge(f3.zr, (t + 1).n)
                dve.wait_ge(f3.xob, (t + 1).n)
                if not (isinstance(t.t, int) and t.t < 2):
                    dve.wait_ge(f3.out[i], (t + -2).landed(2))
                dve.scalar_tensor_tensor(OUT[i], O1[i], zr[:, i:i + 1], XOB[i], ALU.mult, ALU.add
                                         ).then_inc(f3.o, 1)

            run_tiles(dve, 6, T, [(-1, thc), (2, yf), (1, txc), (0, pre), (0, gates), (2, xlo), (-2, zf),
                                  (4, lambda t: carry_lo(t, 3)), (4, lambda t: combine(t, 3)), (0, flo), (3, x2)])

        @block.tensor
        def _(pe):
            pe.wait_ge(s_const, 1)
            pe.wait_ge(s_bm, 1)
            pe.wait_ge(s_constv, 1)
            for m, name in enumerate(NAMES):
                if name == "w1":
                    pe.wait_ge(s_wload[m % 2], 64 * (m // 2 + 1))
                    for c in range(KC):
                        mm = pe.matmul(psA[1][:, :], bmat[:, c, :], raw[:, m % 2, c, :], start=(c == 0), stop=(c == KC - 1))
                    mm.then_inc(s_ffb, 1)
                    pe.wait_ge(s_b1done, 1)
                    for c in range(KC):
                        mm = pe.matmul(psA[1][:, 0:EX_], bmat[:, c, :], wgr[:, c, :], start=(c == 0), stop=(c == KC - 1))
                    mm.then_inc(s_ffb, 1)
                pe.wait_ge(s_sq, m + 1)
                after(pe, s_cmax, m)
                for c in range(KC):
                    mm = pe.matmul(psA[0][:, :], ones[:, :], sq[:, c, :], start=(c == 0),
                                   stop=(c == KC - 1 and name != "w2"))
                if name == "w2":
                    pe.wait_ge(s_sqb, 1)
                    mm = pe.matmul(psA[0][:, :], ones[0:EX_, :], sqb2[:, :], start=False, stop=True)
                mm.then_inc(s_cn, 1)
            pe.wait_ge(s_sq, 9)
            pe.wait_ge(s_cmax, 8)
            for c in range(KC):
                mm = pe.matmul(psA[0][:, 0:EX_], ones[:, :], sq[:, 0, EX_ * c:EX_ * (c + 1)], start=(c == 0),
                               stop=(c == KC - 1))
            mm.then_inc(s_cn, 1)

            def tp(o, i, rows):
                return pe.transpose(o, i, iden[0:rows, 0:rows])

            pe.wait_ge(s_tab, 1)
            tp(psA[1][0:1, 0:T], pm_col[:, 0:1], T).then_inc(s_tabp, 1)
            pe.wait_ge(s_tab, 2)
            tp(psA[1][0:T, 0:1], pm_row[0:1, 0:T], 1).then_inc(s_tabp, 1)
            pe.wait_ge(s_tab, 3)
            for k, a in enumerate((eCOL, eSLOT, eDEG, eDST, eSRC)):
                mm = tp(psA[1][:, k * T:(k + 1) * T], a, T)
            mm.then_inc(s_tabp, 1)
            pe.wait_ge(s_tab, 4)
            pe.matmul(psA[1][0:NP_, 0:1], upper[0:NP_, 0:NP_], small[0:NP_, 5:6], start=True, stop=True)
            pe.matmul(psA[1][0:NP_, 1:1 + 2 * T], smat, iu, start=True, stop=True).then_inc(s_tabp, 1)
            pe.wait_ge(s_tab, 5)
            for k, a in enumerate((nSL, node_no[:, :], nDG)):
                mm = tp(psA[1][0:NF, k * NP_:(k + 1) * NP_], a, NP_)
            mm.then_inc(s_tabp, 1)
            pe.wait_ge(s_tab, 6)
            tp(psA[1][:, 0:T], tA, T)
            tp(psA[1][:, T:2 * T], tB, T).then_inc(s_tabp, 1)

            pe.wait_ge(s_wlo, 8)
            pe.wait_ge(s_tables, 1)

            def turn(t, l):
                s = ph[l]
                i = t.slot(2)
                pe.wait_ge(s.hhi, (t + 1).n)
                pe.wait_ge(s.hlo, (t + 1).n)
                after(pe, s.ht, (t + -1).n)
                for a in range(2):
                    for c in range(KC):
                        mm = pe.transpose(psT[i][:, a, c, :], HH[i][:, a, c * P:(c + 1) * P], iden16[:, :])
                mm.then_inc(s.tr, 1)

            def neigh(t, l):
                s = ph[l]
                i = t.slot(2)
                pe.wait_ge(s.ht, (t + 1).n)
                after(pe, s.ylo, (t + -1).n)
                products(pe, psY[i][:, :], HT[i], WT[f"n{l}"]).then_inc(s.y, 1)

            def own(t, l):
                s = ph[l]
                i = t.slot(2)
                after(pe, s.sev, (t + -1).n)
                products(pe, psS[i][:, :], HT[i], WT[f"s{l}"]).then_inc(s.sp, 1)

            run_tiles(pe, 2, TN, [(0, lambda t: neigh(t, 0)), (1, lambda t: turn(t, 0)), (0, lambda t: own(t, 0))])

            def aggregate(t, l):
                s = ph[l]
                i = t.slot(2)
                pe.wait_ge(s.g[i], t.landed(2))
                pe.wait_ge(s.smat, (t + 1).n)
                if isinstance(t.t, int) and t.t == 0:
                    pe.wait_ge(s.c0, t.run + 1)
                else:
                    pe.wait_ge(s.clo, t.n - t.run)
                back = 0 if l == 3 else -1
                after(pe, s.r, (t + back).n)
                if l == 3:
                    pass
                acc = psA[0 if l == 3 else i][:, :]
                pe.matmul(acc, Sm[i][:, :], G[i][:, 0:D], start=True, stop=False)
                pe.matmul(acc, Sm[i][:, :], G[i][:, D:2 * D], start=False, stop=True).then_inc(s.agg, 1)

            for l in (1, 2):
                run_tiles(pe, 2, T, [(0, lambda t, l=l: neigh(t, l)), (1, lambda t, l=l: turn(t, l)),
                                     (0, lambda t, l=l: own(t, l)), (3, lambda t, l=l: aggregate(t, l))], l - 1)

            def up(t):
                i = t.slot(2)
                pe.wait_ge(f3.txc, (t + 1).n)
                after(pe, f3.u, (t + -1).n)
                products(pe, psY[i][:, :], HT[i], WT["w1"])
                after(pe, f3.w, t.t)
                for a in range(2):
                    for c in range(KC):
                        mm = pe.matmul(psG[:, 0:16], HT[i][:, a, c, :], wg16[:, c, :], start=(a == 0 and c == 0),
                                       stop=(a == 1 and c == KC - 1))
                mm.then_inc(f3.pre, 1)

            def turn_h(t):
                i = t.slot(2)
                pe.wait_ge(f3.hhi, (t + 1).n)
                pe.wait_ge(f3.hlo, (t + 1).n)
                pe.wait_ge(f3.w24, (t + 1).n)
                after(pe, f3.thc, t.t)
                after(pe, f3.wtt, t.t)
                pe.transpose(psG16[0:24, 512:640], W24[i][:, :], iden16[:, :])
                for a in range(2):
                    for c in range(KC):
                        mm = pe.transpose(psH[:, a, c, :], FH[i][:, a, c * P:(c + 1) * P], iden16[:, :])
                mm.then_inc(f3.th2, 1)

            def turn_x(t):
                i = t.slot(2)
                pe.wait_ge(f3.xhi, (t + 1).n)
                pe.wait_ge(f3.xlo, (t + 1).n)
                after(pe, f3.txc, t.t)
                for a in range(2):
                    for c in range(KC):
                        mm = pe.transpose(psX[:, a, c, :], HH[i][:, a, c * P:(c + 1) * P], iden16[:, :])
                mm.then_inc(f3.tx, 1)

            def down(t):
                i = t.slot(2)
                pe.wait_ge(f3.thc, (t + 1).n)
                pe.wait_ge(f3.wtt, (t + 1).n)
                after(pe, f3.z, (t + -1).n)
                products(pe, psS[i][:, :], FT[i], WT["w2"], stop=False)
                pe.matmul(psS[i][:, :], WTT[i][:, :], b2s[:, :], start=False, stop=True).then_inc(f3.cmb, 1)

            run_tiles(pe, 6, T, [(0, up), (-1, turn_h), (1, turn_x), (-2, down), (4, lambda t: aggregate(t, 3))])


_INS = ['x', 'src', 'dst', 'L0_gnn_W_self', 'L0_gnn_W_neigh', 'L0_gnn_b', 'L0_ffn_Wg', 'L0_ffn_W1', 'L0_ffn_b1',
        'L0_ffn_W2', 'L0_ffn_b2', 'L0_ffn_ln_g', 'L0_ffn_ln_b', 'L0_ffn_out_g', 'L0_ffn_out_b']
_OUTS = [((N, D), 'float32')]


def kernel(**inputs):
    import numpy as _np
    import concourse.bacc as _bacc
    from concourse import mybir as _mybir
    from concourse.bass_utils import run_bass_kernel_spmd as _run

    nc = _bacc.Bacc("TRN2", target_bir_lowering=False, num_devices=1)
    arrays, args = {}, []
    for name in _INS:
        a = _np.ascontiguousarray(inputs[name])
        arrays[f"in_{name}_dram"] = a
        args.append(nc.dram_tensor(f"in_{name}_dram", a.shape, _mybir.dt.from_np(a.dtype), kind="ExternalInput").ap())
    for i, (shape, dtype) in enumerate(_OUTS):
        dt = _mybir.dt.from_np(_np.dtype(dtype))
        args.append(nc.dram_tensor(f"out_{i}_dram", shape, dt, kind="ExternalOutput").ap())
    build(nc, *args)
    r = _run(nc, [arrays], core_ids=[0])
    return r.results[0]["out_0_dram"]
```

```python
from contextlib import ExitStack

import concourse.bass as bass
from concourse import mybir

ALU = mybir.AluOpType
ACT = mybir.ActivationFunctionType
AX = mybir.AxisListType
F32 = mybir.dt.float32
F16 = mybir.dt.float16
I32 = mybir.dt.int32
U32 = mybir.dt.uint32

P = 128
N = 10000
E = 10000
D = 512
KC = D // P
LAYERS = 3
EXPERTS = 8
HIDDEN = 64
EPT = P - 1
T = -(-E // EPT)
TN = -(-N // P)
NLAST = N - (TN - 1) * P
NP_, NF = 80, N // 80
SLOTS = T * P
GRING = 4
BIG = float(1 << 20)
LN_EPS = 1e-5
CARRY = 2.0 ** 14

WUP = 2.0 ** 12
LN_UP = 2.0 ** 10
H_UP = 2.0 ** 14
FF_UP = 2.0 ** 13
Y_LN, Y_H = 2.0 ** 8, 2.0 ** 13
ROOT_D = 22.63


class Tile:

    def __init__(self, U, j, k, run=0):
        self.U, self.j, self.k, self.run = U, j, k, run

    def __add__(self, n):
        return Tile(self.U, self.j, self.k + n, self.run)

    @property
    def t(self):
        return self.j * self.U + self.k

    @property
    def n(self):
        return self.t + self.run * T

    def slot(self, ring):
        return self.k % ring

    def landed(self, ring):
        before = self.run * ((T + ring - 1 - self.k % ring) // ring)
        return 16 * (self.j * (self.U // ring) + self.k // ring + 1 + before)


def run_tiles(eng, U, tiles, stages, run=0):
    offs = [o for o, _ in stages]
    lo = U if min(offs) >= 0 else U * (-(-(2 - min(offs)) // U))
    trips = (tiles - 1 - max(max(offs), 0) - lo) // U

    def step(j, k, first, last):
        for off, f in stages:
            if first is None or 0 <= first + off < tiles:
                f(Tile(U, j, k + off, run))

    for t in range(-max(max(offs), 0), lo):
        step(0, t, t, None)
    with eng.Fori(lo // U, lo // U + trips) as j:
        for k in range(U):
            step(j, k, None, None)
    for t in range(lo + U * trips, tiles - min(min(offs), 0)):
        step(0, t, t, None)


def after(eng, sem, n):
    if not (isinstance(n, int) and n <= 0):
        eng.wait_ge(sem, n)


def hold(eng, done, *waits):
    for _, n in waits:
        if not isinstance(n, int):
            eng.lower_val(n)
    eng.wait_ge(done, 1)
    for sem, n in waits:
        if not (isinstance(n, int) and n <= 0):
            eng.wait_ge(sem, n)


class NaturalSems:

    def __init__(self, sem):
        self.x = [sem(f"p0_x{i}") for i in range(2)]
        self.ys = [sem(f"p0_ys{i}") for i in range(2)]
        self.s2 = [sem(f"p0_s2{i}") for i in range(2)]
        self.r = sem("p0_stats")
        self.dv = sem("p0_mean_var")
        self.ss = sem("p0_var_eps")
        self.sc = sem("p0_rstd")
        self.rr = sem("p0_rows")
        self.hhi = sem("p0_hhi")
        self.hlo = sem("p0_hlo")
        self.tr = sem("p0_turned")
        self.ht = sem("p0_ht")
        self.y = sem("p0_y")
        self.yhi = sem("p0_yhi")
        self.ylo = sem("p0_ylo")
        self.sp = sem("p0_own")
        self.sev = sem("p0_self")


class SlotSems:

    def __init__(self, sem):
        self.g = [sem(f"g{i}") for i in range(GRING)]
        self.x = [sem(f"x{i}") for i in range(2)]
        self.xs = [sem(f"xs{i}") for i in range(2)]
        self.xg = [sem(f"xg{i}") for i in range(2)]
        self.ys = [sem(f"ys{i}") for i in range(2)]
        self.s2 = [sem(f"s2{i}") for i in range(2)]
        self.idx = sem("idx")
        self.idx_in1 = sem("idx_in1")
        self.idx_in3 = sem("idx_in3")
        self.idx_out = sem("idx_out")
        self.smat = sem("smat")
        self.c0 = sem("c0")
        self.chi = sem("chi")
        self.clo = sem("clo")
        self.agg = sem("agg")
        self.r = sem("r")
        self.rr = sem("relu")
        self.dv2 = sem("sumsq")
        self.ss = sem("sumsq_max")
        self.sc = sem("rnorm")
        self.hhi = sem("hhi")
        self.hlo = sem("hlo")
        self.tr = sem("turned")
        self.ht = sem("ht")
        self.y = sem("y")
        self.yhi = sem("yhi")
        self.ylo = sem("ylo")
        self.sp = sem("own")
        self.sev = sem("self")


class FfnSems:

    def __init__(self, sem):
        self.out = [sem(f"f3_out{i}") for i in range(2)]
        self.x2 = sem("f3_x2")
        self.tiny = sem("f3_tiny")
        self.v2 = sem("f3_v2")
        self.idx = sem("f3_idx")
        self.nmr = sem("f3_nmr")
        self.rs = sem("f3_rs")
        self.r2s = sem("f3_r2s")
        self.y = sem("f3_y")
        self.xhi = sem("f3_xhi")
        self.xlo = sem("f3_xlo")
        self.tx = sem("f3_tx")
        self.txc = sem("f3_txc")
        self.pre = sem("f3_pre")
        self.gel = sem("f3_gel")
        self.tiny2 = sem("f3_tiny2")
        self.lg = sem("f3_lg")
        self.th = sem("f3_th")
        self.w = sem("f3_w")
        self.z24 = sem("f3_z24")
        self.w24 = sem("f3_w24")
        self.hs = sem("f3_hs")
        self.hhi = sem("f3_hhi")
        self.hlo = sem("f3_hlo")
        self.th2 = sem("f3_th2")
        self.wtt = sem("f3_wtt")
        self.thc = sem("f3_thc")
        self.cmb = sem("f3_cmb")
        self.z = sem("f3_z")
        self.tiny3 = sem("f3_tiny3")
        self.zv = sem("f3_zv")
        self.zr = sem("f3_zr")
        self.o1 = sem("f3_o1")
        self.xob = sem("f3_xob")
        self.o = sem("f3_o")


def build(nc, x, src, dst, W_self, W_neigh, b, Wg, W1, b1, W2, b2, ln_g, ln_b, out_g, out_b, out):
    with ExitStack() as ctx:
        def sb(name, shape, dt=F32):
            return ctx.enter_context(nc.sbuf_tensor(name, shape, dt))

        def ps(name, shape, dt=F32):
            return ctx.enter_context(nc.psum_tensor(name, shape, dt))

        def sem(name):
            return ctx.enter_context(nc.semaphore(name))

        def dram(name, shape, dt):
            return nc.dram_tensor(name, shape, dt)

        Yd = [dram(f"y_rows{l}", [N, 2 * D], F16) for l in range(LAYERS)]
        Sd0 = dram("self_rows0", [N, D], F32)
        Sd = [None] + [dram(f"self_rows{l}", [SLOTS, D], F32) for l in (1, 2)]
        info = dram("node_info", [N, 2], F32)
        table = dram("slot_table", [SLOTS, 2], F32)

        NAMES = ["n0", "s0", "n1", "s1", "n2", "s2", "w1", "w2"]
        WT = {n: sb(f"w_{n}", [P, 2, KC, D], F16) for n in NAMES}
        wg16 = sb("wg16", [P, KC, 2 * EXPERTS], F16)
        b2s = sb("b2s", [3 * EXPERTS, D], F16)
        raw = sb("raw", [P, 2, KC, D])
        sq = sb("sq", [P, KC, D])
        ups = sb("ups", [P, 16])
        downs = sb("downs", [P, 16])
        nrm = sb("nrm", [P, 16])
        cmax = sb("cmax", [P, 16])
        bias = sb("bias", [P, LAYERS, D])
        b1b = sb("b1b", [P, D])
        ogb = sb("ogb", [P, D])
        obb = sb("obb", [P, D])
        wgr = sb("wgr", [P, KC, EXPERTS])
        wgs = sb("wgs", [P, KC, EXPERTS])
        bgb = sb("bgb", [P, EXPERTS])
        b2r = sb("b2r", [3 * EXPERTS, D])
        b2h = sq[0:3 * EXPERTS, 3, 0:D // 2].bitcast(F16)
        sqb2 = sb("sqb2", [EXPERTS, D])
        rowmask = sb("rowmask", [3 * EXPERTS, 1])
        gcol = sb("gcol", [P, KC])
        bcol = sb("bcol", [P, KC])
        bmat = sb("bmat", [P, KC, P])
        small = sb("small", [P, 16])

        ones = sb("ones", [P, P])
        iden = sb("iden", [P, P])
        iden16 = sb("iden16", [P, P], F16)
        upper = sb("upper", [P, P])
        iota_i = sb("iota_i", [P, 3 * P], I32)
        iota_row = sb("iota_row", [P, P])
        iota127 = sb("iota127", [P, P])
        edge_no = sb("edge_no", [P, EPT])
        node_no_i = sb("node_no_i", [NP_, NF], I32)
        node_no = sb("node_no", [NP_, NF])
        tile128 = sb("tile128", [P, 1])
        rowval = sb("rowval", [P, 1])
        halfpow = sb("halfpow", [P, 2])
        mhalf2 = sb("mhalf2", [P, 2])
        expo = sb("expo", [P, 1], U32)

        colT = sb("colT", [P, T])
        srcT = sb("srcT", [P, T], U32)
        pinT = sb("pinT", [P, T], U32)
        poutT = sb("poutT", [P, T], U32)
        invdeg = sb("invdeg", [P, T])
        invs = sb("invs", [P, LAYERS, T])

        area = sb("area", [P, 12288])

        G = [sb(f"G{i}", [P, 2 * D], F16) for i in range(2)]
        G += [area[:, 22 * D + D * i:23 * D + D * i].bitcast(F16) for i in range(GRING - 2)]
        Sm = [sb(f"Sm{i}", [P, P], F16) for i in range(GRING)]
        Sl = [sb(f"Sl{i}", [P, D]) for i in range(2)]
        X = [sb(f"X{i}", [P, D]) for i in range(2)]
        R = [sb(f"R{i}", [P, D]) for i in range(2)]
        RR = [sb(f"RR{i}", [P, D]) for i in range(2)]
        junk = sb("junk", [P, D])
        HH = [sb(f"HH{i}", [P, 2, D], F16) for i in range(2)]
        HT = [sb(f"HT{i}", [P, 2, KC, P], F16) for i in range(2)]
        YB = [sb(f"YB{i}", [P, 2 * D], F16) for i in range(2)]
        SB = [sb(f"SB{i}", [P, D]) for i in range(2)]
        idx = [[sb(f"idx{a}{i}", [P, 1], U32) for i in range(GRING if a == 0 else 2)] for a in range(3)]
        ss = sb("ss", [P, 2])
        ssm = sb("ssm", [P, 2])
        scl = sb("scl", [P, 2])
        st6 = sb("st6", [P, 6])
        mv = sb("mv", [P, 2, 2])
        gi = sb("gi", [P, 2, 8], U32)
        gv = sb("gv", [P, 2, 40])
        wv = sb("wv", [P, 2, EXPERTS])
        nmr = sb("nmr", [P, 2])
        c2row = sb("c2row", [2, P], F16)
        b1s = sb("b1s", [2, D], F16)
        b1h = sq[0:2, 3, 0:D // 2].bitcast(F16)

        psA = [ps(f"psA{i}", [P, D]) for i in range(2)]
        psT = [ps(f"psT{i}", [P, 2, KC, P], F16) for i in range(2)]
        psY = [ps(f"psY{i}", [P, D]) for i in range(2)]
        psS = [ps(f"psS{i}", [P, D]) for i in range(2)]

        s_const = sem("s_const")
        s_constv = sem("s_constv")
        s_wload = [sem(f"s_wload{i}") for i in range(2)]
        s_sq = sem("s_sq")
        s_sqb = sem("s_sqb")
        s_b1done = sem("s_b1done")
        s_cn = sem("s_cn")
        s_cmax = sem("s_cmax")
        s_nrm = sem("s_nrm")
        s_scale = sem("s_scale")
        s_whi = sem("s_whi")
        s_wlo = sem("s_wlo")
        s_bload = sem("s_bload")
        s_dv = sem("s_dv")
        s_pl = sem("s_pl")
        s_bm = sem("s_bm")
        s_ffb = sem("s_ffb")
        s_wgain = sem("s_wgain")
        s_epad = sem("s_epad")
        s_eload = sem("s_eload")
        s_tab = sem("s_tab")
        s_tabp = sem("s_tabp")
        s_infoz = sem("s_infoz")
        s_sc = [sem(f"s_scat{i}") for i in range(2)]
        s_nload = sem("s_nload")
        s_tload = sem("s_tload")
        s_tinit = sem("s_tinit")
        s_scat_in = sem("s_scat_in")
        s_scat_cp = sem("s_scat_cp")
        s_tables = sem("s_tables")

        def view(at, parts, n, dt=F32):
            v = area[0:parts, at:at + n]
            return v if dt is F32 else v.bitcast(dt)

        eDi, eNi, eSi = (view(P * i, T, EPT, I32) for i in range(3))
        eD, eN, eL, eCS, eEX, eM, eT1 = (view(P * (3 + i), T, P) for i in range(7))
        eCOL, eSLOT, eDEG, eDST, eSRC, eSC = (view(P * (10 + i), T, P) for i in range(6))
        pm_row = view(P * 16, 1, P)
        pm_col = view(P * 17, T, 2)
        dstT = view(P * 18, P, 80, U32)
        infoT = view(P * 19, P, 160).rearrange("p (t two) -> p t two", two=2)
        cpI = [view(P * (21 + i), P, 8, U32) for i in range(2)]
        cpV = [view(P * (21 + i) + 16, P, 16).rearrange("p (t two) -> p t two", two=2) for i in range(2)]
        zero = view(P * 23, NP_, 2 * NF)
        tinit = view(P * 25, T, 2 * P).rearrange("p (k two) -> p k two", two=2)
        stot = view(P * 27, T, 1)
        smat = view(P * 28, T, NP_)
        iu = view(P * 29, T, 2 * T)
        NB = 0
        nI = view(NB, NP_, 2 * NF).rearrange("p (k two) -> p k two", two=2)
        nZ, nCZ, nR, nSL, nDG = (view(NB + P * (2 + i), NP_, NF) for i in range(5))
        Fj = view(NB + P * 7, NP_, T)
        S1 = view(NB + P * 8, NP_, T)
        slotT = view(P * 9, P, 80, U32)
        ndT = view(P * 10, P, 160).rearrange("p (t two) -> p t two", two=2)
        tI = view(P * 12, T, 2 * P).rearrange("p (k two) -> p k two", two=2)
        tA = view(P * 14, T, P)
        tB = view(P * 15, T, P)
        permf = view(P * 16, P, T)
        degf = view(P * 17, P, T)
        cube = raw.rearrange("p a c n -> p (a c n)")

        M_OF = {"n0": (W_neigh, 0), "s0": (W_self, 0), "n1": (W_neigh, 1), "s1": (W_self, 1),
                "n2": (W_neigh, 2), "s2": (W_self, 2)}

        C = {n: i for i, n in enumerate(NAMES)}
        CG, CB = 8, 9
        FINAL = 10
        NPREP = 10

        ctx.enter_context(nc.allow_non_contiguous_dma(reason="the layernorm's gain and bias, as columns"))
        block = ctx.enter_context(nc.Block())
        EX_ = EXPERTS

        p0, ps_ = NaturalSems(sem), SlotSems(sem)
        ph = [p0, ps_, ps_, ps_]
        f3 = FfnSems(sem)

        def ring(at, n):
            return [area[:, at + D * i:at + D * (i + 1)] for i in range(n)]

        X2 = ring(0, 8)
        YF = ring(8 * D, 8)
        GEL = ring(16 * D, 2)
        HS = ring(18 * D, 2)
        Z = ring(20 * D, 2)
        rawf = raw.rearrange("p a c n -> p (a c n)")
        OUT = [rawf[:, D * i:D * (i + 1)] for i in range(2)]
        FH = [rawf[:, D * (2 + i):D * (3 + i)].bitcast(F16).rearrange("p (a n) -> p a n", a=2) for i in range(2)]
        FT = [rawf[:, D * (4 + i):D * (5 + i)].bitcast(F16).rearrange("p (a c n) -> p a c n", a=2, c=KC)
              for i in range(2)]
        W24 = [sb(f"W24_{i}", [P, 3 * EXPERTS], F16) for i in range(2)]
        WTT = [sb(f"WTT{i}", [3 * EXPERTS, P], F16) for i in range(2)]
        wsc = sb("wsc", [P, 2, 8])
        mv3 = sb("mv3", [P, 2, 2])
        vv = sb("vv", [P, 2, 2])
        rs = sb("rs", [P, 2, 2])
        r2s = sb("r2s", [P, 2])
        zv = sb("zv", [P, 2])
        zr = sb("zr", [P, 2])
        zm = sb("zm", [P, 2, 2])
        st6b = sb("st6b", [P, 6])
        psX = psT[0]
        psH = psT[1]
        psG = psA[1]
        psO = psS[0]
        psW = psS[1][:, :].bitcast(F16)

        def products(eng, acc, lhs, w, stop=True):
            n = 0
            for c in range(KC):
                for a, bpart in ((0, 0), (0, 1), (1, 0)):
                    mm = eng.matmul(acc, lhs[:, a, c, :], w[:, bpart, c, :], start=(n == 0),
                                    stop=(stop and n == 3 * KC - 1))
                    n += 1
            return mm

        @block.sync
        def _(sp):
            sp.dma_start(bcol[:, :], ln_b.rearrange("(c p) -> p c", p=P)).then_inc(s_bload, 16)
            sp.dma_start(gcol[:, :], ln_g.rearrange("(c p) -> p c", p=P)).then_inc(s_bload, 16)
            for l in range(LAYERS):
                sp.dma_start(bias[:, l, :], b[l, :].partition_broadcast(P)).then_inc(s_bload, 16)
            sp.dma_start(b1b[:, :], b1.rearrange("e h -> (e h)").partition_broadcast(P)).then_inc(s_bload, 16)
            sp.dma_start(ogb[:, :], out_g.partition_broadcast(P)).then_inc(s_bload, 16)
            sp.dma_start(obb[:, :], out_b.partition_broadcast(P)).then_inc(s_bload, 16)
            sp.dma_start(wgr[:, :, :], Wg.rearrange("(c p) e -> p c e", p=P)).then_inc(s_bload, 16)
            for i in range(3):
                sp.dma_start(b2r[EX_ * i:EX_ * (i + 1), :], b2[:, :]).then_inc(s_bload, 16)
            sp.wait_ge(s_epad, 3)
            full = (E // EPT) * EPT
            for to, frm, count in ((eDi, dst, E), (eSi, src, E), (eNi, dst[1:E], E - 1)):
                sp.dma_start(to[0:T - 1, :], frm[0:full].rearrange("(t k) -> t k", k=EPT)).then_inc(s_eload, 16)
                sp.dma_start(to[T - 1:T, 0:count - full], frm[full:count].rearrange("(a k) -> a k", a=1)
                             ).then_inc(s_eload, 16)
            for m, name in enumerate(NAMES):
                if m >= 2:
                    sp.wait_ge(s_wlo, m - 1)
                    sp.wait_ge(s_whi, m - 1)
                to = raw[:, m % 2, :, :]
                if name == "w1":
                    for c in range(KC):
                        sp.dma_start(to[:, c, :].rearrange("p (e h) -> p e h", e=EX_),
                                     W1[:, c * P:(c + 1) * P, :].rearrange("e p h -> p e h")).then_inc(s_wload[m % 2], 16)
                elif name == "w2":
                    w2f = W2.rearrange("e h d -> (e h) d")
                    for c in range(KC):
                        sp.dma_start(to[:, c, :], w2f[c * P:(c + 1) * P, :]).then_inc(s_wload[m % 2], 16)
                else:
                    w, l = M_OF[name]
                    for c in range(KC):
                        sp.dma_start(to[:, c, :], w[l, c * P:(c + 1) * P, :]).then_inc(s_wload[m % 2], 16)
            sp.wait_ge(s_infoz, 2)
            sp.dma_start(info.rearrange("(p k) two -> p (k two)", p=NP_), zero).then_inc(s_tinit, 16)
            sp.dma_start(table.rearrange("(p k) two -> p k two", p=T), tinit).then_inc(s_tinit, 16)

            s = ph[0]

            def load_x(t):
                after(sp, s.rr, (t + -1).n)
                rows = P if not (isinstance(t.t, int) and t.t == TN - 1) else NLAST
                sp.dma_start(X[t.slot(2)][0:rows, :], x[bass.ds(t.t * P, rows), :]).then_inc(s.x[t.slot(2)], 16)

            def store(t):
                rows = P if not (isinstance(t.t, int) and t.t == TN - 1) else NLAST
                sp.wait_ge(s.yhi, (t + 1).n)
                sp.wait_ge(s.ylo, (t + 1).n)
                sp.dma_start(Yd[0][bass.ds(t.t * P, rows), :], YB[t.slot(2)][0:rows, :]).then_inc(s.ys[t.slot(2)], 16)
                sp.wait_ge(s.sev, (t + 1).n)
                sp.dma_start(Sd0[bass.ds(t.t * P, rows), :], SB[t.slot(2)][0:rows, :]).then_inc(s.s2[t.slot(2)], 16)

            run_tiles(sp, 2, TN, [(4, load_x), (0, store)])
            for l in (1, 2):
                s = ph[l]
                q = ph[l - 1]
                if l == 2:
                    for i in range(2):
                        sp.wait_ge(q.s2[i], 16 * ((T + 1 - i) // 2))

                def load_self(t, s=s, l=l):
                    after(sp, s.r, (t + -1).n)
                    sp.dma_start(Sl[t.slot(2)][:, :], Sd[l - 1][bass.ds(t.t * P, P), :]).then_inc(s.xs[t.slot(2)], 16)

                def store_self(t, s=s, l=l):
                    sp.wait_ge(s.sev, (t + 1).n)
                    sp.dma_start(Sd[l][bass.ds(t.t * P, P), :], SB[t.slot(2)][:, :]).then_inc(s.s2[t.slot(2)], 16)

                if l == 1:
                    run_tiles(sp, 4, T, [(0, store_self)])
                else:
                    run_tiles(sp, 4, T, [(0, store_self), (5, load_self)], 1)
            s = ph[3]
            for i in range(2):
                sp.wait_ge(ph[2].s2[i], 2 * 16 * ((T + 1 - i) // 2))

            def load_self3(t):
                after(sp, s.r, (t + -1).n)
                sp.dma_start(Sl[t.slot(2)][:, :], Sd[2][bass.ds(t.t * P, P), :]).then_inc(s.xs[t.slot(2)], 16)

            run_tiles(sp, 8, T, [(6, load_self3)], 2)

        @block.gpsimd
        def _(pool):
            node_limit = pool.alloc_register("node_limit")
            slot_limit = pool.alloc_register("slot_limit")
            pool.reg_mov(node_limit, N - 1)
            pool.reg_mov(slot_limit, SLOTS - 1)
            n = [0]

            def link(ins):
                n[0] += 1
                ins.then_inc(s_pl, 1)
                pool.wait_ge(s_pl, n[0])

            pool.memset(ones[:, :], 1.0).then_inc(s_const, 1)
            link(pool.memset(iden[:, :], 0.0))
            link(pool.affine_select(out=iden[:, :], in_=iden[:, :], compare_op=ALU.not_equal, fill=1.0, base=0,
                                    pattern=[[-1, P]], channel_multiplier=1))
            link(pool.memset(upper[:, :], 1.0))
            link(pool.affine_select(out=upper[:, :], in_=upper[:, :], compare_op=ALU.is_gt, fill=0.0, base=0,
                                    pattern=[[1, P]], channel_multiplier=-1))
            link(pool.iota(iota_i[:, 0:P], [[1, P]], base=0, channel_multiplier=0))
            link(pool.iota(iota_i[:, P:2 * P], [[EPT, P]], base=0, channel_multiplier=0))
            link(pool.iota(iota_i[:, 2 * P:2 * P + EPT], [[1, EPT]], base=1, channel_multiplier=EPT))
            link(pool.iota(iota_i[:, 3 * P - 1:3 * P], [[1, 1]], base=0, channel_multiplier=P))
            link(pool.iota(node_no_i[:, :], [[1, NF]], base=0, channel_multiplier=NF))
            link(pool.memset(rowval[:, :], 1.0))
            link(pool.memset(rowval[0:1, :], CARRY))
            link(pool.memset(halfpow[:, 0:1], 0.5))
            link(pool.memset(halfpow[:, 1:2], -0.5))
            link(pool.memset(mhalf2[:, :], -0.5))
            link(pool.memset(rowmask[:, :], 1.0))
            pool.memset(rowmask[0:1, :], 1.0).then_inc(s_const, 1)
            for m in range(NPREP - 1):
                pool.wait_ge(s_cmax, m + 1)
                pool.tensor_tensor(nrm[:, m:m + 1], cmax[:, m:m + 1], halfpow[:, 0:1], ALU.pow).then_inc(s_nrm, 1)

            def scatter_pass(index, value, to, limit, rows, base):
                def one(g, i, landed, copied):
                    if landed is not None:
                        pool.wait_ge(s_sc[i], landed)
                    pool.tensor_copy(cpI[i][0:rows, :], index[0:rows, bass.ds(g * 8, 8)]).then_inc(s_scat_cp, 1)
                    pool.tensor_copy(cpV[i][0:rows, :, :], value[0:rows, bass.ds(g * 8, 8), :]).then_inc(s_scat_cp, 1)
                    hold(pool, s_const, (s_scat_cp, copied))
                    for k in range(8):
                        pool.indirect_dma_start(
                            to[:, :], bass.IndirectOffsetOnAxis(ap=cpI[i][0:rows, k:k + 1], axis=0),
                            cpV[i][0:rows, k, :], None, bounds_check=limit, oob_is_err=False).then_inc(s_sc[i], 16)

                one(0, 0, None if base == 0 else base * 5 * 128, base * 20 + 2)
                one(1, 1, None if base == 0 else base * 5 * 128, base * 20 + 4)
                with pool.Fori(1, 5) as j:
                    one(j * 2, 0, base * 5 * 128 + j * 128, base * 20 + j * 4 + 2)
                    one(j * 2 + 1, 1, base * 5 * 128 + j * 128, base * 20 + j * 4 + 4)

            pool.wait_ge(s_tinit, 32)
            pool.wait_ge(s_scat_in, 1)
            scatter_pass(dstT, infoT, info, node_limit, P, 0)
            for i in range(2):
                pool.wait_ge(s_sc[i], 640)
            pool.dma_start(nI, info.rearrange("(p k) two -> p k two", p=NP_)).then_inc(s_nload, 16)
            pool.wait_ge(s_scat_in, 2)
            scatter_pass(slotT, ndT, table, slot_limit, NF, 1)
            for i in range(2):
                pool.wait_ge(s_sc[i], 1280)
            pool.dma_start(tI, table.rearrange("(p k) two -> p k two", p=T)).then_inc(s_tload, 16)

            s = ph[0]

            def dev0(t):
                pool.wait_ge(s.ss, (t + 1).n)
                after(pool, s.rr, (t + -1).n)
                pool.tensor_tensor(scl[:, t.slot(2):t.slot(2) + 1], ssm[:, t.slot(2):t.slot(2) + 1],
                                   halfpow[:, 1:2], ALU.pow).then_inc(s.sc, 1)

            run_tiles(pool, 2, TN, [(3, dev0)])
            pool.wait_ge(s_tables, 1)

            for l in (1, 2, 3):
                s = ph[l]
                U = 4
                last = ph[l - 1]
                tiles = TN if l == 1 else T
                for i in range(2):
                    pool.wait_ge(last.ys[i], (2 if l == 3 else 1) * 16 * ((tiles + 1 - i) // 2))
                    if l == 1:
                        pool.wait_ge(last.s2[i], 16 * ((tiles + 1 - i) // 2))

                def gather(t, s=s, l=l):
                    i = t.slot(GRING)
                    after(pool, s.agg, (t + (1 - GRING)).n)
                    pool.tensor_copy(idx[0][i][:, :], srcT[:, bass.ds(t.t, 1)]).then_inc(s.idx, 1)
                    hold(pool, s_const, (s.idx, (t + 1).n))
                    pool.indirect_dma_start(G[i][:, :], None, Yd[l - 1][:, :],
                                            bass.IndirectOffsetOnAxis(ap=idx[0][i][:, 0:1], axis=0),
                                            bounds_check=node_limit, oob_is_err=False).then_inc(s.g[i], 16)

                def by_node(t, s=s, l=l):
                    i = t.slot(2)
                    own = Tile(t.U, t.j, t.k)
                    if l == 1:
                        after(pool, s.r, (t + -1).n)
                    else:
                        after(pool, f3.x2, (own + -1).n)
                    done = s.idx_in1 if l == 1 else s.idx_in3
                    pool.tensor_copy(idx[1][i][:, :], pinT[:, bass.ds(t.t, 1)]).then_inc(done, 1)
                    to, frm = (Sl[i], Sd0) if l == 1 else (X[i], x)
                    hold(pool, s_const, (done, (own + 1).n))
                    pool.indirect_dma_start(to[:, :], None, frm[:, :],
                                            bass.IndirectOffsetOnAxis(ap=idx[1][i][:, 0:1], axis=0),
                                            bounds_check=node_limit, oob_is_err=False
                                            ).then_inc((s.x if l == 1 else s.xg)[i], 16)

                def norm(t, s=s, l=l):
                    i = t.slot(2)
                    pool.wait_ge(s.ss, (t + 1).n)
                    if l < 3:
                        after(pool, s.hlo, (t + -1).n)
                    else:
                        after(pool, f3.x2, (Tile(t.U, t.j, t.k) + -1).n)
                    pool.tensor_tensor(scl[:, i:i + 1], ssm[:, i:i + 1], halfpow[:, 1:2], ALU.pow).then_inc(s.sc, 1)

                def put_y(t, s=s, l=l):
                    i = t.slot(2)
                    if not (isinstance(t.t, int) and t.t < 2):
                        pool.wait_ge(s.ys[i], (t + -2).landed(2))
                    pool.tensor_copy(idx[2][i][:, :], poutT[:, bass.ds(t.t, 1)]).then_inc(s.idx_out, 1)
                    hold(pool, s_const, (s.idx_out, (t + 1).n), (s.yhi, (t + 1).n), (s.ylo, (t + 1).n))
                    pool.indirect_dma_start(Yd[l][:, :], bass.IndirectOffsetOnAxis(ap=idx[2][i][:, 0:1], axis=0),
                                            YB[i][:, :], None, bounds_check=node_limit, oob_is_err=False
                                            ).then_inc(s.ys[i], 16)

                if l < 3:
                    st = [(6, gather), (0, put_y), (3, norm)]
                    if l == 1:
                        st.append((5, by_node))
                    run_tiles(pool, U, T, st, l - 1)
            s = ph[3]

            def own(t):
                return Tile(t.U, t.j, t.k)

            def rs_of(t):
                t = own(t)
                i = t.slot(2)
                pool.wait_ge(f3.v2, (t + 1).n)
                after(pool, f3.y, (t + -1).n)
                after(pool, f3.r2s, (t + -1).n)
                pool.tensor_tensor(rs[:, i, :], vv[:, i, :], mhalf2[:, :], ALU.pow).then_inc(f3.rs, 1)

            def xob(t):
                t = own(t)
                pool.wait_ge(f3.y, (t + 1).n)
                pool.tensor_tensor(X2[t.slot(8)], X2[t.slot(8)], obb[:, :], ALU.add).then_inc(f3.xob, 1)

            def hs_of(t):
                t = own(t)
                pool.wait_ge(f3.gel, (t + 1).n)
                pool.wait_ge(f3.w, (t + 1).n)
                after(pool, f3.hlo, (t + -1).n)
                i = t.slot(2)
                pool.tensor_tensor(HS[i].rearrange("p (e h) -> p e h", e=EX_),
                                   GEL[i].rearrange("p (e h) -> p e h", e=EX_),
                                   wv[:, i, :].unsqueeze(2).to_broadcast([P, EX_, HIDDEN]), ALU.mult
                                   ).then_inc(f3.hs, 1)

            def zr_of(t):
                t = own(t)
                i = t.slot(2)
                pool.wait_ge(f3.zv, (t + 1).n)
                after(pool, f3.o, (t + -1).n)
                pool.tensor_tensor(zr[:, i:i + 1], zv[:, i:i + 1], halfpow[:, 1:2], ALU.pow).then_inc(f3.zr, 1)

            def put_out(t):
                t = own(t)
                i = t.slot(2)
                if not (isinstance(t.t, int) and t.t < 2):
                    pool.wait_ge(f3.out[i], (t + -2).landed(2))
                pool.tensor_copy(idx[2][i][:, :], poutT[:, bass.ds(t.t, 1)]).then_inc(f3.idx, 1)
                hold(pool, s_const, (f3.idx, (t + 1).n), (f3.o, (t + 1).n))
                pool.indirect_dma_start(out[:, :], bass.IndirectOffsetOnAxis(ap=idx[2][i][:, 0:1], axis=0),
                                        OUT[i], None, bounds_check=node_limit, oob_is_err=False
                                        ).then_inc(f3.out[i], 16)

            run_tiles(pool, 8, T, [(7, gather), (5, by_node), (1, xob), (3, rs_of), (-1, hs_of), (-5, put_out),
                                   (4, norm), (-4, zr_of)], 2)
            for i in range(2):
                pool.wait_ge(f3.out[i], 16 * ((T + 1 - i) // 2))

        @block.scalar
        def _(act):
            act.wait_ge(s_bload, 0 + 16 * 12)
            for m, name in enumerate(NAMES):
                act.wait_ge(s_wload[m % 2], 64 * (m // 2 + 1))
                if name == "w1":
                    act.wait_ge(s_wgain, 1)
                after(act, s_cn, m)
                act.activation(sq[:, :, :], raw[:, m % 2, :, :], ACT.Square).then_inc(s_sq, 1)
                if name == "w2":
                    act.activation(sqb2[:, :], b2r[0:EX_, :], ACT.Square).then_inc(s_sqb, 1)
                act.wait_ge(s_scale, m + 1)
                act.activation(WT[name][:, 0, :, :], raw[:, m % 2, :, :], ACT.Copy, scale=ups[:, m:m + 1]
                               ).then_inc(s_whi, 1)
            act.wait_ge(s_wgain, 2)
            act.wait_ge(s_cn, 8)
            act.activation(sq[:, 0, 0:KC * EX_].rearrange("p (c e) -> p c e", c=KC), wgs[:, :, :], ACT.Square
                           ).then_inc(s_sq, 1)

            s = ph[0]

            def hi0(t):
                i = t.slot(2)
                act.wait_ge(s.rr, (t + 1).n)
                after(act, s.tr, (t + -1).n)
                act.activation(HH[i][:, 0, :], R[i][:, :], ACT.Copy, scale=LN_UP).then_inc(s.hhi, 1)

            def yhi(t, l):
                i = t.slot(2)
                s = ph[l]
                act.wait_ge(s.y, (t + 1).n)
                if not (isinstance(t.t, int) and t.t < 2):
                    act.wait_ge(s.ys[i], (t + -2).landed(2))
                k = Y_LN / (WUP * LN_UP) if l == 0 else Y_H / (WUP * H_UP)
                act.activation(YB[i][:, 0:D], psY[i][:, :], ACT.Copy, scale=k).then_inc(s.yhi, 1)

            run_tiles(act, 2, TN, [(2, hi0), (0, lambda t: yhi(t, 0))])

            def carry_hi(t, l):
                s = ph[l]
                i, nxt = t.slot(2), t + 1
                if isinstance(t.t, int) and t.t == T - 1:
                    return
                act.wait_ge(s.agg, (t + 1).n)
                o = nxt.slot(GRING)
                act.wait_ge(s.g[o], nxt.landed(GRING))
                act.activation(G[o][0:1, 0:D], psA[0 if l == 3 else i][0:1, :], ACT.Copy, scale=1.0 / CARRY
                               ).then_inc(s.chi, 1)

            def relu(t, l):
                s = ph[l]
                i = t.slot(2)
                act.wait_ge(s.r, (t + 1).n)
                if l < 3:
                    after(act, s.hlo, (t + -1).n)
                else:
                    after(act, f3.x2, (Tile(t.U, t.j, t.k) + -1).n)
                act.activation(RR[i][:, :], R[i][:, :], ACT.Relu).then_inc(s.rr, 1)

            def hhi(t, l):
                s = ph[l]
                i = t.slot(2)
                act.wait_ge(s.sc, (t + 1).n)
                act.wait_ge(s.rr, (t + 1).n)
                after(act, s.tr, (t + -1).n)
                act.activation(HH[i][:, 0, :], RR[i][:, :], ACT.Copy, scale=scl[:, i:i + 1]).then_inc(s.hhi, 1)

            def first_carry(l):
                act.wait_ge(ph[l].g[0], Tile(GRING, 0, 0, l - 1).landed(GRING))
                act.activation(G[0][0:1, :], G[0][0:1, :], ACT.Copy, scale=0.0).then_inc(ph[l].c0, 1)

            for l in (1, 2):
                first_carry(l)
                run_tiles(act, 4, T, [(2, lambda t, l=l: hhi(t, l)), (0, lambda t, l=l: yhi(t, l)),
                                      (3, lambda t, l=l: carry_hi(t, l)), (3, lambda t, l=l: relu(t, l))], l - 1)
            first_carry(3)

            def own(t):
                return Tile(t.U, t.j, t.k)

            def yf(t):
                t = own(t)
                i, q = t.slot(2), t.slot(8)
                act.wait_ge(f3.r2s, (t + 1).n)
                after(act, f3.z, (t + -7).n)
                act.activation(YF[q], X2[q], ACT.Identity, bias=nmr[:, i:i + 1], scale=rs[:, i, 0:1]).then_inc(f3.y, 1)

            def xhi(t):
                t = own(t)
                i = t.slot(2)
                act.wait_ge(f3.y, (t + 1).n)
                after(act, f3.tx, (t + -1).n)
                act.activation(HH[i][:, 0, :], YF[t.slot(8)], ACT.Copy, scale=r2s[:, i:i + 1]).then_inc(f3.xhi, 1)

            def txc(t):
                t = own(t)
                i = t.slot(2)
                act.wait_ge(f3.tx, (t + 1).n)
                after(act, f3.pre, (t + -1).n)
                act.activation(HT[i][:, :, :, :], psX[:, :, :, :], ACT.Copy).then_inc(f3.txc, 1)

            def gelu(t):
                t = own(t)
                i = t.slot(2)
                act.wait_ge(f3.pre, (t + 1).n)
                after(act, f3.hs, (t + -1).n)
                c = C["w1"]
                act.activation(GEL[i], psY[i][:, :], ACT.Gelu_apprx_tanh, scale=downs[:, c:c + 1]).then_inc(f3.gel, 1)

            def gate(t):
                t = own(t)
                i = t.slot(2)
                act.wait_ge(f3.lg, (t + 1).n)
                after(act, f3.w, (t + -1).n)
                act.activation(gv[:, i, 9:10], gv[:, i, 8:9], ACT.Tanh, scale=0.5).then_inc(f3.th, 1)

            def fhi(t):
                t = own(t)
                i = t.slot(2)
                act.wait_ge(f3.hs, (t + 1).n)
                after(act, f3.th2, (t + -1).n)
                act.activation(FH[i][:, 0, :], HS[i], ACT.Copy, scale=ups[:, CB:CB + 1]).then_inc(f3.hhi, 1)

            def thc(t):
                t = own(t)
                i = t.slot(2)
                act.wait_ge(f3.th2, (t + 1).n)
                after(act, f3.cmb, (t + -1).n)
                act.activation(WTT[i][:, :], psW[0:24, 0:P], ACT.Copy).then_inc(f3.wtt, 1)
                act.activation(FT[i], psH[:, :, :, :], ACT.Copy).then_inc(f3.thc, 1)

            run_tiles(act, 8, T, [(0, txc), (4, lambda t: carry_hi(t, 3)), (-1, gelu), (-1, gate),
                                  (4, lambda t: relu(t, 3)), (-2, fhi), (2, yf), (2, xhi), (-3, thc)], 2)

        @block.vector
        def _(dve):
            n = [0]

            def link(ins):
                n[0] += 1
                ins.then_inc(s_dv, 1)
                dve.wait_ge(s_dv, n[0])

            dve.memset(eDi, -1).then_inc(s_epad, 1)
            dve.memset(eNi, -1).then_inc(s_epad, 1)
            dve.memset(eSi, 0).then_inc(s_epad, 1)
            dve.memset(zero, 0.0).then_inc(s_infoz, 1)
            link(dve.memset(tinit[:, :, 0:1], BIG))
            dve.memset(tinit[:, :, 1:2], 1.0).then_inc(s_infoz, 1)
            dve.wait_ge(s_const, 2)
            link(dve.tensor_copy(iden16[:, :], iden[:, :]))
            link(dve.tensor_copy(iota_row[:, :], iota_i[:, 0:P]))
            link(dve.tensor_copy(iota127[:, :], iota_i[:, P:2 * P]))
            link(dve.tensor_copy(edge_no[:, :], iota_i[:, 2 * P:2 * P + EPT]))
            link(dve.tensor_copy(tile128[:, :], iota_i[:, 3 * P - 1:3 * P]))
            link(dve.tensor_copy(node_no[:, :], node_no_i[:, :]))
            link(dve.tensor_reduce(small[0:24, 0:1], iden[0:24, 8:16], AX.X, ALU.add))
            dve.tensor_scalar(rowmask[:, :], small[0:24, 0:1], -1.0, 1.0, ALU.mult, ALU.add).then_inc(s_constv, 1)

            def scales(c, k):
                dve.wait_ge(s_nrm, k)
                if c == C["w1"]:
                    link(dve.tensor_reduce(small[:, 2:3], b1b[:, :], AX.X, ALU.max, apply_absolute_value=True))
                    link(dve.tensor_scalar(nrm[:, c:c + 1], small[:, 2:3], 1.0 / 32, nrm[:, c:c + 1], ALU.mult, ALU.max))
                bits = nrm[:, c:c + 1].bitcast(U32)
                link(dve.tensor_scalar(expo[:, :], bits, 0x7F800000, None, ALU.bitwise_and))
                link(dve.tensor_scalar(downs[:, c:c + 1], expo[:, :].bitcast(F32), 0.5 / WUP, None, ALU.mult))
                link(dve.tensor_scalar(ups[:, c:c + 1].bitcast(U32), expo[:, :], 0x7F800000, None, ALU.bitwise_xor))
                return dve.tensor_scalar(ups[:, c:c + 1], ups[:, c:c + 1], WUP, None, ALU.mult)

            dve.wait_ge(s_bload, 16 * 12)
            for c in range(KC):
                link(dve.tensor_scalar(bmat[:, c, :], ones[:, :], bcol[:, c:c + 1], None, ALU.mult))
            dve.tensor_scalar(small[:, 0:1], ones[:, 0:1], 1.0, None, ALU.mult).then_inc(s_bm, 1)
            for m, name in enumerate(NAMES):
                w = raw[:, m % 2, :, :]
                dve.wait_ge(s_wload[m % 2], 64 * (m // 2 + 1))
                if name == "w1":
                    dve.wait_ge(s_ffb, 1)
                    dve.tensor_tensor(b1b[:, :], psA[1][:, :], b1b[:, :], ALU.add).then_inc(s_b1done, 1)
                    dve.wait_ge(s_b1done, 1)
                    dve.wait_ge(s_ffb, 2)
                    link(dve.tensor_copy(bgb[:, :], psA[1][:, 0:EX_]))
                    for c in range(KC):
                        link(dve.tensor_scalar(w[:, c, :], w[:, c, :], gcol[:, c:c + 1], None, ALU.mult))
                    dve.tensor_scalar(small[:, 0:1], ones[:, 0:1], 1.0, None, ALU.mult).then_inc(s_wgain, 1)
                    for c in range(KC):
                        link(dve.tensor_scalar(wgs[:, c, :], wgr[:, c, :], gcol[:, c:c + 1], None, ALU.mult))
                    dve.tensor_scalar(small[:, 0:1], ones[:, 0:1], 1.0, None, ALU.mult).then_inc(s_wgain, 1)
                dve.wait_ge(s_cn, m + 1)
                link(dve.tensor_reduce(cmax[:, m:m + 1], psA[0][:, :], AX.X, ALU.max))
                dve.tensor_scalar(cmax[:, m:m + 1], cmax[:, m:m + 1], 1e-30, None, ALU.max).then_inc(s_cmax, 1)
                scales(m, m + 1).then_inc(s_scale, 1)
                dve.wait_ge(s_scale, m + 1)
                dve.wait_ge(s_whi, m + 1)
                dve.scalar_tensor_tensor(WT[name][:, 1, :, :].rearrange("p c n -> p (c n)"),
                                         w.rearrange("p c n -> p (c n)"), ups[:, m:m + 1],
                                         WT[name][:, 0, :, :].rearrange("p c n -> p (c n)"),
                                         ALU.mult, ALU.subtract).then_inc(s_wlo, 1)
            dve.wait_ge(s_cn, 9)
            link(dve.tensor_reduce(cmax[:, CG:CG + 1], psA[0][:, 0:EX_], AX.X, ALU.max))
            dve.tensor_scalar(cmax[:, CG:CG + 1], cmax[:, CG:CG + 1], 1e-30, None, ALU.max).then_inc(s_cmax, 1)
            link(scales(CG, 9))
            link(dve.tensor_scalar(wg16[:, :, 0:EX_], wgs[:, :, :], ups[:, CG:CG + 1], None, ALU.mult))
            link(dve.scalar_tensor_tensor(wg16[:, :, EX_:2 * EX_], wgs[:, :, :], ups[:, CG:CG + 1],
                                          wg16[:, :, 0:EX_], ALU.mult, ALU.subtract))
            c1 = C["w1"]
            link(dve.tensor_scalar(small[:, 3:4], nrm[:, c1:c1 + 1], ROOT_D, small[:, 2:3], ALU.mult, ALU.add))
            link(dve.tensor_scalar(small[:, 3:4], small[:, 3:4], 1.0, None, ALU.max))
            link(dve.tensor_scalar(expo[:, :], small[:, 3:4].bitcast(U32), 0x7F800000, None, ALU.bitwise_and))
            link(dve.tensor_scalar(downs[:, CB:CB + 1], expo[:, :].bitcast(F32), 0.5 / FF_UP, None, ALU.mult))
            link(dve.tensor_scalar(ups[:, CB:CB + 1].bitcast(U32), expo[:, :], 0x7F800000, None, ALU.bitwise_xor))
            link(dve.tensor_scalar(ups[:, CB:CB + 1], ups[:, CB:CB + 1], FF_UP, None, ALU.mult))
            link(dve.memset(c2row[:, :], CARRY))
            link(dve.tensor_scalar(sq[0:2, 0, :], b1b[0:2, :], ups[0:2, c1:c1 + 1], LN_UP / CARRY, ALU.mult, ALU.mult))
            link(dve.tensor_copy(b1h, sq[0:2, 0, :]))
            link(dve.tensor_tensor(sq[0:2, 1, :], sq[0:2, 0, :], b1h, ALU.subtract))
            link(dve.tensor_scalar(sq[0:2, 2, :], b1h, iden[0:2, 0:1], None, ALU.mult))
            link(dve.scalar_tensor_tensor(b1s[:, :], sq[0:2, 1, :], iden[0:2, 1:2], sq[0:2, 2, :], ALU.mult, ALU.add))
            c2 = C["w2"]
            link(dve.tensor_scalar(downs[:, FINAL:FINAL + 1], downs[:, CB:CB + 1], downs[:, c2:c2 + 1], None, ALU.mult))
            link(dve.tensor_scalar(ups[:, CB:CB + 1], ups[:, CB:CB + 1], 0.5, None, ALU.mult))
            for c in (CG, c1, C["s0"]):
                link(dve.tensor_scalar(downs[:, c:c + 1], downs[:, c:c + 1], 1.0 / LN_UP, None, ALU.mult))
            for name in ("s1", "s2"):
                c = C[name]
                link(dve.tensor_scalar(downs[:, c:c + 1], downs[:, c:c + 1], 1.0 / H_UP, None, ALU.mult))
            link(dve.tensor_scalar(b2h, b2r[:, :], ups[0:24, c2:c2 + 1], None, ALU.mult))
            lo24 = sq[0:24, 1, :]
            hi24 = sq[0:24, 2, :]
            link(dve.scalar_tensor_tensor(lo24, b2r[:, :], ups[0:24, c2:c2 + 1], b2h, ALU.mult, ALU.subtract))
            link(dve.tensor_scalar(hi24, b2h, rowmask[:, 0:1], None, ALU.mult))
            link(dve.tensor_scalar(small[0:24, 4:5], rowmask[:, 0:1], -1.0, 1.0, ALU.mult, ALU.add))
            link(dve.scalar_tensor_tensor(b2s[:, :], lo24, small[0:24, 4:5], hi24, ALU.mult, ALU.add))

            dve.wait_ge(s_eload, 96)
            r1 = slice(0, EPT)
            link(dve.tensor_copy(eD[:, r1], eDi))
            link(dve.tensor_copy(eN[:, r1], eNi))
            link(dve.tensor_copy(eSRC[:, 1:P], eSi))
            link(dve.memset(eSRC[:, 0:1], 0.0))
            link(dve.tensor_tensor(eL[:, r1], eD[:, r1], eN[:, r1], ALU.not_equal))
            link(dve.tensor_tensor_scan(eCS[:, r1], ones[0:T, r1], eL[:, r1], 0.0, ALU.mult, ALU.add))
            link(dve.tensor_copy(stot, eCS[:, EPT - 1:EPT]))
            link(dve.tensor_tensor(eEX[:, r1], eCS[:, r1], eL[:, r1], ALU.subtract))
            link(dve.tensor_scalar(eT1[:, r1], eEX[:, r1], stot, None, ALU.is_lt))
            link(dve.scalar_tensor_tensor(eCOL[:, 1:P], eEX[:, r1], 1.0, eT1[:, r1], ALU.add, ALU.mult))
            link(dve.tensor_copy(eCOL[:, 0:1], eCOL[:, 1:2]))
            link(dve.tensor_tensor(eM[:, r1], eL[:, r1], edge_no[0:T, :], ALU.mult))
            link(dve.memset(eSC[:, 0:1], 0.0))
            link(dve.tensor_tensor_scan(eSC[:, 1:P], eM[:, r1], eM[:, r1], 0.0, ALU.max, ALU.max))
            dve.tensor_copy(pm_col[:, 0:1], eSC[:, P - 1:P]).then_inc(s_tab, 1)
            dve.wait_ge(s_tabp, 1)
            link(dve.tensor_copy(eT1[0:1, 0:T], psA[1][0:1, 0:T]))
            link(dve.memset(pm_row[0:1, 0:1], 0.0))
            dve.tensor_tensor_scan(pm_row[0:1, 1:T + 1], eT1[0:1, 0:T], eT1[0:1, 0:T], 0.0, ALU.max, ALU.max
                                   ).then_inc(s_tab, 1)
            dve.wait_ge(s_tabp, 2)
            link(dve.tensor_copy(pm_col[:, 1:2], psA[1][0:T, 0:1]))
            link(dve.tensor_scalar(eT1[:, r1], eSC[:, 0:EPT], pm_col[:, 1:2], None, ALU.max))
            link(dve.tensor_tensor(eDEG[:, 1:P], edge_no[0:T, :], eT1[:, r1], ALU.subtract))
            link(dve.memset(eDEG[:, 0:1], 1.0))
            link(dve.tensor_scalar(eSLOT[:, :], eCOL[:, :], tile128[0:T, 0:1], None, ALU.add))
            link(dve.scalar_tensor_tensor(eDST[:, 1:P], eD[:, r1], -BIG, eL[:, r1], ALU.add, ALU.mult))
            link(dve.memset(eDST[:, 0:1], 0.0))
            dve.tensor_scalar(eDST[:, :], eDST[:, :], BIG, None, ALU.add).then_inc(s_tab, 1)
            dve.wait_ge(s_tabp, 3)
            link(dve.memset(dstT[:, 79:80].bitcast(I32), int(BIG)))
            link(dve.memset(infoT[:, 79:80, :], 0.0))
            link(dve.tensor_copy(colT[:, :], psA[1][:, 0:T]))
            link(dve.tensor_copy(infoT[:, 0:T, 0], psA[1][:, T:2 * T]))
            link(dve.tensor_copy(infoT[:, 0:T, 1], psA[1][:, 2 * T:3 * T]))
            link(dve.tensor_copy(dstT[:, 0:T], psA[1][:, 3 * T:4 * T]))
            dve.tensor_copy(srcT[:, :], psA[1][:, 4 * T:5 * T]).then_inc(s_scat_in, 1)

            link(dve.tensor_scalar(smat, ones[0:T, 0:NP_], stot, None, ALU.mult))
            link(dve.tensor_copy(iu[:, 0:T], iden[0:T, 0:T]))
            link(dve.tensor_copy(iu[:, T:2 * T], upper[0:T, 0:T]))
            dve.wait_ge(s_nload, 16)
            link(dve.tensor_scalar(nZ, nI[:, :, 0], 0.0, None, ALU.is_equal))
            link(dve.tensor_tensor_scan(nCZ, ones[0:NP_, 0:NF], nZ, 0.0, ALU.mult, ALU.add))
            dve.tensor_copy(small[0:NP_, 5:6], nCZ[:, NF - 1:NF]).then_inc(s_tab, 1)
            dve.wait_ge(s_tabp, 4)
            link(dve.tensor_copy(small[0:NP_, 6:7], psA[1][0:NP_, 0:1]))
            link(dve.tensor_scalar(S1, psA[1][0:NP_, 1:1 + T], 1.0, None, ALU.add))
            link(dve.tensor_tensor(Fj, iota127[0:NP_, 0:T], psA[1][0:NP_, 1 + T:1 + 2 * T], ALU.subtract))
            link(dve.tensor_tensor(nR, nCZ, nZ, ALU.subtract))
            link(dve.tensor_scalar(nR, nR, small[0:NP_, 6:7], None, ALU.add))
            for q in range(NF // 25):
                cq = cube[0:NP_, 0:25 * T].rearrange("p (k t) -> p k t", t=T)
                rq = nR[:, q * 25:(q + 1) * 25].unsqueeze(2).to_broadcast([NP_, 25, T])
                link(dve.tensor_tensor(cq, rq, Fj.unsqueeze(1).to_broadcast([NP_, 25, T]), ALU.is_ge))
                link(dve.tensor_tensor(cq, cq, S1.unsqueeze(1).to_broadcast([NP_, 25, T]), ALU.mult))
                link(dve.tensor_reduce(nSL[:, q * 25:(q + 1) * 25], cq, AX.X, ALU.add))
            link(dve.tensor_tensor(nSL, nSL, nR, ALU.add))
            link(dve.tensor_tensor(nSL, nSL, nZ, ALU.mult))
            link(dve.tensor_tensor(nSL, nSL, nI[:, :, 0], ALU.add))
            dve.tensor_scalar(nDG, nI[:, :, 1], 1.0, None, ALU.max).then_inc(s_tab, 1)
            dve.wait_ge(s_tabp, 5)
            link(dve.tensor_copy(slotT[0:NF, :], psA[1][0:NF, 0:NP_]))
            link(dve.tensor_copy(ndT[0:NF, :, 0], psA[1][0:NF, NP_:2 * NP_]))
            dve.tensor_copy(ndT[0:NF, :, 1], psA[1][0:NF, 2 * NP_:3 * NP_]).then_inc(s_scat_in, 1)
            dve.wait_ge(s_tload, 16)
            link(dve.tensor_copy(tA, tI[:, :, 0]))
            dve.tensor_copy(tB, tI[:, :, 1]).then_inc(s_tab, 1)
            dve.wait_ge(s_tabp, 6)
            link(dve.tensor_copy(permf, psA[1][:, 0:T]))
            link(dve.tensor_copy(degf, psA[1][:, T:2 * T]))
            link(dve.tensor_copy(poutT[:, :], permf))
            link(dve.scalar_tensor_tensor(pinT[:, :], permf, float(N), permf, ALU.is_lt, ALU.mult))
            link(dve.reciprocal(invdeg[:, :], degf))
            for l in range(LAYERS):
                c = C[f"n{l}"]
                link(dve.tensor_scalar(invs[:, l, :], invdeg[:, :], downs[:, c:c + 1],
                                       WUP / (Y_LN if l == 0 else Y_H), ALU.mult, ALU.mult))
            dve.tensor_scalar(small[:, 0:1], ones[:, 0:1], 1.0, None, ALU.mult).then_inc(s_tables, 1)

            s = ph[0]

            def stats0(t):
                i = t.slot(2)
                dve.wait_ge(s.x[i], t.landed(2))
                after(dve, s.rr, (t + -1).n)
                dve.bn_stats(st6[:, :], X[i][:, :]).then_inc(s.r, 1)
                hold(dve, s_const, (s.r, (t + 1).n))
                dve.bn_aggr(mv[:, i, :], st6[:, :]).then_inc(s.dv, 1)
                dve.wait_ge(s.dv, (t + 1).n)
                after(dve, s.sc, (t + -1).n)
                dve.tensor_scalar(ssm[:, i:i + 1], mv[:, i, 1:2], LN_EPS, None, ALU.add).then_inc(s.ss, 1)

            def norm0(t):
                i = t.slot(2)
                dve.wait_ge(s.sc, (t + 1).n)
                after(dve, s.hhi, (t + -1).n)
                after(dve, s.hlo, (t + -1).n)
                dve.tensor_scalar(R[i][:, :], X[i][:, :], mv[:, i, 0:1], scl[:, i:i + 1], ALU.subtract, ALU.mult
                                  ).then_inc(s.rr, 1)
                dve.wait_ge(s.hhi, (t + 1).n)
                dve.wait_ge(s.rr, (t + 1).n)
                dve.scalar_tensor_tensor(HH[i][:, 1, :], R[i][:, :], LN_UP, HH[i][:, 0, :], ALU.mult, ALU.subtract
                                         ).then_inc(s.hlo, 1)

            def turn(t, l):
                s = ph[l]
                i = t.slot(2)
                dve.wait_ge(s.tr, (t + 1).n)
                after(dve, s.sp, (t + -1).n)
                dve.tensor_copy(HT[i][:, :, :, :], psT[i][:, :, :, :]).then_inc(s.ht, 1)

            def ylo(t, l):
                s = ph[l]
                i = t.slot(2)
                dve.wait_ge(s.yhi, (t + 1).n)
                k = Y_LN / (WUP * LN_UP) if l == 0 else Y_H / (WUP * H_UP)
                dve.scalar_tensor_tensor(YB[i][:, D:2 * D], psY[i][:, :], k, YB[i][:, 0:D], ALU.mult, ALU.subtract
                                         ).then_inc(s.ylo, 1)

            def sev(t, l):
                s = ph[l]
                i = t.slot(2)
                dve.wait_ge(s.sp, (t + 1).n)
                if not (isinstance(t.t, int) and t.t < 2):
                    dve.wait_ge(s.s2[i], (t + -2).landed(2))
                c = C[f"s{l}"]
                dve.scalar_tensor_tensor(SB[i][:, :], psS[i][:, :], downs[:, c:c + 1], bias[:, l, :],
                                         ALU.mult, ALU.add).then_inc(s.sev, 1)

            run_tiles(dve, 2, TN, [(2, norm0), (0, lambda t: ylo(t, 0)), (1, lambda t: turn(t, 0)),
                                   (3, stats0), (0, lambda t: sev(t, 0))])

            def one_hot(t, l):
                s = ph[l]
                i = t.slot(GRING)
                after(dve, s.agg, (t + (1 - GRING)).n)
                dve.tensor_scalar(Sm[i][:, :], iota_row[:, :], colT[:, bass.ds(t.t, 1)], rowval[:, 0:1],
                                  ALU.is_equal, ALU.mult).then_inc(s.smat, 1)

            def carry_lo(t, l):
                s = ph[l]
                i, o = t.slot(2), (t + 1).slot(GRING)
                if isinstance(t.t, int) and t.t == T - 1:
                    return
                dve.wait_ge(s.chi, (t + 1).n - t.run)
                dve.scalar_tensor_tensor(G[o][0:1, D:2 * D], psA[0 if l == 3 else i][0:1, :], 1.0 / CARRY,
                                         G[o][0:1, 0:D], ALU.mult, ALU.subtract).then_inc(s.clo, 1)

            def combine(t, l):
                s = ph[l]
                i = t.slot(2)
                if l == 1:
                    dve.wait_ge(s.x[i], t.landed(2))
                else:
                    dve.wait_ge(s.xs[i], Tile(t.U, t.j, t.k, l - 2).landed(2))
                dve.wait_ge(s.agg, (t + 1).n)
                after(dve, s.rr, (t + -1).n)
                dve.scalar_tensor_tensor(R[i][:, :], psA[0 if l == 3 else i][:, :], invs[:, l - 1, bass.ds(t.t, 1)],
                                         Sl[i][:, :], ALU.mult, ALU.add).then_inc(s.r, 1)
                dve.wait_ge(s.r, (t + 1).n)
                dve.scalar_tensor_tensor(junk[:, :], R[i][:, :], 0.0, R[i][:, :], ALU.max, ALU.mult,
                                         accum_out=ss[:, i:i + 1]).then_inc(s.dv2, 1)
                dve.wait_ge(s.dv2, (t + 1).n)
                after(dve, s.sc, (t + -1).n)
                up = 1.0 if l == 3 else H_UP ** -2
                dve.tensor_scalar(ssm[:, i:i + 1], ss[:, i:i + 1], 1e-24, up, ALU.max, ALU.mult).then_inc(s.ss, 1)

            def hlo(t, l):
                s = ph[l]
                i = t.slot(2)
                dve.wait_ge(s.hhi, (t + 1).n)
                dve.scalar_tensor_tensor(HH[i][:, 1, :], RR[i][:, :], scl[:, i:i + 1], HH[i][:, 0, :],
                                         ALU.mult, ALU.subtract).then_inc(s.hlo, 1)

            for l in (1, 2):
                run_tiles(dve, 4, T, [(5, lambda t, l=l: one_hot(t, l)), (2, lambda t, l=l: hlo(t, l)), (0, lambda t, l=l: ylo(t, l)),
                                      (1, lambda t, l=l: turn(t, l)), (3, lambda t, l=l: carry_lo(t, l)),
                                      (3, lambda t, l=l: combine(t, l)), (0, lambda t, l=l: sev(t, l))], l - 1)

            s = ph[3]

            def own(t):
                return Tile(t.U, t.j, t.k)

            def x2(t):
                i, q = t.slot(2), t.slot(8)
                dve.wait_ge(s.sc, (t + 1).n)
                dve.wait_ge(s.rr, (t + 1).n)
                t = own(t)
                dve.wait_ge(s.xg[i], t.landed(2))
                after(dve, f3.o, (t + -7).n)
                dve.scalar_tensor_tensor(X2[q], RR[i][:, :], scl[:, i:i + 1], X[i][:, :], ALU.mult, ALU.add
                                         ).then_inc(f3.x2, 1)
                dve.wait_ge(f3.x2, (t + 1).n)
                dve.bn_stats(st6[:, :], X2[q]).then_inc(f3.tiny, 1)

            def var2(t):
                t = own(t)
                i = t.slot(2)
                hold(dve, s_const, (f3.tiny, t.t * 4 + 1))
                dve.bn_aggr(mv3[:, i, :], st6[:, :]).then_inc(f3.tiny, 1)
                dve.wait_ge(f3.tiny, t.t * 4 + 2)
                after(dve, f3.rs, (t + -1).n)
                dve.tensor_scalar(vv[:, i, 0:1], mv3[:, i, 1:2], LN_EPS, None, ALU.add).then_inc(f3.tiny, 1)
                dve.wait_ge(f3.tiny, t.t * 4 + 3)
                dve.reciprocal(vv[:, i, 1:2], vv[:, i, 0:1]).then_inc(f3.tiny, 1)
                dve.wait_ge(f3.tiny, t.t * 4 + 4)
                dve.tensor_scalar(vv[:, i, 1:2], vv[:, i, 1:2], mv3[:, i, 1:2], LN_EPS, ALU.mult, ALU.add
                                  ).then_inc(f3.v2, 1)

            def factors(t):
                t = own(t)
                i = t.slot(2)
                dve.wait_ge(f3.rs, (t + 1).n)
                after(dve, f3.xlo, (t + -1).n)
                after(dve, f3.xhi, (t + -1).n)
                dve.tensor_scalar(nmr[:, i:i + 1], mv3[:, i, 0:1], rs[:, i, 0:1], -1.0, ALU.mult, ALU.mult
                                  ).then_inc(f3.nmr, 1)
                dve.wait_ge(f3.nmr, (t + 1).n)
                dve.tensor_scalar(r2s[:, i:i + 1], rs[:, i, 1:2], LN_UP, None, ALU.mult).then_inc(f3.r2s, 1)

            def xlo(t):
                t = own(t)
                i, q = t.slot(2), t.slot(8)
                dve.wait_ge(f3.y, (t + 1).n)
                dve.wait_ge(f3.xhi, (t + 1).n)
                dve.scalar_tensor_tensor(HH[i][:, 1, :], YF[q], r2s[:, i:i + 1], HH[i][:, 0, :],
                                         ALU.mult, ALU.subtract).then_inc(f3.xlo, 1)

            TOP = 8

            def top_two(t):
                t = own(t)
                i = t.slot(2)
                base = t.t * TOP

                def nxt(ins, k):
                    ins.then_inc(f3.tiny2, 1)
                    hold(dve, s_const, (f3.tiny2, base + k))

                dve.wait_ge(f3.pre, (t + 1).n)
                lg, g = gv[:, i, 0:8], wsc[:, i, :]
                nxt(dve.scalar_tensor_tensor(g, psG[:, 8:16], downs[:, CG:CG + 1], bgb[:, :], ALU.mult, ALU.add), 1)
                nxt(dve.scalar_tensor_tensor(g, psG[:, 0:8], downs[:, CG:CG + 1], g, ALU.mult, ALU.add), 2)
                nxt(dve.max(lg, g), 3)
                nxt(dve.max_index(gi[:, i, :], lg, g), 4)
                dve.tensor_scalar(gv[:, i, 8:9], lg[:, 0:1], lg[:, 1:2], None, ALU.subtract).then_inc(f3.lg, 1)
                dve.tensor_copy(gv[:, i, 10:12], gi[:, i, 0:2]).then_inc(f3.tiny2, 1)
                dve.wait_ge(f3.tiny2, base + 5)
                dve.tensor_scalar(gv[:, i, 16:24], iota_row[:, 0:8], gv[:, i, 10:11], None, ALU.is_equal
                                  ).then_inc(f3.tiny2, 1)
                dve.wait_ge(f3.tiny2, base + 6)
                dve.scalar_tensor_tensor(gv[:, i, 24:32], iota_row[:, 0:8], gv[:, i, 11:12], gv[:, i, 16:24],
                                         ALU.is_equal, ALU.add).then_inc(f3.tiny2, 1)
                dve.wait_ge(f3.tiny2, base + 7)
                dve.scalar_tensor_tensor(gv[:, i, 32:40], gv[:, i, 16:24], 2.0, gv[:, i, 24:32],
                                         ALU.mult, ALU.subtract).then_inc(f3.tiny2, 1)

            def confidences(t):
                t = own(t)
                i = t.slot(2)
                dve.wait_ge(f3.th, (t + 1).n)
                dve.wait_ge(f3.tiny2, t.t * TOP + TOP)
                after(dve, f3.hs, (t + -1).n)
                dve.scalar_tensor_tensor(wv[:, i, :], gv[:, i, 32:40], gv[:, i, 9:10], gv[:, i, 24:32],
                                         ALU.mult, ALU.add).then_inc(f3.w, 1)
                dve.wait_ge(f3.w, (t + 1).n)
                after(dve, f3.th2, (t + -1).n)
                dve.tensor_scalar(W24[i][:, 0:16].rearrange("p (a e) -> p a e", a=2),
                                  wv[:, i, :].unsqueeze(1).to_broadcast([P, 2, EX_]), ups[:, CB:CB + 1], None,
                                  ALU.mult).then_inc(f3.z24, 1)
                dve.wait_ge(f3.z24, (t + 1).n)
                dve.scalar_tensor_tensor(W24[i][:, 16:24], wv[:, i, :], ups[:, CB:CB + 1], W24[i][:, 0:8],
                                         ALU.mult, ALU.subtract).then_inc(f3.w24, 1)

            def flo(t):
                t = own(t)
                i = t.slot(2)
                dve.wait_ge(f3.hhi, (t + 1).n)
                dve.scalar_tensor_tensor(FH[i][:, 1, :], HS[i], ups[:, CB:CB + 1], FH[i][:, 0, :],
                                         ALU.mult, ALU.subtract).then_inc(f3.hlo, 1)

            def zf(t):
                t = own(t)
                i, q = t.slot(2), t.slot(8)
                dve.wait_ge(f3.cmb, (t + 1).n)
                dve.scalar_tensor_tensor(Z[i], psO[:, :], downs[:, FINAL:FINAL + 1], YF[q], ALU.mult, ALU.add
                                         ).then_inc(f3.z, 1)
                dve.wait_ge(f3.z, (t + 1).n)
                dve.bn_stats(st6b[:, :], Z[i]).then_inc(f3.tiny3, 1)
                hold(dve, s_const, (f3.tiny3, t.t * 2 + 1))
                dve.bn_aggr(zm[:, i, :], st6b[:, :]).then_inc(f3.tiny3, 1)
                dve.wait_ge(f3.tiny3, t.t * 2 + 2)
                dve.tensor_scalar(zv[:, i:i + 1], zm[:, i, 1:2], LN_EPS, None, ALU.add).then_inc(f3.zv, 1)
                dve.scalar_tensor_tensor(Z[i], Z[i], zm[:, i, 0:1], ogb[:, :], ALU.subtract, ALU.mult
                                         ).then_inc(f3.o1, 1)

            def result(t):
                t = own(t)
                i = t.slot(2)
                dve.wait_ge(f3.o1, (t + 1).n)
                dve.wait_ge(f3.zr, (t + 1).n)
                dve.wait_ge(f3.xob, (t + 1).n)
                if not (isinstance(t.t, int) and t.t < 2):
                    dve.wait_ge(f3.out[i], (t + -2).landed(2))
                dve.scalar_tensor_tensor(OUT[i], Z[i], zr[:, i:i + 1], X2[t.slot(8)], ALU.mult, ALU.add
                                         ).then_inc(f3.o, 1)

            run_tiles(dve, 8, T, [(2, factors), (-5, result), (3, x2), (-1, top_two), (4, lambda t: carry_lo(t, 3)),
                                  (4, lambda t: combine(t, 3)), (3, var2), (-1, confidences),
                                  (-2, flo), (6, lambda t: one_hot(t, 3)), (2, xlo), (-4, zf)], 2)

        @block.tensor
        def _(pe):
            pe.wait_ge(s_const, 1)
            pe.wait_ge(s_bm, 1)
            pe.wait_ge(s_constv, 1)
            for m, name in enumerate(NAMES):
                if name == "w1":
                    pe.wait_ge(s_wload[m % 2], 64 * (m // 2 + 1))
                    for c in range(KC):
                        mm = pe.matmul(psA[1][:, :], bmat[:, c, :], raw[:, m % 2, c, :], start=(c == 0), stop=(c == KC - 1))
                    mm.then_inc(s_ffb, 1)
                    pe.wait_ge(s_b1done, 1)
                    for c in range(KC):
                        mm = pe.matmul(psA[1][:, 0:EX_], bmat[:, c, :], wgr[:, c, :], start=(c == 0), stop=(c == KC - 1))
                    mm.then_inc(s_ffb, 1)
                pe.wait_ge(s_sq, m + 1)
                after(pe, s_cmax, m)
                for c in range(KC):
                    mm = pe.matmul(psA[0][:, :], ones[:, :], sq[:, c, :], start=(c == 0),
                                   stop=(c == KC - 1 and name != "w2"))
                if name == "w2":
                    pe.wait_ge(s_sqb, 1)
                    mm = pe.matmul(psA[0][:, :], ones[0:EX_, :], sqb2[:, :], start=False, stop=True)
                mm.then_inc(s_cn, 1)
            pe.wait_ge(s_sq, 9)
            pe.wait_ge(s_cmax, 8)
            for c in range(KC):
                mm = pe.matmul(psA[0][:, 0:EX_], ones[:, :], sq[:, 0, EX_ * c:EX_ * (c + 1)], start=(c == 0),
                               stop=(c == KC - 1))
            mm.then_inc(s_cn, 1)

            def tp(o, i, rows):
                return pe.transpose(o, i, iden[0:rows, 0:rows])

            pe.wait_ge(s_tab, 1)
            tp(psA[1][0:1, 0:T], pm_col[:, 0:1], T).then_inc(s_tabp, 1)
            pe.wait_ge(s_tab, 2)
            tp(psA[1][0:T, 0:1], pm_row[0:1, 0:T], 1).then_inc(s_tabp, 1)
            pe.wait_ge(s_tab, 3)
            for k, a in enumerate((eCOL, eSLOT, eDEG, eDST, eSRC)):
                mm = tp(psA[1][:, k * T:(k + 1) * T], a, T)
            mm.then_inc(s_tabp, 1)
            pe.wait_ge(s_tab, 4)
            pe.matmul(psA[1][0:NP_, 0:1], upper[0:NP_, 0:NP_], small[0:NP_, 5:6], start=True, stop=True)
            pe.matmul(psA[1][0:NP_, 1:1 + 2 * T], smat, iu, start=True, stop=True).then_inc(s_tabp, 1)
            pe.wait_ge(s_tab, 5)
            for k, a in enumerate((nSL, node_no[:, :], nDG)):
                mm = tp(psA[1][0:NF, k * NP_:(k + 1) * NP_], a, NP_)
            mm.then_inc(s_tabp, 1)
            pe.wait_ge(s_tab, 6)
            tp(psA[1][:, 0:T], tA, T)
            tp(psA[1][:, T:2 * T], tB, T).then_inc(s_tabp, 1)

            pe.wait_ge(s_wlo, 8)
            pe.wait_ge(s_tables, 1)

            def turn(t, l):
                s = ph[l]
                i = t.slot(2)
                pe.wait_ge(s.hhi, (t + 1).n)
                pe.wait_ge(s.hlo, (t + 1).n)
                after(pe, s.ht, (t + -1).n)
                for a in range(2):
                    for c in range(KC):
                        mm = pe.transpose(psT[i][:, a, c, :], HH[i][:, a, c * P:(c + 1) * P], iden16[:, :])
                mm.then_inc(s.tr, 1)

            def neigh(t, l):
                s = ph[l]
                i = t.slot(2)
                pe.wait_ge(s.ht, (t + 1).n)
                after(pe, s.ylo, (t + -1).n)
                products(pe, psY[i][:, :], HT[i], WT[f"n{l}"]).then_inc(s.y, 1)

            def own(t, l):
                s = ph[l]
                i = t.slot(2)
                after(pe, s.sev, (t + -1).n)
                products(pe, psS[i][:, :], HT[i], WT[f"s{l}"]).then_inc(s.sp, 1)

            run_tiles(pe, 2, TN, [(0, lambda t: neigh(t, 0)), (1, lambda t: turn(t, 0)), (0, lambda t: own(t, 0))])

            def aggregate(t, l):
                s = ph[l]
                i = t.slot(2)
                g = t.slot(GRING)
                pe.wait_ge(s.g[g], t.landed(GRING))
                pe.wait_ge(s.smat, (t + 1).n)
                if isinstance(t.t, int) and t.t == 0:
                    pe.wait_ge(s.c0, t.run + 1)
                else:
                    pe.wait_ge(s.clo, t.n - t.run)
                back = 0 if l == 3 else -1
                after(pe, s.r, (t + back).n)
                acc = psA[0 if l == 3 else i][:, :]
                pe.matmul(acc, Sm[g][:, :], G[g][:, 0:D], start=True, stop=False)
                pe.matmul(acc, Sm[g][:, :], G[g][:, D:2 * D], start=False, stop=True).then_inc(s.agg, 1)

            for l in (1, 2):
                run_tiles(pe, 4, T, [(0, lambda t, l=l: neigh(t, l)), (1, lambda t, l=l: turn(t, l)),
                                     (0, lambda t, l=l: own(t, l)), (3, lambda t, l=l: aggregate(t, l))], l - 1)

            def own(t):
                return Tile(t.U, t.j, t.k)

            def up(t):
                t = own(t)
                i = t.slot(2)
                pe.wait_ge(f3.txc, (t + 1).n)
                after(pe, f3.gel, (t + -1).n)
                products(pe, psY[i][:, :], HT[i], WT["w1"], stop=False)
                pe.matmul(psY[i][:, :], c2row[:, :], b1s[:, :], start=False, stop=True)
                after(pe, f3.lg, t.t)
                for a in range(2):
                    for c in range(KC):
                        mm = pe.matmul(psG[:, 0:16], HT[i][:, a, c, :], wg16[:, c, :], start=(a == 0 and c == 0),
                                       stop=(a == 1 and c == KC - 1))
                mm.then_inc(f3.pre, 1)

            def turn_h(t):
                t = own(t)
                i = t.slot(2)
                pe.wait_ge(f3.hhi, (t + 1).n)
                pe.wait_ge(f3.hlo, (t + 1).n)
                pe.wait_ge(f3.w24, (t + 1).n)
                after(pe, f3.thc, t.t)
                after(pe, f3.wtt, t.t)
                pe.transpose(psW[0:24, 0:P], W24[i][:, :], iden16[:, :])
                for a in range(2):
                    for c in range(KC):
                        mm = pe.transpose(psH[:, a, c, :], FH[i][:, a, c * P:(c + 1) * P], iden16[:, :])
                mm.then_inc(f3.th2, 1)

            def turn_x(t):
                t = own(t)
                i = t.slot(2)
                pe.wait_ge(f3.xhi, (t + 1).n)
                pe.wait_ge(f3.xlo, (t + 1).n)
                after(pe, f3.txc, t.t)
                for a in range(2):
                    for c in range(KC):
                        mm = pe.transpose(psX[:, a, c, :], HH[i][:, a, c * P:(c + 1) * P], iden16[:, :])
                mm.then_inc(f3.tx, 1)

            def down(t):
                t = own(t)
                i = t.slot(2)
                pe.wait_ge(f3.thc, (t + 1).n)
                pe.wait_ge(f3.wtt, (t + 1).n)
                after(pe, f3.z, t.t)
                products(pe, psO[:, :], FT[i], WT["w2"], stop=False)
                pe.matmul(psO[:, :], WTT[i][:, :], b2s[:, :], start=False, stop=True).then_inc(f3.cmb, 1)

            run_tiles(pe, 8, T, [(4, lambda t: aggregate(t, 3)), (-4, down), (-3, turn_h), (0, up), (1, turn_x)], 2)


_INS = ['x', 'src', 'dst', 'L0_gnn_W_self', 'L0_gnn_W_neigh', 'L0_gnn_b', 'L0_ffn_Wg', 'L0_ffn_W1', 'L0_ffn_b1',
        'L0_ffn_W2', 'L0_ffn_b2', 'L0_ffn_ln_g', 'L0_ffn_ln_b', 'L0_ffn_out_g', 'L0_ffn_out_b']
_OUTS = [((N, D), 'float32')]


def kernel(**inputs):
    import numpy as _np
    import concourse.bacc as _bacc
    from concourse import mybir as _mybir
    from concourse.bass_utils import run_bass_kernel_spmd as _run

    nc = _bacc.Bacc("TRN2", target_bir_lowering=False, num_devices=1)
    arrays, args = {}, []
    for name in _INS:
        a = _np.ascontiguousarray(inputs[name])
        arrays[f"in_{name}_dram"] = a
        args.append(nc.dram_tensor(f"in_{name}_dram", a.shape, _mybir.dt.from_np(a.dtype), kind="ExternalInput").ap())
    for i, (shape, dtype) in enumerate(_OUTS):
        dt = _mybir.dt.from_np(_np.dtype(dtype))
        args.append(nc.dram_tensor(f"out_{i}_dram", shape, dt, kind="ExternalOutput").ap())
    build(nc, *args)
    r = _run(nc, [arrays], core_ids=[0])
    return r.results[0]["out_0_dram"]
```

```python
from contextlib import ExitStack

import concourse.bass as bass
from concourse import mybir

ALU = mybir.AluOpType
ACT = mybir.ActivationFunctionType
AX = mybir.AxisListType
F32 = mybir.dt.float32
F16 = mybir.dt.float16
BF16 = mybir.dt.bfloat16
I32 = mybir.dt.int32
U32 = mybir.dt.uint32

P = 128
N = 10000
E = 10000
D = 512
KC = D // P
LAYERS = 3
EXPERTS = 8
HIDDEN = 64
EPT = P - 1
T = -(-E // EPT)
TN = -(-N // P)
NLAST = N - (TN - 1) * P
NP_, NF = 80, N // 80
SLOTS = T * P
N_FIRST = 2
STEP_GATE = 26
STEP_INFO = 16
STEP_SLOTS = 20
STEP_SCATTER = 48
STEP_TABLES = 71


def WSTEP(m):
    return 2 + 4 * (m - N_FIRST)


GRING = 4
BIG = float(1 << 20)
LN_EPS = 1e-5
CARRY = 2.0 ** 14

WUP = 2.0 ** 12
LN_UP = 2.0 ** 10
H_UP = 2.0 ** 14
FF_UP = 2.0 ** 13
Y_LN, Y_H = 2.0 ** 8, 2.0 ** 13
ROOT_D = 22.63


class Tile:

    def __init__(self, U, j, k, run=0):
        self.U, self.j, self.k, self.run = U, j, k, run

    def __add__(self, n):
        return Tile(self.U, self.j, self.k + n, self.run)

    @property
    def t(self):
        return self.j * self.U + self.k

    @property
    def n(self):
        return self.t + self.run * T

    @property
    def own(self):
        return Tile(self.U, self.j, self.k)

    def slot(self, ring):
        return self.k % ring

    def landed(self, ring):
        before = self.run * ((T + ring - 1 - self.k % ring) // ring)
        return 16 * (self.j * (self.U // ring) + self.k // ring + 1 + before)


def run_steps(eng, U, tiles, stages, begin, end, run=0):
    offs = [o for o, _ in stages]
    first = U if min(offs) >= 0 else U * (-(-(2 - min(offs)) // U))
    last = first + (tiles - 1 - max(max(offs), 0) - first) // U * U
    lo, hi = max(first, -(-begin // U) * U), min(last, end // U * U)

    def step(j, k, peeled):
        for off, f in stages:
            if not peeled or 0 <= k + off < tiles:
                f(Tile(U, j, k + off, run))

    if hi - lo < 2 * U:
        lo = hi = end
    for t in range(begin, lo):
        step(0, t, True)
    if lo < hi:
        with eng.Fori(lo // U, hi // U) as j:
            for k in range(U):
                step(j, k, False)
    for t in range(hi, end):
        step(0, t, True)


def run_tiles(eng, U, tiles, stages, run=0):
    offs = [o for o, _ in stages]
    run_steps(eng, U, tiles, stages, -max(max(offs), 0), tiles - min(min(offs), 0), run)


def run_plan(eng, U, tiles, stages, jobs, windows=()):
    offs = [o for o, _ in stages]
    begin, end = -max(max(offs), 0), tiles - min(min(offs), 0)
    cuts = sorted({begin, end} | {j[0] for j in jobs} | {e for w in windows for e in w[:2]})
    for a, b in zip(cuts, cuts[1:]):
        for at, f, arg in jobs:
            if at == a:
                f() if arg is None else f(arg)
        run_steps(eng, U, tiles, stages + [(0, f) for x, y, f in windows if x <= a and b <= y], a, b)


def after(eng, sem, n):
    if not (isinstance(n, int) and n <= 0):
        eng.wait_ge(sem, n)


def hold(eng, done, *waits):
    for _, n in waits:
        if not isinstance(n, int):
            eng.lower_val(n)
    eng.wait_ge(done, 1)
    for sem, n in waits:
        if not (isinstance(n, int) and n <= 0):
            eng.wait_ge(sem, n)


class NaturalSems:

    def __init__(self, sem):
        self.x = [sem(f"p0_x{i}") for i in range(2)]
        self.ys = [sem(f"p0_ys{i}") for i in range(2)]
        self.s2 = [sem(f"p0_s2{i}") for i in range(2)]
        self.r = sem("p0_stats")
        self.dv = sem("p0_mean_var")
        self.ss = sem("p0_var_eps")
        self.sc = sem("p0_rstd")
        self.rr = sem("p0_rows")
        self.hhi = sem("p0_hhi")
        self.hlo = sem("p0_hlo")
        self.tr = sem("p0_turned")
        self.ht = sem("p0_ht")
        self.y = sem("p0_y")
        self.yhi = sem("p0_yhi")
        self.ylo = sem("p0_ylo")
        self.sp = sem("p0_own")
        self.sev = sem("p0_self")


class SlotSems:

    def __init__(self, sem):
        self.g = [sem(f"g{i}") for i in range(GRING)]
        self.x = [sem(f"x{i}") for i in range(2)]
        self.xs = [sem(f"xs{i}") for i in range(2)]
        self.xg = [sem(f"xg{i}") for i in range(2)]
        self.ys = [sem(f"ys{i}") for i in range(2)]
        self.s2 = [sem(f"s2{i}") for i in range(2)]
        self.idx = sem("idx")
        self.idx_in1 = sem("idx_in1")
        self.idx_in3 = sem("idx_in3")
        self.idx_out = sem("idx_out")
        self.smat = sem("smat")
        self.c0 = sem("c0")
        self.chi = sem("chi")
        self.clo = sem("clo")
        self.agg = sem("agg")
        self.r = sem("r")
        self.rr = sem("relu")
        self.dv2 = sem("sumsq")
        self.ss = sem("sumsq_max")
        self.sc = sem("rnorm")
        self.hhi = sem("hhi")
        self.hlo = sem("hlo")
        self.tr = sem("turned")
        self.ht = sem("ht")
        self.y = sem("y")
        self.yhi = sem("yhi")
        self.ylo = sem("ylo")
        self.sp = sem("own")
        self.sev = sem("self")


class FfnSems:

    def __init__(self, sem):
        self.out = [sem(f"f3_out{i}") for i in range(2)]
        self.x2 = sem("f3_x2")
        self.bnx = sem("f3_bnx")
        self.aggx = sem("f3_aggx")
        self.epsx = sem("f3_epsx")
        self.recx = sem("f3_recx")
        self.v2 = sem("f3_v2")
        self.dist = sem("f3_dist")
        self.rest = sem("f3_rest")
        self.idx = sem("f3_idx")
        self.nmr = sem("f3_nmr")
        self.rs = sem("f3_rs")
        self.r2s = sem("f3_r2s")
        self.y = sem("f3_y")
        self.xhi = sem("f3_xhi")
        self.xlo = sem("f3_xlo")
        self.tx = sem("f3_tx")
        self.txc = sem("f3_txc")
        self.pre = sem("f3_pre")
        self.gel = sem("f3_gel")
        self.logit = sem("f3_logit")
        self.top = sem("f3_top")
        self.topi = sem("f3_topi")
        self.topf = sem("f3_topf")
        self.hot1 = sem("f3_hot1")
        self.hot2 = sem("f3_hot2")
        self.hotd = sem("f3_hotd")
        self.lg = sem("f3_lg")
        self.th = sem("f3_th")
        self.w = sem("f3_w")
        self.z24 = sem("f3_z24")
        self.w24 = sem("f3_w24")
        self.hs = sem("f3_hs")
        self.hhi = sem("f3_hhi")
        self.hlo = sem("f3_hlo")
        self.th2 = sem("f3_th2")
        self.wtt = sem("f3_wtt")
        self.thc = sem("f3_thc")
        self.cmb = sem("f3_cmb")
        self.z = sem("f3_z")
        self.bnz = sem("f3_bnz")
        self.aggz = sem("f3_aggz")
        self.zv = sem("f3_zv")
        self.zr = sem("f3_zr")
        self.o1 = sem("f3_o1")
        self.xob = sem("f3_xob")
        self.o = sem("f3_o")


def build(nc, x, src, dst, W_self, W_neigh, b, Wg, W1, b1, W2, b2, ln_g, ln_b, out_g, out_b, out):
    with ExitStack() as ctx:
        def sb(name, shape, dt=F32):
            return ctx.enter_context(nc.sbuf_tensor(name, shape, dt))

        def ps(name, shape, dt=F32):
            return ctx.enter_context(nc.psum_tensor(name, shape, dt))

        def sem(name):
            return ctx.enter_context(nc.semaphore(name))

        def dram(name, shape, dt):
            return nc.dram_tensor(name, shape, dt)

        Yd = [dram(f"y_rows{l}", [N, 2 * D], F16) for l in range(LAYERS)]
        Sd0 = dram("self_rows0", [N, D], F32)
        Sd = [None] + [dram(f"self_rows{l}", [SLOTS, D], F32) for l in (1, 2)]
        info = dram("node_info", [N, 2], F32)
        table = dram("slot_table", [SLOTS, 2], F32)

        NAMES = ["n0", "s0", "n1", "s1", "n2", "s2", "w1", "w2"]
        WT = {n: sb(f"w_{n}", [P, 2, KC, D], F16) for n in NAMES}
        wg16 = sb("wg16", [P, KC, 2 * EXPERTS], F16)
        b2s = sb("b2s", [3 * EXPERTS, D], F16)
        raw = sb("raw", [P, 2, KC, D])
        sq = sb("sq", [P, KC, D])
        ups = sb("ups", [P, 16])
        downs = sb("downs", [P, 16])
        nrm = sb("nrm", [P, 16])
        cmax = sb("cmax", [P, 16])
        bias = sb("bias", [P, LAYERS, D])
        b1b = sb("b1b", [P, D])
        ogb = sb("ogb", [P, D])
        obb = sb("obb", [P, D])
        wgr = sb("wgr", [P, KC, EXPERTS])
        wgs = sb("wgs", [P, KC, EXPERTS])
        bgb = sb("bgb", [P, EXPERTS])
        b2r = sb("b2r", [3 * EXPERTS, D])
        b2h = sq[0:3 * EXPERTS, 3, 0:D // 2].bitcast(F16)
        sqb2 = sb("sqb2", [EXPERTS, D], BF16)
        sqw = sq[:, 0:2, :].rearrange("p c n -> p (c n)").bitcast(BF16).rearrange("p (c n) -> p c n", c=KC)
        rowmask = sb("rowmask", [3 * EXPERTS, 1])
        gcol = sb("gcol", [P, KC])
        bcol = sb("bcol", [P, KC])
        bmat = sb("bmat", [P, KC, P])
        small = sb("small", [P, 16])

        ones = sb("ones", [P, P])
        iden = sb("iden", [P, P])
        iden16 = sb("iden16", [P, P], F16)
        upper = sb("upper", [P, P])
        iota_i = sb("iota_i", [P, 3 * P], I32)
        iota_row = sb("iota_row", [P, P])
        ones16 = sb("ones16", [P, P], BF16)
        iota16 = sb("iota16", [P, P], F16)
        iota127 = sb("iota127", [P, P])
        edge_no = sb("edge_no", [P, EPT])
        node_no_i = sb("node_no_i", [NP_, NF], I32)
        node_no = sb("node_no", [NP_, NF])
        tile128 = sb("tile128", [P, 1])
        rowval = sb("rowval", [P, 1])
        minus_rowval = sb("minus_rowval", [P, 1])
        dist = sb("dist", [P, P])
        halfpow = sb("halfpow", [P, 2])
        mhalf2 = sb("mhalf2", [P, 2])
        expo = sb("expo", [P, 1], U32)

        colT = sb("colT", [P, T])
        minus_colT = sb("minus_colT", [P, T])
        srcT = sb("srcT", [P, T], U32)
        pinT = sb("pinT", [P, T], U32)
        poutT = sb("poutT", [P, T], U32)
        invdeg = sb("invdeg", [P, T])
        invs = sb("invs", [P, LAYERS, T])

        area = sb("area", [P, 12288])

        G = [sb(f"G{i}", [P, 2 * D], F16) for i in range(2)]
        G += [area[:, 22 * D + D * i:23 * D + D * i].bitcast(F16) for i in range(GRING - 2)]
        Sm = [sb(f"Sm{i}", [P, P], F16) for i in range(GRING)]
        Sl = [sb(f"Sl{i}", [P, D]) for i in range(2)]
        X = [sb(f"X{i}", [P, D]) for i in range(2)]
        R = [sb(f"R{i}", [P, D]) for i in range(2)]
        RR = [sb(f"RR{i}", [P, D]) for i in range(2)]
        junk = sb("junk", [P, D])
        HH = [sb(f"HH{i}", [P, 2, D], F16) for i in range(2)]
        HT = [sb(f"HT{i}", [P, 2, KC, P], F16) for i in range(2)]
        YB = [sb(f"YB{i}", [P, 2 * D], F16) for i in range(2)]
        SB = [sb(f"SB{i}", [P, D]) for i in range(2)]
        idx = [[sb(f"idx{a}{i}", [P, 1], U32) for i in range(GRING if a == 0 else 2)] for a in range(3)]
        ss = sb("ss", [P, 2])
        ssm = sb("ssm", [P, 2])
        scl = sb("scl", [P, 2])
        st6 = sb("st6", [P, 6])
        mv = sb("mv", [P, 2, 2])
        gi = sb("gi", [P, 2, 8], U32)
        gv = sb("gv", [P, 2, 40])
        wv = sb("wv", [P, 2, EXPERTS])
        nmr = sb("nmr", [P, 2])
        minus = sb("minus", [P, P], F16)
        vinv = sb("vinv", [P, 2])
        c2row = sb("c2row", [2, P], F16)
        b1s = sb("b1s", [2, D], F16)
        b1h = sq[0:2, 3, 0:D // 2].bitcast(F16)

        psA = [ps(f"psA{i}", [P, D]) for i in range(2)]
        psT = [ps(f"psT{i}", [P, 2, KC, P], F16) for i in range(2)]
        psY = [ps(f"psY{i}", [P, D]) for i in range(2)]
        psS = [ps(f"psS{i}", [P, D]) for i in range(2)]

        s_const = sem("s_const")
        s_constv = sem("s_constv")
        s_wload = [sem(f"s_wload{i}") for i in range(2)]
        s_free = sem("s_free")
        s_sq = sem("s_sq")
        s_sqb = sem("s_sqb")
        s_cn = sem("s_cn")
        s_cmax = sem("s_cmax")
        s_nrm = sem("s_nrm")
        s_scale = sem("s_scale")
        s_whi = sem("s_whi")
        s_wlo = sem("s_wlo")
        s_bload = sem("s_bload")
        s_dv = sem("s_dv")
        s_pl = sem("s_pl")
        s_bm = sem("s_bm")
        s_ffb = sem("s_ffb")
        s_wgain = sem("s_wgain")
        s_epad = sem("s_epad")
        s_eload = sem("s_eload")
        s_tab = sem("s_tab")
        s_tabp = sem("s_tabp")
        s_infoz = sem("s_infoz")
        s_sc = [sem(f"s_scat{i}") for i in range(2)]
        s_nload = sem("s_nload")
        s_tload = sem("s_tload")
        s_tinit = sem("s_tinit")
        s_scat_in = sem("s_scat_in")
        s_scat_cp = sem("s_scat_cp")
        s_tables = sem("s_tables")

        def view(at, parts, n, dt=F32):
            v = area[0:parts, at:at + n]
            return v if dt is F32 else v.bitcast(dt)

        eDi, eNi, eSi = (view(P * i, T, EPT, I32) for i in range(3))
        eD, eN, eL, eCS, eEX, eM, eT1 = (view(P * (3 + i), T, P) for i in range(7))
        eCOL, eSLOT, eDEG, eDST, eSRC, eSC = (view(P * (10 + i), T, P) for i in range(6))
        pm_row = view(P * 16, 1, P)
        pm_col = view(P * 17, T, 2)
        dstT = view(P * 18, P, 80, U32)
        infoT = view(P * 19, P, 160).rearrange("p (t two) -> p t two", two=2)
        cpI = [view(P * (21 + i), P, 8, U32) for i in range(2)]
        cpV = [view(P * (21 + i) + 16, P, 16).rearrange("p (t two) -> p t two", two=2) for i in range(2)]
        zero = view(P * 23, NP_, 2 * NF)
        tinit = view(P * 25, T, 2 * P).rearrange("p (k two) -> p k two", two=2)
        stot = view(P * 27, T, 1)
        smat = view(P * 28, T, NP_)
        iu = view(P * 29, T, 2 * T)
        NB = 0
        nI = view(NB, NP_, 2 * NF).rearrange("p (k two) -> p k two", two=2)
        nZ, nCZ, nR, nSL, nDG = (view(NB + P * (2 + i), NP_, NF) for i in range(5))
        Fj = view(NB + P * 7, NP_, T)
        S1 = view(NB + P * 8, NP_, T)
        slotT = view(P * 9, P, 80, U32)
        ndT = view(P * 10, P, 160).rearrange("p (t two) -> p t two", two=2)
        tI = view(P * 12, T, 2 * P).rearrange("p (k two) -> p k two", two=2)
        tA = view(P * 14, T, P)
        tB = view(P * 15, T, P)
        permf = view(P * 16, P, T)
        degf = view(P * 17, P, T)

        M_OF = {"n0": (W_neigh, 0), "s0": (W_self, 0), "n1": (W_neigh, 1), "s1": (W_self, 1),
                "n2": (W_neigh, 2), "s2": (W_self, 2)}

        C = {n: i for i, n in enumerate(NAMES)}
        CG, CB = 8, 9
        FINAL = 10

        ctx.enter_context(nc.allow_non_contiguous_dma(reason="the layernorm's gain and bias, as columns"))
        block = ctx.enter_context(nc.Block())

        slot_sems = SlotSems(sem)
        ph = [NaturalSems(sem), slot_sems, slot_sems, slot_sems]
        f3 = FfnSems(sem)

        def ring(at, n):
            return [area[:, at + D * i:at + D * (i + 1)] for i in range(n)]

        X2 = ring(0, 8)
        YF = ring(8 * D, 8)
        GEL = ring(16 * D, 2)
        HS = ring(18 * D, 2)
        Z = ring(20 * D, 2)
        rawf = raw.rearrange("p a c n -> p (a c n)")
        OUT = [rawf[:, D * i:D * (i + 1)] for i in range(2)]
        FH = [rawf[:, D * (2 + i):D * (3 + i)].bitcast(F16).rearrange("p (a n) -> p a n", a=2) for i in range(2)]
        FT = [rawf[:, D * (4 + i):D * (5 + i)].bitcast(F16).rearrange("p (a c n) -> p a c n", a=2, c=KC)
              for i in range(2)]
        W24 = [sb(f"W24_{i}", [P, 3 * EXPERTS], F16) for i in range(2)]
        WTT = [sb(f"WTT{i}", [3 * EXPERTS, P], F16) for i in range(2)]
        wsc = sb("wsc", [P, 2, 8])
        mv3 = sb("mv3", [P, 2, 2])
        vv = sb("vv", [P, 2, 2])
        rs = sb("rs", [P, 2, 2])
        r2s = sb("r2s", [P, 2])
        zr = sb("zr", [P, 2])
        zv = sb("zv", [P, 2])
        zm = sb("zm", [P, 2, 2])
        st6b = sb("st6b", [P, 6])
        psX = psT[0]
        psH = psT[1]
        psG = psA[1]
        psO = psS[0]
        psW = psS[1][:, :].bitcast(F16)

        def products(eng, acc, lhs, w, stop=True):
            n = 0
            for c in range(KC):
                for a, bpart in ((0, 0), (0, 1), (1, 0)):
                    mm = eng.matmul(acc, lhs[:, a, c, :], w[:, bpart, c, :], start=(n == 0),
                                    stop=(stop and n == 3 * KC - 1))
                    n += 1
            return mm

        @block.sync
        def _(sp):
            sp.wait_ge(s_epad, 3)
            full = (E // EPT) * EPT
            for to, frm, count in ((eDi, dst, E), (eSi, src, E), (eNi, dst[1:E], E - 1)):
                sp.dma_start(to[0:T - 1, :], frm[0:full].rearrange("(t k) -> t k", k=EPT)).then_inc(s_eload, 16)
                sp.dma_start(to[T - 1:T, 0:count - full], frm[full:count].rearrange("(a k) -> a k", a=1)
                             ).then_inc(s_eload, 16)
            sp.wait_ge(s_infoz, 2)
            sp.dma_start(info.rearrange("(p k) two -> p (k two)", p=NP_), zero).then_inc(s_tinit, 16)
            sp.dma_start(table.rearrange("(p k) two -> p k two", p=T), tinit).then_inc(s_tinit, 16)
            sp.dma_start(bcol[:, :], ln_b.rearrange("(c p) -> p c", p=P)).then_inc(s_bload, 16)
            sp.dma_start(gcol[:, :], ln_g.rearrange("(c p) -> p c", p=P)).then_inc(s_bload, 16)
            for l in range(LAYERS):
                sp.dma_start(bias[:, l, :], b[l, :].partition_broadcast(P)).then_inc(s_bload, 16)
            sp.dma_start(b1b[:, :], b1.rearrange("e h -> (e h)").partition_broadcast(P)).then_inc(s_bload, 16)
            sp.dma_start(ogb[:, :], out_g.partition_broadcast(P)).then_inc(s_bload, 16)
            sp.dma_start(obb[:, :], out_b.partition_broadcast(P)).then_inc(s_bload, 16)
            sp.dma_start(wgr[:, :, :], Wg.rearrange("(c p) e -> p c e", p=P)).then_inc(s_bload, 16)
            for i in range(3):
                sp.dma_start(b2r[EXPERTS * i:EXPERTS * (i + 1), :], b2[:, :]).then_inc(s_bload, 16)
            def load_weight(m):
                name = NAMES[m]
                if m >= 2:
                    sp.wait_ge(s_wlo, m - 1)
                    sp.wait_ge(s_whi, m - 1)
                to = raw[:, m % 2, :, :]
                if name == "w1":
                    for c in range(KC):
                        sp.dma_start(to[:, c, :].rearrange("p (e h) -> p e h", e=EXPERTS),
                                     W1[:, c * P:(c + 1) * P, :].rearrange("e p h -> p e h")).then_inc(s_wload[m % 2], 16)
                elif name == "w2":
                    w2f = W2.rearrange("e h d -> (e h) d")
                    for c in range(KC):
                        sp.dma_start(to[:, c, :], w2f[c * P:(c + 1) * P, :]).then_inc(s_wload[m % 2], 16)
                else:
                    w, l = M_OF[name]
                    for c in range(KC):
                        sp.dma_start(to[:, c, :], w[l, c * P:(c + 1) * P, :]).then_inc(s_wload[m % 2], 16)

            load_weight(0)
            load_weight(1)

            s = ph[0]

            def load_x(t):
                after(sp, s.rr, (t + -1).n)
                rows = P if not (isinstance(t.t, int) and t.t == TN - 1) else NLAST
                sp.dma_start(X[t.slot(2)][0:rows, :], x[bass.ds(t.t * P, rows), :]).then_inc(s.x[t.slot(2)], 16)

            def store(t):
                rows = P if not (isinstance(t.t, int) and t.t == TN - 1) else NLAST
                sp.wait_ge(s.yhi, (t + 1).n)
                sp.wait_ge(s.ylo, (t + 1).n)
                sp.dma_start(Yd[0][bass.ds(t.t * P, rows), :], YB[t.slot(2)][0:rows, :]).then_inc(s.ys[t.slot(2)], 16)
                sp.wait_ge(s.sev, (t + 1).n)
                sp.dma_start(Sd0[bass.ds(t.t * P, rows), :], SB[t.slot(2)][0:rows, :]).then_inc(s.s2[t.slot(2)], 16)

            run_plan(sp, 2, TN, [(4, load_x), (0, store)],
                     [(-2, load_weight, 2), (-2, load_weight, 3)]
                     + [(WSTEP(m - 1) + 1, load_weight, m) for m in range(4, len(NAMES))])
            for l in (1, 2):
                s = ph[l]
                q = ph[l - 1]
                if l == 2:
                    for i in range(2):
                        sp.wait_ge(q.s2[i], 16 * ((T + 1 - i) // 2))

                def load_self(t, s=s, l=l):
                    after(sp, s.r, (t + -1).n)
                    sp.dma_start(Sl[t.slot(2)][:, :], Sd[l - 1][bass.ds(t.t * P, P), :]).then_inc(s.xs[t.slot(2)], 16)

                def store_self(t, s=s, l=l):
                    sp.wait_ge(s.sev, (t + 1).n)
                    sp.dma_start(Sd[l][bass.ds(t.t * P, P), :], SB[t.slot(2)][:, :]).then_inc(s.s2[t.slot(2)], 16)

                if l == 1:
                    run_tiles(sp, 4, T, [(0, store_self)])
                else:
                    run_tiles(sp, 4, T, [(0, store_self), (5, load_self)], 1)
            s = ph[3]
            for i in range(2):
                sp.wait_ge(ph[2].s2[i], 2 * 16 * ((T + 1 - i) // 2))

            def load_self3(t):
                after(sp, s.r, (t + -1).n)
                sp.dma_start(Sl[t.slot(2)][:, :], Sd[2][bass.ds(t.t * P, P), :]).then_inc(s.xs[t.slot(2)], 16)

            run_tiles(sp, 8, T, [(6, load_self3)], 2)

        @block.gpsimd
        def _(pool):
            node_limit = pool.alloc_register("node_limit")
            slot_limit = pool.alloc_register("slot_limit")
            pool.reg_mov(node_limit, N - 1)
            pool.reg_mov(slot_limit, SLOTS - 1)
            n = [0]

            def link(ins):
                n[0] += 1
                ins.then_inc(s_pl, 1)
                pool.wait_ge(s_pl, n[0])

            pool.memset(ones[:, :], 1.0).then_inc(s_const, 1)
            link(pool.memset(iden[:, :], 0.0))
            link(pool.affine_select(out=iden[:, :], in_=iden[:, :], compare_op=ALU.not_equal, fill=1.0, base=0,
                                    pattern=[[-1, P]], channel_multiplier=1))
            link(pool.memset(upper[:, :], 1.0))
            link(pool.affine_select(out=upper[:, :], in_=upper[:, :], compare_op=ALU.is_gt, fill=0.0, base=0,
                                    pattern=[[1, P]], channel_multiplier=-1))
            link(pool.iota(iota_i[:, 0:P], [[1, P]], base=0, channel_multiplier=0))
            link(pool.iota(iota_i[:, P:2 * P], [[EPT, P]], base=0, channel_multiplier=0))
            link(pool.iota(iota_i[:, 2 * P:2 * P + EPT], [[1, EPT]], base=1, channel_multiplier=EPT))
            link(pool.iota(iota_i[:, 3 * P - 1:3 * P], [[1, 1]], base=0, channel_multiplier=P))
            link(pool.iota(node_no_i[:, :], [[1, NF]], base=0, channel_multiplier=NF))
            link(pool.memset(rowval[:, :], 1.0))
            link(pool.memset(rowval[0:1, :], CARRY))
            link(pool.memset(halfpow[:, 0:1], 0.5))
            link(pool.memset(halfpow[:, 1:2], -0.5))
            link(pool.memset(mhalf2[:, :], -0.5))
            link(pool.memset(rowmask[:, :], 1.0))
            pool.memset(rowmask[0:1, :], 1.0).then_inc(s_const, 1)
            def columns(index, value, to, limit, rows, i, at, count, copied):
                pool.tensor_copy(cpI[i][0:rows, 0:count], index[0:rows, bass.ds(at, count)]).then_inc(s_scat_cp, 1)
                pool.tensor_copy(cpV[i][0:rows, 0:count, :], value[0:rows, bass.ds(at, count), :]
                                 ).then_inc(s_scat_cp, 1)
                hold(pool, s_const, (s_scat_cp, copied))
                for k in range(count):
                    pool.indirect_dma_start(
                        to[:, :], bass.IndirectOffsetOnAxis(ap=cpI[i][0:rows, k:k + 1], axis=0),
                        cpV[i][0:rows, k, :], None, bounds_check=limit, oob_is_err=False).then_inc(s_sc[i], 16)

            def largest_norm(m):
                pool.wait_ge(s_cmax, m + 1)
                pool.tensor_tensor(nrm[:, m:m + 1], cmax[:, m:m + 1], halfpow[:, 0:1], ALU.pow).then_inc(s_nrm, 1)

            pool.wait_ge(s_tinit, 32)
            pool.wait_ge(s_scat_in, 1)
            for g in range(2):
                columns(dstT, infoT, info, node_limit, P, g % 2, 8 * g, 8, 2 * (g + 1))
                largest_norm(g)

            s = ph[0]

            def dev0(t):
                pool.wait_ge(s.ss, (t + 1).n)
                after(pool, s.rr, (t + -1).n)
                pool.tensor_tensor(scl[:, t.slot(2):t.slot(2) + 1], ssm[:, t.slot(2):t.slot(2) + 1],
                                   halfpow[:, 1:2], ALU.pow).then_inc(s.sc, 1)

            def info_columns(t):
                i = t.slot(2)
                pool.wait_ge(s_sc[i], (t + -2).landed(2) * 4 + 128)
                columns(dstT, infoT, info, node_limit, P, i, t.t * 4 + 16, 4, t.t * 2 + 6)

            def info_done():
                for i in range(2):
                    pool.wait_ge(s_sc[i], 640)
                pool.dma_start(nI, info.rearrange("(p k) two -> p k two", p=NP_)).then_inc(s_nload, 16)

            def slot_columns(t):
                g = t + -STEP_SCATTER
                i = t.slot(2)
                pool.wait_ge(s_sc[i], (g + -2).landed(2) * 4 + 640)
                columns(slotT, ndT, table, slot_limit, NF, i, g.t * 4, 4, g.t * 2 + 38)

            def slot_columns_in():
                pool.wait_ge(s_scat_in, 2)

            def slot_columns_done():
                for i in range(2):
                    pool.wait_ge(s_sc[i], 1280)
                pool.dma_start(tI, table.rearrange("(p k) two -> p k two", p=T)).then_inc(s_tload, 16)

            run_plan(pool, 2, TN, [(3, dev0)],
                     [(WSTEP(m) + 2, largest_norm, m) for m in range(N_FIRST, len(NAMES))]
                     + [(STEP_GATE + 2, largest_norm, CG), (STEP_INFO, info_done, None),
                        (STEP_SCATTER, slot_columns_in, None), (STEP_SCATTER + 20, slot_columns_done, None)],
                     [(0, STEP_INFO, info_columns), (STEP_SCATTER, STEP_SCATTER + 20, slot_columns)])
            pool.wait_ge(s_tables, 1)

            for l in (1, 2, 3):
                s = ph[l]
                U = 4
                last = ph[l - 1]
                tiles = TN if l == 1 else T
                for i in range(2):
                    pool.wait_ge(last.ys[i], (2 if l == 3 else 1) * 16 * ((tiles + 1 - i) // 2))
                    if l == 1:
                        pool.wait_ge(last.s2[i], 16 * ((tiles + 1 - i) // 2))

                def gather(t, s=s, l=l):
                    i = t.slot(GRING)
                    after(pool, s.agg, (t + (1 - GRING)).n)
                    pool.tensor_copy(idx[0][i][:, :], srcT[:, bass.ds(t.t, 1)]).then_inc(s.idx, 1)
                    hold(pool, s_const, (s.idx, (t + 1).n))
                    pool.indirect_dma_start(G[i][:, :], None, Yd[l - 1][:, :],
                                            bass.IndirectOffsetOnAxis(ap=idx[0][i][:, 0:1], axis=0),
                                            bounds_check=node_limit, oob_is_err=False).then_inc(s.g[i], 16)

                def by_node(t, s=s, l=l):
                    i = t.slot(2)
                    own = t.own
                    if l == 1:
                        after(pool, s.r, (t + -1).n)
                    else:
                        after(pool, f3.x2, (own + -1).n)
                    done = s.idx_in1 if l == 1 else s.idx_in3
                    pool.tensor_copy(idx[1][i][:, :], pinT[:, bass.ds(t.t, 1)]).then_inc(done, 1)
                    to, frm = (Sl[i], Sd0) if l == 1 else (X[i], x)
                    hold(pool, s_const, (done, (own + 1).n))
                    pool.indirect_dma_start(to[:, :], None, frm[:, :],
                                            bass.IndirectOffsetOnAxis(ap=idx[1][i][:, 0:1], axis=0),
                                            bounds_check=node_limit, oob_is_err=False
                                            ).then_inc((s.x if l == 1 else s.xg)[i], 16)

                def norm(t, s=s, l=l):
                    i = t.slot(2)
                    pool.wait_ge(s.ss, (t + 1).n)
                    if l < 3:
                        after(pool, s.hlo, (t + -1).n)
                    else:
                        after(pool, f3.x2, (t.own + -1).n)
                    pool.tensor_tensor(scl[:, i:i + 1], ssm[:, i:i + 1], halfpow[:, 1:2], ALU.pow).then_inc(s.sc, 1)

                def put_y(t, s=s, l=l):
                    i = t.slot(2)
                    if not (isinstance(t.t, int) and t.t < 2):
                        pool.wait_ge(s.ys[i], (t + -2).landed(2))
                    pool.tensor_copy(idx[2][i][:, :], poutT[:, bass.ds(t.t, 1)]).then_inc(s.idx_out, 1)
                    hold(pool, s_const, (s.idx_out, (t + 1).n), (s.yhi, (t + 1).n), (s.ylo, (t + 1).n))
                    pool.indirect_dma_start(Yd[l][:, :], bass.IndirectOffsetOnAxis(ap=idx[2][i][:, 0:1], axis=0),
                                            YB[i][:, :], None, bounds_check=node_limit, oob_is_err=False
                                            ).then_inc(s.ys[i], 16)

                if l < 3:
                    st = [(6, gather), (0, put_y), (3, norm)]
                    if l == 1:
                        st.append((5, by_node))
                    run_tiles(pool, U, T, st, l - 1)
            s = ph[3]

            def rs_of(t):
                t = t.own
                i = t.slot(2)
                pool.wait_ge(f3.v2, (t + 1).n)
                after(pool, f3.y, (t + -1).n)
                after(pool, f3.r2s, (t + -1).n)
                pool.tensor_tensor(rs[:, i, :], vv[:, i, :], mhalf2[:, :], ALU.pow).then_inc(f3.rs, 1)
                hold(pool, s_const, (f3.rs, (t + 1).n))
                pool.tensor_scalar(nmr[:, i:i + 1], mv3[:, i, 0:1], rs[:, i, 0:1], -1.0, ALU.mult, ALU.mult
                                   ).then_inc(f3.nmr, 1)

            def xob(t):
                t = t.own
                pool.wait_ge(f3.y, (t + 1).n)
                pool.tensor_tensor(X2[t.slot(8)], X2[t.slot(8)], obb[:, :], ALU.add).then_inc(f3.xob, 1)

            def hs_of(t):
                t = t.own
                pool.wait_ge(f3.gel, (t + 1).n)
                pool.wait_ge(f3.w, (t + 1).n)
                after(pool, f3.hlo, (t + -1).n)
                i = t.slot(2)
                pool.tensor_tensor(HS[i].rearrange("p (e h) -> p e h", e=EXPERTS),
                                   GEL[i].rearrange("p (e h) -> p e h", e=EXPERTS),
                                   wv[:, i, :].unsqueeze(2).to_broadcast([P, EXPERTS, HIDDEN]), ALU.mult
                                   ).then_inc(f3.hs, 1)

            def zr_of(t):
                t = t.own
                i = t.slot(2)
                hold(pool, s_const, (f3.aggz, (t + 1).n), (f3.o, (t + -1).n))
                pool.tensor_scalar(zv[:, i:i + 1], zm[:, i, 1:2], LN_EPS, None, ALU.add).then_inc(f3.zv, 1)
                pool.wait_ge(f3.zv, (t + 1).n)
                pool.tensor_tensor(zr[:, i:i + 1], zv[:, i:i + 1], halfpow[:, 1:2], ALU.pow).then_inc(f3.zr, 1)

            def put_out(t):
                t = t.own
                i = t.slot(2)
                if not (isinstance(t.t, int) and t.t < 2):
                    pool.wait_ge(f3.out[i], (t + -2).landed(2))
                pool.tensor_copy(idx[2][i][:, :], poutT[:, bass.ds(t.t, 1)]).then_inc(f3.idx, 1)
                hold(pool, s_const, (f3.idx, (t + 1).n), (f3.o, (t + 1).n))
                pool.indirect_dma_start(out[:, :], bass.IndirectOffsetOnAxis(ap=idx[2][i][:, 0:1], axis=0),
                                        OUT[i], None, bounds_check=node_limit, oob_is_err=False
                                        ).then_inc(f3.out[i], 16)

            run_tiles(pool, 8, T, [(3, rs_of), (4, norm), (-4, zr_of), (-1, hs_of), (-5, put_out), (7, gather),
                                   (5, by_node), (1, xob)], 2)
            for i in range(2):
                pool.wait_ge(f3.out[i], 16 * ((T + 1 - i) // 2))

        @block.scalar
        def _(act):
            act.wait_ge(s_bload, 16 * 12)

            def squares(m):
                name = NAMES[m]
                act.wait_ge(s_wload[m % 2], 64 * (m // 2 + 1))
                if name == "w1":
                    act.wait_ge(s_wgain, 1)
                after(act, s_cn, m)
                act.activation(sqw, raw[:, m % 2, :, :], ACT.Square).then_inc(s_sq, 1)
                if name == "w2":
                    act.activation(sqb2[:, :], b2r[0:EXPERTS, :], ACT.Square).then_inc(s_sqb, 1)

            def weight_hi(m):
                act.wait_ge(s_scale, m + 1)
                act.activation(WT[NAMES[m]][:, 0, :, :], raw[:, m % 2, :, :], ACT.Copy, scale=ups[:, m:m + 1]
                               ).then_inc(s_whi, 1)

            def gate_squares():
                act.wait_ge(s_wgain, 2)
                act.wait_ge(s_cn, 8)
                act.activation(sqw[:, 0, 0:KC * EXPERTS].rearrange("p (c e) -> p c e", c=KC), wgs[:, :, :], ACT.Square
                               ).then_inc(s_sq, 1)

            for m in range(N_FIRST):
                squares(m)
                weight_hi(m)

            s = ph[0]

            def hi0(t):
                i = t.slot(2)
                act.wait_ge(s.rr, (t + 1).n)
                after(act, s.tr, (t + -1).n)
                act.activation(HH[i][:, 0, :], R[i][:, :], ACT.Copy, scale=LN_UP).then_inc(s.hhi, 1)

            def yhi(t, l):
                i = t.slot(2)
                s = ph[l]
                act.wait_ge(s.y, (t + 1).n)
                if not (isinstance(t.t, int) and t.t < 2):
                    act.wait_ge(s.ys[i], (t + -2).landed(2))
                k = Y_LN / (WUP * LN_UP) if l == 0 else Y_H / (WUP * H_UP)
                act.activation(YB[i][:, 0:D], psY[i][:, :], ACT.Copy, scale=k).then_inc(s.yhi, 1)

            rest = range(N_FIRST, len(NAMES))
            run_plan(act, 2, TN, [(2, hi0), (0, lambda t: yhi(t, 0))],
                     [(WSTEP(m), squares, m) for m in rest] + [(WSTEP(m) + 3, weight_hi, m) for m in rest]
                     + [(STEP_GATE, gate_squares, None)])

            def carry_hi(t, l):
                s = ph[l]
                i, nxt = t.slot(2), t + 1
                if isinstance(t.t, int) and t.t == T - 1:
                    return
                act.wait_ge(s.agg, (t + 1).n)
                o = nxt.slot(GRING)
                act.wait_ge(s.g[o], nxt.landed(GRING))
                act.activation(G[o][0:1, 0:D], psA[0 if l == 3 else i][0:1, :], ACT.Copy, scale=1.0 / CARRY
                               ).then_inc(s.chi, 1)

            def relu(t, l):
                s = ph[l]
                i = t.slot(2)
                act.wait_ge(s.r, (t + 1).n)
                if l < 3:
                    after(act, s.hlo, (t + -1).n)
                else:
                    after(act, f3.x2, (t.own + -1).n)
                act.activation(RR[i][:, :], R[i][:, :], ACT.Relu).then_inc(s.rr, 1)

            def hhi(t, l):
                s = ph[l]
                i = t.slot(2)
                act.wait_ge(s.sc, (t + 1).n)
                act.wait_ge(s.rr, (t + 1).n)
                after(act, s.tr, (t + -1).n)
                act.activation(HH[i][:, 0, :], RR[i][:, :], ACT.Copy, scale=scl[:, i:i + 1]).then_inc(s.hhi, 1)

            def first_carry(l):
                act.wait_ge(ph[l].g[0], Tile(GRING, 0, 0, l - 1).landed(GRING))
                act.activation(G[0][0:1, :], G[0][0:1, :], ACT.Copy, scale=0.0).then_inc(ph[l].c0, 1)

            for l in (1, 2):
                first_carry(l)
                run_tiles(act, 4, T, [(2, lambda t, l=l: hhi(t, l)), (0, lambda t, l=l: yhi(t, l)),
                                      (3, lambda t, l=l: carry_hi(t, l)), (3, lambda t, l=l: relu(t, l))], l - 1)
            first_carry(3)

            def distances(t):
                after(act, ph[3].smat, t.n)
                act.activation(dist[:, :], iota_row[:, :], ACT.Square, bias=minus_colT[:, bass.ds(t.t, 1)]
                               ).then_inc(f3.dist, 1)

            def one_hot(t):
                act.wait_ge(f3.dist, t.own.t + 1)
                i = t.slot(GRING)
                after(act, ph[3].agg, (t + (1 - GRING)).n)
                act.activation(Sm[i][:, :], dist[:, :], ACT.Relu, bias=rowval[:, 0:1], scale=minus_rowval[:, 0:1]
                               ).then_inc(ph[3].smat, 1)

            def carry_rest_in(t):
                if isinstance(t.t, int) and t.t == T - 1:
                    return
                o = (t + 1).slot(GRING)
                act.wait_ge(f3.rest, (t.own + 1).n)
                act.activation(G[o][0:1, D:2 * D], psA[0][0:1, :], ACT.Copy, scale=1.0 / CARRY
                               ).then_inc(ph[3].clo, 1)

            def yf(t):
                t = t.own
                i, q = t.slot(2), t.slot(8)
                act.wait_ge(f3.nmr, (t + 1).n)
                after(act, f3.z, (t + -7).n)
                act.activation(YF[q], X2[q], ACT.Identity, bias=nmr[:, i:i + 1], scale=rs[:, i, 0:1]).then_inc(f3.y, 1)

            def inner_factor(t):
                t = t.own
                i = t.slot(2)
                act.wait_ge(f3.rs, (t + 1).n)
                after(act, f3.xlo, (t + -1).n)
                act.activation(r2s[:, i:i + 1], rs[:, i, 1:2], ACT.Copy, scale=LN_UP).then_inc(f3.r2s, 1)

            def xhi(t):
                t = t.own
                i = t.slot(2)
                act.wait_ge(f3.y, (t + 1).n)
                act.wait_ge(f3.r2s, (t + 1).n)
                after(act, f3.tx, (t + -1).n)
                act.activation(HH[i][:, 0, :], YF[t.slot(8)], ACT.Copy, scale=r2s[:, i:i + 1]).then_inc(f3.xhi, 1)

            def txc(t):
                t = t.own
                i = t.slot(2)
                act.wait_ge(f3.tx, (t + 1).n)
                after(act, f3.pre, (t + -1).n)
                act.activation(HT[i][:, :, :, :], psX[:, :, :, :], ACT.Copy).then_inc(f3.txc, 1)

            def gelu(t):
                t = t.own
                i = t.slot(2)
                act.wait_ge(f3.pre, (t + 1).n)
                after(act, f3.hs, (t + -1).n)
                c = C["w1"]
                act.activation(GEL[i], psY[i][:, :], ACT.Gelu_apprx_tanh, scale=downs[:, c:c + 1]).then_inc(f3.gel, 1)

            def gate(t):
                t = t.own
                i = t.slot(2)
                act.wait_ge(f3.lg, (t + 1).n)
                after(act, f3.w, (t + -1).n)
                act.activation(gv[:, i, 9:10], gv[:, i, 8:9], ACT.Tanh, scale=0.5).then_inc(f3.th, 1)

            def fhi(t):
                t = t.own
                i = t.slot(2)
                act.wait_ge(f3.hs, (t + 1).n)
                after(act, f3.th2, (t + -1).n)
                act.activation(FH[i][:, 0, :], HS[i], ACT.Copy, scale=ups[:, CB:CB + 1]).then_inc(f3.hhi, 1)

            def thc(t):
                t = t.own
                i = t.slot(2)
                act.wait_ge(f3.th2, (t + 1).n)
                after(act, f3.cmb, (t + -1).n)
                act.activation(WTT[i][:, :], psW[0:24, 0:P], ACT.Copy).then_inc(f3.wtt, 1)
                act.activation(FT[i], psH[:, :, :, :], ACT.Copy).then_inc(f3.thc, 1)

            run_tiles(act, 8, T, [(0, txc), (6, distances), (4, lambda t: carry_hi(t, 3)), (6, one_hot), (-1, gelu),
                                  (-1, gate),
                                  (4, lambda t: relu(t, 3)), (-2, fhi), (2, inner_factor), (2, yf), (2, xhi), (-3, thc),
                                  (4, carry_rest_in)], 2)

        @block.vector
        def _(dve):
            n = [0]

            def link(ins):
                n[0] += 1
                ins.then_inc(s_dv, 1)
                dve.wait_ge(s_dv, n[0])

            dve.memset(eDi, -1).then_inc(s_epad, 1)
            dve.memset(eNi, -1).then_inc(s_epad, 1)
            dve.memset(eSi, 0).then_inc(s_epad, 1)
            dve.memset(zero, 0.0).then_inc(s_infoz, 1)
            link(dve.memset(tinit[:, :, 0:1], BIG))
            dve.memset(tinit[:, :, 1:2], 1.0).then_inc(s_infoz, 1)
            dve.wait_ge(s_const, 2)
            link(dve.tensor_copy(iden16[:, :], iden[:, :]))
            link(dve.tensor_copy(iota_row[:, :], iota_i[:, 0:P]))
            link(dve.tensor_copy(iota16[:, :], iota_i[:, 0:P]))
            link(dve.tensor_scalar(minus_rowval[:, :], rowval[:, :], -1.0, None, ALU.mult))
            link(dve.tensor_copy(ones16[:, :], ones[:, :]))
            link(dve.tensor_copy(iota127[:, :], iota_i[:, P:2 * P]))
            link(dve.tensor_copy(edge_no[:, :], iota_i[:, 2 * P:2 * P + EPT]))
            link(dve.tensor_copy(tile128[:, :], iota_i[:, 3 * P - 1:3 * P]))
            link(dve.tensor_copy(node_no[:, :], node_no_i[:, :]))
            link(dve.tensor_reduce(small[0:24, 0:1], iden[0:24, 8:16], AX.X, ALU.add))
            dve.tensor_scalar(rowmask[:, :], small[0:24, 0:1], -1.0, 1.0, ALU.mult, ALU.add).then_inc(s_constv, 1)

            def scales(c, k):
                dve.wait_ge(s_nrm, k)
                if c == C["w1"]:
                    link(dve.tensor_reduce(small[:, 2:3], b1b[:, :], AX.X, ALU.max, apply_absolute_value=True))
                    link(dve.tensor_scalar(nrm[:, c:c + 1], small[:, 2:3], 1.0 / 32, nrm[:, c:c + 1], ALU.mult, ALU.max))
                bits = nrm[:, c:c + 1].bitcast(U32)
                link(dve.tensor_scalar(expo[:, :], bits, 0x7F800000, None, ALU.bitwise_and))
                link(dve.tensor_scalar(downs[:, c:c + 1], expo[:, :].bitcast(F32), 0.5 / WUP, None, ALU.mult))
                link(dve.tensor_scalar(ups[:, c:c + 1].bitcast(U32), expo[:, :], 0x7F800000, None, ALU.bitwise_xor))
                return dve.tensor_scalar(ups[:, c:c + 1], ups[:, c:c + 1], WUP, None, ALU.mult)

            dve.wait_ge(s_eload, 96)
            r1 = slice(0, EPT)
            link(dve.tensor_copy(eD[:, r1], eDi))
            link(dve.tensor_copy(eN[:, r1], eNi))
            link(dve.tensor_copy(eSRC[:, 1:P], eSi))
            link(dve.memset(eSRC[:, 0:1], 0.0))
            link(dve.tensor_tensor(eL[:, r1], eD[:, r1], eN[:, r1], ALU.not_equal))
            link(dve.tensor_tensor_scan(eCS[:, r1], ones[0:T, r1], eL[:, r1], 0.0, ALU.mult, ALU.add))
            link(dve.tensor_copy(stot, eCS[:, EPT - 1:EPT]))
            link(dve.tensor_tensor(eEX[:, r1], eCS[:, r1], eL[:, r1], ALU.subtract))
            link(dve.tensor_scalar(eT1[:, r1], eEX[:, r1], stot, None, ALU.is_lt))
            link(dve.scalar_tensor_tensor(eCOL[:, 1:P], eEX[:, r1], 1.0, eT1[:, r1], ALU.add, ALU.mult))
            link(dve.tensor_copy(eCOL[:, 0:1], eCOL[:, 1:2]))
            link(dve.tensor_tensor(eM[:, r1], eL[:, r1], edge_no[0:T, :], ALU.mult))
            link(dve.memset(eSC[:, 0:1], 0.0))
            link(dve.tensor_tensor_scan(eSC[:, 1:P], eM[:, r1], eM[:, r1], 0.0, ALU.max, ALU.max))
            dve.tensor_copy(pm_col[:, 0:1], eSC[:, P - 1:P]).then_inc(s_tab, 1)
            dve.wait_ge(s_tabp, 1)
            link(dve.tensor_copy(eT1[0:1, 0:T], psA[1][0:1, 0:T]))
            link(dve.memset(pm_row[0:1, 0:1], 0.0))
            dve.tensor_tensor_scan(pm_row[0:1, 1:T + 1], eT1[0:1, 0:T], eT1[0:1, 0:T], 0.0, ALU.max, ALU.max
                                   ).then_inc(s_tab, 1)
            dve.wait_ge(s_tabp, 2)
            link(dve.tensor_copy(pm_col[:, 1:2], psA[1][0:T, 0:1]))
            link(dve.tensor_scalar(eT1[:, r1], eSC[:, 0:EPT], pm_col[:, 1:2], None, ALU.max))
            link(dve.tensor_tensor(eDEG[:, 1:P], edge_no[0:T, :], eT1[:, r1], ALU.subtract))
            link(dve.memset(eDEG[:, 0:1], 1.0))
            link(dve.tensor_scalar(eSLOT[:, :], eCOL[:, :], tile128[0:T, 0:1], None, ALU.add))
            link(dve.scalar_tensor_tensor(eDST[:, 1:P], eD[:, r1], -BIG, eL[:, r1], ALU.add, ALU.mult))
            link(dve.memset(eDST[:, 0:1], 0.0))
            dve.tensor_scalar(eDST[:, :], eDST[:, :], BIG, None, ALU.add).then_inc(s_tab, 1)
            dve.wait_ge(s_tabp, 3)
            link(dve.memset(dstT[:, 79:80].bitcast(I32), int(BIG)))
            link(dve.memset(infoT[:, 79:80, :], 0.0))
            link(dve.tensor_copy(colT[:, :], psA[1][:, 0:T]))
            link(dve.tensor_scalar(minus_colT[:, :], psA[1][:, 0:T], -1.0, None, ALU.mult))
            link(dve.tensor_copy(infoT[:, 0:T, 0], psA[1][:, T:2 * T]))
            link(dve.tensor_copy(infoT[:, 0:T, 1], psA[1][:, 2 * T:3 * T]))
            link(dve.tensor_copy(dstT[:, 0:T], psA[1][:, 3 * T:4 * T]))
            dve.tensor_copy(srcT[:, :], psA[1][:, 4 * T:5 * T]).then_inc(s_scat_in, 1)

            dve.wait_ge(s_bload, 16 * 12)
            for c in range(KC):
                link(dve.tensor_scalar(bmat[:, c, :], ones[:, :], bcol[:, c:c + 1], None, ALU.mult))
            dve.tensor_scalar(small[:, 0:1], ones[:, 0:1], 1.0, None, ALU.mult).then_inc(s_bm, 1)
            def weight_norm(m):
                dve.wait_ge(s_cn, m + 1)
                link(dve.tensor_reduce(cmax[:, m:m + 1], psA[0][:, :], AX.X, ALU.max))
                dve.tensor_scalar(cmax[:, m:m + 1], cmax[:, m:m + 1], 1e-30, None, ALU.max).then_inc(s_cmax, 1)

            def weight_scale(m):
                scales(m, m + 1).then_inc(s_scale, 1)

            def weight_lo(m):
                dve.wait_ge(s_scale, m + 1)
                dve.wait_ge(s_whi, m + 1)
                parts = WT[NAMES[m]]
                dve.scalar_tensor_tensor(parts[:, 1, :, :].rearrange("p c n -> p (c n)"),
                                         raw[:, m % 2, :, :].rearrange("p c n -> p (c n)"), ups[:, m:m + 1],
                                         parts[:, 0, :, :].rearrange("p c n -> p (c n)"),
                                         ALU.mult, ALU.subtract).then_inc(s_wlo, 1)

            def gain():
                m = C["w1"]
                w = raw[:, m % 2, :, :]
                dve.wait_ge(s_wload[m % 2], 64 * (m // 2 + 1))
                dve.wait_ge(s_ffb, 2)
                link(dve.tensor_tensor(b1b[:, :], psA[1][:, :], b1b[:, :], ALU.add))
                link(dve.tensor_copy(bgb[:, :], psA[0][:, 0:EXPERTS]))
                for c in range(KC):
                    link(dve.tensor_scalar(w[:, c, :], w[:, c, :], gcol[:, c:c + 1], None, ALU.mult))
                dve.tensor_scalar(small[:, 0:1], ones[:, 0:1], 1.0, None, ALU.mult).then_inc(s_wgain, 1)

            def gate_gain():
                for c in range(KC):
                    link(dve.tensor_scalar(wgs[:, c, :], wgr[:, c, :], gcol[:, c:c + 1], None, ALU.mult))
                dve.tensor_scalar(small[:, 0:1], ones[:, 0:1], 1.0, None, ALU.mult).then_inc(s_wgain, 1)

            def gate_norm():
                dve.wait_ge(s_cn, 9)
                link(dve.tensor_reduce(cmax[:, CG:CG + 1], psA[0][:, 0:EXPERTS], AX.X, ALU.max))
                dve.tensor_scalar(cmax[:, CG:CG + 1], cmax[:, CG:CG + 1], 1e-30, None, ALU.max).then_inc(s_cmax, 1)

            def gate_parts():
                link(scales(CG, 9))
                link(dve.tensor_scalar(wg16[:, :, 0:EXPERTS], wgs[:, :, :], ups[:, CG:CG + 1], None, ALU.mult))
                link(dve.scalar_tensor_tensor(wg16[:, :, EXPERTS:2 * EXPERTS], wgs[:, :, :], ups[:, CG:CG + 1],
                                              wg16[:, :, 0:EXPERTS], ALU.mult, ALU.subtract))
                c1 = C["w1"]
                link(dve.tensor_scalar(small[:, 3:4], nrm[:, c1:c1 + 1], ROOT_D, small[:, 2:3], ALU.mult, ALU.add))
                link(dve.tensor_scalar(small[:, 3:4], small[:, 3:4], 1.0, None, ALU.max))
                link(dve.tensor_scalar(expo[:, :], small[:, 3:4].bitcast(U32), 0x7F800000, None, ALU.bitwise_and))
                link(dve.tensor_scalar(downs[:, CB:CB + 1], expo[:, :].bitcast(F32), 0.5 / FF_UP, None, ALU.mult))
                link(dve.tensor_scalar(ups[:, CB:CB + 1].bitcast(U32), expo[:, :], 0x7F800000, None, ALU.bitwise_xor))
                link(dve.tensor_scalar(ups[:, CB:CB + 1], ups[:, CB:CB + 1], FF_UP, None, ALU.mult))

            def bias1_parts():
                c1 = C["w1"]
                link(dve.memset(minus[:, :], 0.0))
                link(dve.memset(minus[0:1, 0:1], -CARRY))
                link(dve.memset(c2row[:, :], CARRY))
                link(dve.tensor_scalar(sq[0:2, 0, :], b1b[0:2, :], ups[0:2, c1:c1 + 1], LN_UP / CARRY, ALU.mult, ALU.mult))
                link(dve.tensor_copy(b1h, sq[0:2, 0, :]))
                link(dve.tensor_tensor(sq[0:2, 1, :], sq[0:2, 0, :], b1h, ALU.subtract))
                link(dve.tensor_scalar(sq[0:2, 2, :], b1h, iden[0:2, 0:1], None, ALU.mult))
                link(dve.scalar_tensor_tensor(b1s[:, :], sq[0:2, 1, :], iden[0:2, 1:2], sq[0:2, 2, :], ALU.mult, ALU.add))

            def last_scales():
                c1, c2 = C["w1"], C["w2"]
                link(dve.tensor_scalar(downs[:, FINAL:FINAL + 1], downs[:, CB:CB + 1], downs[:, c2:c2 + 1], None, ALU.mult))
                link(dve.tensor_scalar(ups[:, CB:CB + 1], ups[:, CB:CB + 1], 0.5, None, ALU.mult))
                for c in (CG, c1):
                    link(dve.tensor_scalar(downs[:, c:c + 1], downs[:, c:c + 1], 1.0 / LN_UP, None, ALU.mult))
                for name in ("s1", "s2"):
                    c = C[name]
                    link(dve.tensor_scalar(downs[:, c:c + 1], downs[:, c:c + 1], 1.0 / H_UP, None, ALU.mult))

            def bias2_parts():
                c2 = C["w2"]
                link(dve.tensor_scalar(b2h, b2r[:, :], ups[0:24, c2:c2 + 1], None, ALU.mult))
                lo24 = sq[0:24, 1, :]
                hi24 = sq[0:24, 2, :]
                link(dve.scalar_tensor_tensor(lo24, b2r[:, :], ups[0:24, c2:c2 + 1], b2h, ALU.mult, ALU.subtract))
                link(dve.tensor_scalar(hi24, b2h, rowmask[:, 0:1], None, ALU.mult))
                link(dve.tensor_scalar(small[0:24, 4:5], rowmask[:, 0:1], -1.0, 1.0, ALU.mult, ALU.add))
                link(dve.scalar_tensor_tensor(b2s[:, :], lo24, small[0:24, 4:5], hi24, ALU.mult, ALU.add))


            for m in range(N_FIRST):
                weight_norm(m)
                weight_scale(m)
                weight_lo(m)
            c = C["s0"]
            link(dve.tensor_scalar(downs[:, c:c + 1], downs[:, c:c + 1], 1.0 / LN_UP, None, ALU.mult))

            s = ph[0]

            def stats0(t):
                i = t.slot(2)
                dve.wait_ge(s.x[i], t.landed(2))
                after(dve, s.rr, (t + -1).n)
                dve.bn_stats(st6[:, :], X[i][:, :]).then_inc(s.r, 1)
                hold(dve, s_const, (s.r, (t + 1).n))
                dve.bn_aggr(mv[:, i, :], st6[:, :]).then_inc(s.dv, 1)
                dve.wait_ge(s.dv, (t + 1).n)
                after(dve, s.sc, (t + -1).n)
                dve.tensor_scalar(ssm[:, i:i + 1], mv[:, i, 1:2], LN_EPS, None, ALU.add).then_inc(s.ss, 1)

            def norm0(t):
                i = t.slot(2)
                dve.wait_ge(s.sc, (t + 1).n)
                after(dve, s.hhi, (t + -1).n)
                after(dve, s.hlo, (t + -1).n)
                dve.tensor_scalar(R[i][:, :], X[i][:, :], mv[:, i, 0:1], scl[:, i:i + 1], ALU.subtract, ALU.mult
                                  ).then_inc(s.rr, 1)
                dve.wait_ge(s.hhi, (t + 1).n)
                dve.wait_ge(s.rr, (t + 1).n)
                dve.scalar_tensor_tensor(HH[i][:, 1, :], R[i][:, :], LN_UP, HH[i][:, 0, :], ALU.mult, ALU.subtract
                                         ).then_inc(s.hlo, 1)

            def turn(t, l):
                s = ph[l]
                i = t.slot(2)
                dve.wait_ge(s.tr, (t + 1).n)
                after(dve, s.sp, (t + -1).n)
                dve.tensor_copy(HT[i][:, :, :, :], psT[i][:, :, :, :]).then_inc(s.ht, 1)

            def ylo(t, l):
                s = ph[l]
                i = t.slot(2)
                dve.wait_ge(s.yhi, (t + 1).n)
                k = Y_LN / (WUP * LN_UP) if l == 0 else Y_H / (WUP * H_UP)
                dve.scalar_tensor_tensor(YB[i][:, D:2 * D], psY[i][:, :], k, YB[i][:, 0:D], ALU.mult, ALU.subtract
                                         ).then_inc(s.ylo, 1)

            def sev(t, l):
                s = ph[l]
                i = t.slot(2)
                dve.wait_ge(s.sp, (t + 1).n)
                if not (isinstance(t.t, int) and t.t < 2):
                    dve.wait_ge(s.s2[i], (t + -2).landed(2))
                c = C[f"s{l}"]
                dve.scalar_tensor_tensor(SB[i][:, :], psS[i][:, :], downs[:, c:c + 1], bias[:, l, :],
                                         ALU.mult, ALU.add).then_inc(s.sev, 1)

            def unplaced_nodes():
                link(dve.tensor_scalar(smat, ones[0:T, 0:NP_], stot, None, ALU.mult))
                link(dve.tensor_copy(iu[:, 0:T], iden[0:T, 0:T]))
                link(dve.tensor_copy(iu[:, T:2 * T], upper[0:T, 0:T]))
                dve.wait_ge(s_nload, 16)
                link(dve.tensor_scalar(nZ, nI[:, :, 0], 0.0, None, ALU.is_equal))
                link(dve.tensor_tensor_scan(nCZ, ones[0:NP_, 0:NF], nZ, 0.0, ALU.mult, ALU.add))
                dve.tensor_copy(small[0:NP_, 5:6], nCZ[:, NF - 1:NF]).then_inc(s_tab, 1)

            def node_ranks():
                dve.wait_ge(s_tabp, 4)
                link(dve.tensor_copy(small[0:NP_, 6:7], psA[1][0:NP_, 0:1]))
                link(dve.tensor_scalar(S1, psA[1][0:NP_, 1:1 + T], 1.0, None, ALU.add))
                link(dve.tensor_tensor(Fj, iota127[0:NP_, 0:T], psA[1][0:NP_, 1 + T:1 + 2 * T], ALU.subtract))
                link(dve.tensor_tensor(nR, nCZ, nZ, ALU.subtract))
                link(dve.tensor_scalar(nR, nR, small[0:NP_, 6:7], None, ALU.add))
            def free_slots(t):
                for c in range(5):
                    at = bass.ds((t + -STEP_SLOTS).t * 5 + c, 1)
                    dve.scalar_tensor_tensor(junk[0:NP_, c * T:(c + 1) * T], Fj, nR[:, at], S1, ALU.is_le, ALU.mult,
                                             accum_out=nSL[:, at]).then_inc(s_free, 1)

            def slots_by_node():
                dve.wait_ge(s_free, NF)
                link(dve.tensor_tensor(nSL, nSL, nR, ALU.add))
                link(dve.tensor_tensor(nSL, nSL, nZ, ALU.mult))
                link(dve.tensor_tensor(nSL, nSL, nI[:, :, 0], ALU.add))
                dve.tensor_scalar(nDG, nI[:, :, 1], 1.0, None, ALU.max).then_inc(s_tab, 1)

            def slots_turned():
                dve.wait_ge(s_tabp, 5)
                link(dve.tensor_copy(slotT[0:NF, :], psA[1][0:NF, 0:NP_]))
                link(dve.tensor_copy(ndT[0:NF, :, 0], psA[1][0:NF, NP_:2 * NP_]))
                dve.tensor_copy(ndT[0:NF, :, 1], psA[1][0:NF, 2 * NP_:3 * NP_]).then_inc(s_scat_in, 1)

            def slot_table_loaded():
                dve.wait_ge(s_tload, 16)
                link(dve.tensor_copy(tA, tI[:, :, 0]))
                dve.tensor_copy(tB, tI[:, :, 1]).then_inc(s_tab, 1)

            def tables():
                dve.wait_ge(s_tabp, 6)
                link(dve.tensor_copy(permf, psA[1][:, 0:T]))
                link(dve.tensor_copy(degf, psA[1][:, T:2 * T]))
                link(dve.tensor_copy(poutT[:, :], permf))
                link(dve.scalar_tensor_tensor(pinT[:, :], permf, float(N), permf, ALU.is_lt, ALU.mult))
                link(dve.reciprocal(invdeg[:, :], degf))
                for l in range(LAYERS):
                    c = C[f"n{l}"]
                    link(dve.tensor_scalar(invs[:, l, :], invdeg[:, :], downs[:, c:c + 1],
                                           WUP / (Y_LN if l == 0 else Y_H), ALU.mult, ALU.mult))
                dve.tensor_scalar(small[:, 0:1], ones[:, 0:1], 1.0, None, ALU.mult).then_inc(s_tables, 1)

            rest = range(N_FIRST, len(NAMES))
            run_plan(dve, 2, TN,
                     [(2, norm0), (0, lambda t: ylo(t, 0)), (1, lambda t: turn(t, 0)), (3, stats0),
                      (0, lambda t: sev(t, 0))],
                     [(WSTEP(m) + 2, weight_norm, m) for m in rest] + [(WSTEP(m) + 3, weight_scale, m) for m in rest]
                     + [(WSTEP(m) + 4, weight_lo, m) for m in rest]
                     + [(WSTEP(C["w1"]), gain, None), (WSTEP(C["w1"]) + 1, gate_gain, None),
                        (STEP_GATE + 2, gate_norm, None),
                        (STEP_GATE + 3, gate_parts, None),
                        (STEP_GATE + 5, bias1_parts, None), (STEP_GATE + 7, last_scales, None),
                        (STEP_GATE + 9, bias2_parts, None),
                        (STEP_SLOTS - 2, unplaced_nodes, None),
                        (STEP_SLOTS, node_ranks, None), (STEP_SLOTS + NF // 5, slots_by_node, None),
                        (STEP_SCATTER - 1, slots_turned, None), (STEP_TABLES, slot_table_loaded, None),
                        (STEP_TABLES + 2, tables, None)],
                     [(STEP_SLOTS, STEP_SLOTS + NF // 5, free_slots)])

            def one_hot(t, l):
                s = ph[l]
                i = t.slot(GRING)
                after(dve, s.agg, (t + (1 - GRING)).n)
                dve.tensor_scalar(Sm[i][:, :], iota16[:, :], colT[:, bass.ds(t.t, 1)], rowval[:, 0:1],
                                  ALU.is_equal, ALU.mult).then_inc(s.smat, 1)

            def carry_lo(t, l):
                s = ph[l]
                i, o = t.slot(2), (t + 1).slot(GRING)
                if isinstance(t.t, int) and t.t == T - 1:
                    return
                dve.wait_ge(s.chi, (t + 1).n - t.run)
                dve.scalar_tensor_tensor(G[o][0:1, D:2 * D], psA[0 if l == 3 else i][0:1, :], 1.0 / CARRY,
                                         G[o][0:1, 0:D], ALU.mult, ALU.subtract).then_inc(s.clo, 1)

            def combine(t, l):
                s = ph[l]
                i = t.slot(2)
                if l == 1:
                    dve.wait_ge(s.x[i], t.landed(2))
                else:
                    dve.wait_ge(s.xs[i], Tile(t.U, t.j, t.k, l - 2).landed(2))
                dve.wait_ge(s.agg, (t + 1).n)
                if l == 3 and not (isinstance(t.t, int) and t.t == T - 1):
                    dve.wait_ge(s.chi, (t + 1).n - t.run)
                after(dve, s.rr, (t + -1).n)
                dve.scalar_tensor_tensor(R[i][:, :], psA[0 if l == 3 else i][:, :], invs[:, l - 1, bass.ds(t.t, 1)],
                                         Sl[i][:, :], ALU.mult, ALU.add).then_inc(s.r, 1)

            def sum_squares(t, l):
                s = ph[l]
                i = t.slot(2)
                dve.wait_ge(s.r, (t + 1).n)
                dve.scalar_tensor_tensor(junk[:, :], R[i][:, :], 0.0, R[i][:, :], ALU.max, ALU.mult,
                                         accum_out=ss[:, i:i + 1]).then_inc(s.dv2, 1)

            def sum_floor(t, l):
                s = ph[l]
                i = t.slot(2)
                dve.wait_ge(s.dv2, (t + 1).n)
                after(dve, s.sc, (t + -1).n)
                up = 1.0 if l == 3 else H_UP ** -2
                dve.tensor_scalar(ssm[:, i:i + 1], ss[:, i:i + 1], 1e-24, up, ALU.max, ALU.mult).then_inc(s.ss, 1)

            def hlo(t, l):
                s = ph[l]
                i = t.slot(2)
                dve.wait_ge(s.hhi, (t + 1).n)
                dve.scalar_tensor_tensor(HH[i][:, 1, :], RR[i][:, :], scl[:, i:i + 1], HH[i][:, 0, :],
                                         ALU.mult, ALU.subtract).then_inc(s.hlo, 1)

            for l in (1, 2):
                run_tiles(dve, 4, T, [(5, lambda t, l=l: one_hot(t, l)), (2, lambda t, l=l: hlo(t, l)), (0, lambda t, l=l: ylo(t, l)),
                                      (1, lambda t, l=l: turn(t, l)), (3, lambda t, l=l: carry_lo(t, l)),
                                      (3, lambda t, l=l: combine(t, l)), (3, lambda t, l=l: sum_squares(t, l)),
                                      (3, lambda t, l=l: sum_floor(t, l)), (0, lambda t, l=l: sev(t, l))], l - 1)

            s = ph[3]

            def x2(t):
                i, q = t.slot(2), t.slot(8)
                dve.wait_ge(s.sc, (t + 1).n)
                dve.wait_ge(s.rr, (t + 1).n)
                t = t.own
                dve.wait_ge(s.xg[i], t.landed(2))
                after(dve, f3.o, (t + -7).n)
                dve.scalar_tensor_tensor(X2[q], RR[i][:, :], scl[:, i:i + 1], X[i][:, :], ALU.mult, ALU.add
                                         ).then_inc(f3.x2, 1)

            def x2_stats(t):
                t = t.own
                dve.wait_ge(f3.x2, (t + 1).n)
                dve.bn_stats(st6[:, :], X2[t.slot(8)]).then_inc(f3.bnx, 1)

            def x2_mean_var(t):
                t = t.own
                hold(dve, s_const, (f3.bnx, (t + 1).n))
                dve.bn_aggr(mv3[:, t.slot(2), :], st6[:, :]).then_inc(f3.aggx, 1)

            def x2_eps(t):
                t = t.own
                i = t.slot(2)
                dve.wait_ge(f3.aggx, (t + 1).n)
                after(dve, f3.rs, (t + -1).n)
                dve.tensor_scalar(vv[:, i, 0:1], mv3[:, i, 1:2], LN_EPS, None, ALU.add).then_inc(f3.epsx, 1)

            def x2_inverse(t):
                t = t.own
                i = t.slot(2)
                dve.wait_ge(f3.epsx, (t + 1).n)
                dve.reciprocal(vinv[:, i:i + 1], vv[:, i, 0:1]).then_inc(f3.recx, 1)

            def inner_var(t):
                t = t.own
                i = t.slot(2)
                dve.wait_ge(f3.recx, (t + 1).n)
                dve.tensor_scalar(vv[:, i, 1:2], vinv[:, i:i + 1], mv3[:, i, 1:2], LN_EPS, ALU.mult, ALU.add
                                  ).then_inc(f3.v2, 1)

            def xlo(t):
                t = t.own
                i, q = t.slot(2), t.slot(8)
                dve.wait_ge(f3.xhi, (t + 1).n)
                dve.scalar_tensor_tensor(HH[i][:, 1, :], YF[q], r2s[:, i:i + 1], HH[i][:, 0, :],
                                         ALU.mult, ALU.subtract).then_inc(f3.xlo, 1)

            def logits(t):
                t = t.own
                dve.wait_ge(f3.pre, (t + 1).n)
                dve.scalar_tensor_tensor(wsc[:, t.slot(2), :], psG[:, 0:EXPERTS], downs[:, CG:CG + 1], bgb[:, :],
                                         ALU.mult, ALU.add).then_inc(f3.logit, 1)

            def largest(t):
                t = t.own
                i = t.slot(2)
                hold(dve, s_const, (f3.logit, (t + 1).n))
                dve.max(gv[:, i, 0:8], wsc[:, i, :]).then_inc(f3.top, 1)

            def largest_index(t):
                t = t.own
                i = t.slot(2)
                hold(dve, s_const, (f3.top, (t + 1).n))
                dve.max_index(gi[:, i, :], gv[:, i, 0:8], wsc[:, i, :]).then_inc(f3.topi, 1)

            def gap(t):
                t = t.own
                i = t.slot(2)
                dve.tensor_scalar(gv[:, i, 8:9], gv[:, i, 0:1], gv[:, i, 1:2], None, ALU.subtract).then_inc(f3.lg, 1)

            def index_float(t):
                t = t.own
                i = t.slot(2)
                dve.wait_ge(f3.topi, (t + 1).n)
                dve.tensor_copy(gv[:, i, 10:12], gi[:, i, 0:2]).then_inc(f3.topf, 1)

            def first_hot(t):
                t = t.own
                i = t.slot(2)
                dve.wait_ge(f3.topf, (t + 1).n)
                dve.tensor_scalar(gv[:, i, 16:24], iota_row[:, 0:8], gv[:, i, 10:11], None, ALU.is_equal
                                  ).then_inc(f3.hot1, 1)

            def both_hot(t):
                t = t.own
                i = t.slot(2)
                dve.wait_ge(f3.hot1, (t + 1).n)
                dve.scalar_tensor_tensor(gv[:, i, 24:32], iota_row[:, 0:8], gv[:, i, 11:12], gv[:, i, 16:24],
                                         ALU.is_equal, ALU.add).then_inc(f3.hot2, 1)

            def hot_difference(t):
                t = t.own
                i = t.slot(2)
                dve.wait_ge(f3.hot2, (t + 1).n)
                dve.scalar_tensor_tensor(gv[:, i, 32:40], gv[:, i, 16:24], 2.0, gv[:, i, 24:32],
                                         ALU.mult, ALU.subtract).then_inc(f3.hotd, 1)

            def confidences(t):
                t = t.own
                i = t.slot(2)
                dve.wait_ge(f3.th, (t + 1).n)
                dve.wait_ge(f3.hotd, (t + 1).n)
                after(dve, f3.hs, (t + -1).n)
                dve.scalar_tensor_tensor(wv[:, i, :], gv[:, i, 32:40], gv[:, i, 9:10], gv[:, i, 24:32],
                                         ALU.mult, ALU.add).then_inc(f3.w, 1)

            def conf_hi(t):
                t = t.own
                i = t.slot(2)
                dve.wait_ge(f3.w, (t + 1).n)
                after(dve, f3.th2, (t + -1).n)
                dve.tensor_scalar(W24[i][:, 0:16].rearrange("p (a e) -> p a e", a=2),
                                  wv[:, i, :].unsqueeze(1).to_broadcast([P, 2, EXPERTS]), ups[:, CB:CB + 1], None,
                                  ALU.mult).then_inc(f3.z24, 1)

            def conf_lo(t):
                t = t.own
                i = t.slot(2)
                dve.wait_ge(f3.z24, (t + 1).n)
                dve.scalar_tensor_tensor(W24[i][:, 16:24], wv[:, i, :], ups[:, CB:CB + 1], W24[i][:, 0:8],
                                         ALU.mult, ALU.subtract).then_inc(f3.w24, 1)

            def flo(t):
                t = t.own
                i = t.slot(2)
                dve.wait_ge(f3.hhi, (t + 1).n)
                dve.scalar_tensor_tensor(FH[i][:, 1, :], HS[i], ups[:, CB:CB + 1], FH[i][:, 0, :],
                                         ALU.mult, ALU.subtract).then_inc(f3.hlo, 1)

            def zf(t):
                t = t.own
                i, q = t.slot(2), t.slot(8)
                dve.wait_ge(f3.cmb, (t + 1).n)
                dve.scalar_tensor_tensor(Z[i], psO[:, :], downs[:, FINAL:FINAL + 1], YF[q], ALU.mult, ALU.add
                                         ).then_inc(f3.z, 1)

            def z_stats(t):
                t = t.own
                dve.wait_ge(f3.z, (t + 1).n)
                dve.bn_stats(st6b[:, :], Z[t.slot(2)]).then_inc(f3.bnz, 1)

            def z_mean_var(t):
                t = t.own
                hold(dve, s_const, (f3.bnz, (t + 1).n), (f3.zr, (t + -1).n))
                dve.bn_aggr(zm[:, t.slot(2), :], st6b[:, :]).then_inc(f3.aggz, 1)

            def z_gain(t):
                t = t.own
                i = t.slot(2)
                dve.wait_ge(f3.aggz, (t + 1).n)
                dve.scalar_tensor_tensor(Z[i], Z[i], zm[:, i, 0:1], ogb[:, :], ALU.subtract, ALU.mult
                                         ).then_inc(f3.o1, 1)

            def result(t):
                t = t.own
                i = t.slot(2)
                dve.wait_ge(f3.o1, (t + 1).n)
                dve.wait_ge(f3.zr, (t + 1).n)
                dve.wait_ge(f3.xob, (t + 1).n)
                if not (isinstance(t.t, int) and t.t < 2):
                    dve.wait_ge(f3.out[i], (t + -2).landed(2))
                dve.scalar_tensor_tensor(OUT[i], Z[i], zr[:, i:i + 1], X2[t.slot(8)], ALU.mult, ALU.add
                                         ).then_inc(f3.o, 1)

            run_tiles(dve, 8, T, [
                (-5, result), (-1, logits), (3, x2), (-1, largest), (3, x2_stats), (4, lambda t: combine(t, 3)), (-1, largest_index),
                (3, x2_mean_var), (-1, gap), (-1, index_float), (4, lambda t: sum_squares(t, 3)), (-1, first_hot),
                (3, x2_eps), (-4, zf), (-1, both_hot), (3, x2_inverse),
                (-4, z_stats), (-1, hot_difference), (3, inner_var), (4, lambda t: sum_floor(t, 3)), (-2, flo),
                (-4, z_mean_var), (-1, confidences), (2, xlo), (-1, conf_hi), (-4, z_gain),
                (-1, conf_lo)], 2)

        @block.tensor
        def _(pe):
            pe.wait_ge(s_const, 1)
            pe.wait_ge(s_constv, 1)

            def tp(o, i, rows):
                return pe.transpose(o, i, iden[0:rows, 0:rows])

            pe.wait_ge(s_tab, 1)
            tp(psA[1][0:1, 0:T], pm_col[:, 0:1], T).then_inc(s_tabp, 1)
            pe.wait_ge(s_tab, 2)
            tp(psA[1][0:T, 0:1], pm_row[0:1, 0:T], 1).then_inc(s_tabp, 1)
            pe.wait_ge(s_tab, 3)
            for k, a in enumerate((eCOL, eSLOT, eDEG, eDST, eSRC)):
                mm = tp(psA[1][:, k * T:(k + 1) * T], a, T)
            mm.then_inc(s_tabp, 1)
            pe.wait_ge(s_bm, 1)

            def bias_products():
                m = C["w1"]
                pe.wait_ge(s_wload[m % 2], 64 * (m // 2 + 1))
                for c in range(KC):
                    mm = pe.matmul(psA[1][:, :], bmat[:, c, :], raw[:, m % 2, c, :], start=(c == 0), stop=(c == KC - 1))
                mm.then_inc(s_ffb, 1)
                pe.wait_ge(s_cmax, m)
                for c in range(KC):
                    mm = pe.matmul(psA[0][:, 0:EXPERTS], bmat[:, c, :], wgr[:, c, :], start=(c == 0), stop=(c == KC - 1))
                mm.then_inc(s_ffb, 1)

            def square_sums(m):
                name = NAMES[m]
                pe.wait_ge(s_sq, m + 1)
                after(pe, s_cmax, m)
                for c in range(KC):
                    mm = pe.matmul(psA[0][:, :], ones16[:, :], sqw[:, c, :], start=(c == 0),
                                   stop=(c == KC - 1 and name != "w2"))
                if name == "w2":
                    pe.wait_ge(s_sqb, 1)
                    mm = pe.matmul(psA[0][:, :], ones16[0:EXPERTS, :], sqb2[:, :], start=False, stop=True)
                mm.then_inc(s_cn, 1)

            def gate_sums():
                pe.wait_ge(s_sq, 9)
                pe.wait_ge(s_cmax, 8)
                for c in range(KC):
                    mm = pe.matmul(psA[0][:, 0:EXPERTS], ones16[:, :], sqw[:, 0, EXPERTS * c:EXPERTS * (c + 1)], start=(c == 0),
                                   stop=(c == KC - 1))
                mm.then_inc(s_cn, 1)

            def counts_before():
                pe.wait_ge(s_tab, 4)
                pe.wait_ge(s_wgain, 1)
                pe.matmul(psA[1][0:NP_, 0:1], upper[0:NP_, 0:NP_], small[0:NP_, 5:6], start=True, stop=True)
                pe.matmul(psA[1][0:NP_, 1:1 + 2 * T], smat, iu, start=True, stop=True).then_inc(s_tabp, 1)

            def turn_nodes():
                pe.wait_ge(s_tab, 5)
                for k, a in enumerate((nSL, node_no[:, :], nDG)):
                    mm = tp(psA[1][0:NF, k * NP_:(k + 1) * NP_], a, NP_)
                mm.then_inc(s_tabp, 1)

            def turn_slots():
                pe.wait_ge(s_tab, 6)
                tp(psA[1][:, 0:T], tA, T)
                tp(psA[1][:, T:2 * T], tB, T).then_inc(s_tabp, 1)

            for m in range(N_FIRST):
                square_sums(m)
            pe.wait_ge(s_wlo, N_FIRST)

            def turn(t, l):
                s = ph[l]
                i = t.slot(2)
                pe.wait_ge(s.hhi, (t + 1).n)
                pe.wait_ge(s.hlo, (t + 1).n)
                after(pe, s.ht, (t + -1).n)
                for a in range(2):
                    for c in range(KC):
                        mm = pe.transpose(psT[i][:, a, c, :], HH[i][:, a, c * P:(c + 1) * P], iden16[:, :])
                mm.then_inc(s.tr, 1)

            def neigh(t, l):
                s = ph[l]
                i = t.slot(2)
                pe.wait_ge(s.ht, (t + 1).n)
                after(pe, s.ylo, (t + -1).n)
                products(pe, psY[i][:, :], HT[i], WT[f"n{l}"]).then_inc(s.y, 1)

            def own(t, l):
                s = ph[l]
                i = t.slot(2)
                after(pe, s.sev, (t + -1).n)
                products(pe, psS[i][:, :], HT[i], WT[f"s{l}"]).then_inc(s.sp, 1)

            run_plan(pe, 2, TN, [(0, lambda t: neigh(t, 0)), (1, lambda t: turn(t, 0)), (0, lambda t: own(t, 0))],
                     [(WSTEP(m) + 1, square_sums, m) for m in range(N_FIRST, len(NAMES))]
                     + [(WSTEP(C["w1"]) - 1, bias_products, None), (STEP_GATE + 1, gate_sums, None),
                        (STEP_SLOTS - 1, counts_before, None), (STEP_SCATTER - 2, turn_nodes, None),
                        (STEP_TABLES + 1, turn_slots, None)])

            pe.wait_ge(s_wlo, len(NAMES))
            pe.wait_ge(s_tables, 1)

            def aggregate(t, l):
                s = ph[l]
                i = t.slot(2)
                g = t.slot(GRING)
                pe.wait_ge(s.g[g], t.landed(GRING))
                pe.wait_ge(s.smat, (t + 1).n)
                if isinstance(t.t, int) and t.t == 0:
                    pe.wait_ge(s.c0, t.run + 1)
                else:
                    pe.wait_ge(s.clo, t.n - t.run)
                back = 0 if l == 3 else -1
                after(pe, s.r, (t + back).n)
                acc = psA[0 if l == 3 else i][:, :]
                pe.matmul(acc, Sm[g][:, :], G[g][:, 0:D], start=True, stop=False)
                pe.matmul(acc, Sm[g][:, :], G[g][:, D:2 * D], start=False, stop=True).then_inc(s.agg, 1)

            for l in (1, 2):
                run_tiles(pe, 4, T, [(0, lambda t, l=l: neigh(t, l)), (1, lambda t, l=l: turn(t, l)),
                                     (0, lambda t, l=l: own(t, l)), (3, lambda t, l=l: aggregate(t, l))], l - 1)

            def up(t):
                t = t.own
                i = t.slot(2)
                pe.wait_ge(f3.txc, (t + 1).n)
                after(pe, f3.gel, (t + -1).n)
                products(pe, psY[i][:, :], HT[i], WT["w1"], stop=False)
                pe.matmul(psY[i][:, :], c2row[:, :], b1s[:, :], start=False, stop=True)
                after(pe, f3.logit, t.t)
                mm = products(pe, psG[:, 0:EXPERTS], HT[i], wg16.rearrange("p c (a e) -> p a c e", a=2))
                mm.then_inc(f3.pre, 1)

            def turn_h(t):
                t = t.own
                i = t.slot(2)
                pe.wait_ge(f3.hhi, (t + 1).n)
                pe.wait_ge(f3.hlo, (t + 1).n)
                pe.wait_ge(f3.w24, (t + 1).n)
                after(pe, f3.thc, t.t)
                after(pe, f3.wtt, t.t)
                pe.transpose(psW[0:24, 0:P], W24[i][:, :], iden16[:, :])
                for a in range(2):
                    for c in range(KC):
                        mm = pe.transpose(psH[:, a, c, :], FH[i][:, a, c * P:(c + 1) * P], iden16[:, :])
                mm.then_inc(f3.th2, 1)

            def turn_x(t):
                t = t.own
                i = t.slot(2)
                pe.wait_ge(f3.xhi, (t + 1).n)
                pe.wait_ge(f3.xlo, (t + 1).n)
                after(pe, f3.txc, t.t)
                for a in range(2):
                    for c in range(KC):
                        mm = pe.transpose(psX[:, a, c, :], HH[i][:, a, c * P:(c + 1) * P], iden16[:, :])
                mm.then_inc(f3.tx, 1)

            def down(t):
                t = t.own
                i = t.slot(2)
                pe.wait_ge(f3.thc, (t + 1).n)
                pe.wait_ge(f3.wtt, (t + 1).n)
                after(pe, f3.z, t.t)
                products(pe, psO[:, :], FT[i], WT["w2"], stop=False)
                pe.matmul(psO[:, :], WTT[i][:, :], b2s[:, :], start=False, stop=True).then_inc(f3.cmb, 1)

            def carry_rest(t):
                if isinstance(t.t, int) and t.t == T - 1:
                    return
                o = (t + 1).slot(GRING)
                pe.wait_ge(s.r, (t + 1).n)
                pe.wait_ge(s.chi, (t + 1).n - t.run)
                pe.matmul(psA[0][:, :], minus[:, :], G[o][:, 0:D], start=False, stop=True,
                          skip_group_check=True).then_inc(f3.rest, 1)

            s = ph[3]
            run_tiles(pe, 8, T, [(4, lambda t: aggregate(t, 3)), (-4, down), (-3, turn_h), (0, up), (4, carry_rest),
                                 (1, turn_x)], 2)


_INS = ['x', 'src', 'dst', 'L0_gnn_W_self', 'L0_gnn_W_neigh', 'L0_gnn_b', 'L0_ffn_Wg', 'L0_ffn_W1', 'L0_ffn_b1',
        'L0_ffn_W2', 'L0_ffn_b2', 'L0_ffn_ln_g', 'L0_ffn_ln_b', 'L0_ffn_out_g', 'L0_ffn_out_b']
_OUTS = [((N, D), 'float32')]


def kernel(**inputs):
    import numpy as _np
    import concourse.bacc as _bacc
    from concourse import mybir as _mybir
    from concourse.bass_utils import run_bass_kernel_spmd as _run

    nc = _bacc.Bacc("TRN2", target_bir_lowering=False, num_devices=1)
    arrays, args = {}, []
    for name in _INS:
        a = _np.ascontiguousarray(inputs[name])
        arrays[f"in_{name}_dram"] = a
        args.append(nc.dram_tensor(f"in_{name}_dram", a.shape, _mybir.dt.from_np(a.dtype), kind="ExternalInput").ap())
    for i, (shape, dtype) in enumerate(_OUTS):
        dt = _mybir.dt.from_np(_np.dtype(dtype))
        args.append(nc.dram_tensor(f"out_{i}_dram", shape, dt, kind="ExternalOutput").ap())
    build(nc, *args)
    r = _run(nc, [arrays], core_ids=[0])
    return r.results[0]["out_0_dram"]
```
